# Optimizing a Trainium2 kernel written in Bass

```python
import numpy as np
import jax
import jax.numpy as jnp

def _softmax(x, axis=-1):
    return jax.nn.softmax(x, axis=axis)

def _gelu(x):
    return jax.nn.gelu(x, approximate=True)

def _silu(x):
    return jax.nn.silu(x)

def _sigmoid(x):
    return jax.nn.sigmoid(x)

def _layernorm(x, axis=-1, eps=1e-05):
    m = jnp.mean(x, axis=axis, keepdims=True)
    v = jnp.var(x, axis=axis, keepdims=True)
    return (x - m) / jnp.sqrt(v + eps)

def _scatter_add(tgt, idx, src, axis=0):
    return tgt.at[idx].add(src)

def _segment_sum(src, seg, n):
    return jax.ops.segment_sum(src, seg, n)
kernel_name = 'mk_vit_tower_cls_d1_tok_img768_r4_440c8b'

def setup_inputs(seed: int=0):
    np.random.seed(seed)
    _w = jnp.asarray

    def _rec_inputs():
        import jax
        import jax.numpy as jnp
        _rk = jax.random.key(seed)
        x = 7.57192e-06 + 1.00007 * jax.random.normal(jax.random.fold_in(_rk, 1), (32, 3, 112, 112), jnp.float32)
        cls_tok = 0.02 * jax.random.normal(jax.random.fold_in(_rk, 5), (1, 1, 192), jnp.float32)
        return (x, cls_tok)
    x, cls_tok = _rec_inputs()

    def _L0_tok_setup():
        import jax, jax.numpy as jnp
        import numpy as np
        K = 4
        STRIDE = 4
        EPS = 1e-05
        SLOPE = 0.01

        def conv2d(x, w, b, stride):
            out = jax.lax.conv_general_dilated(x, w, (stride, stride), 'VALID', dimension_numbers=('NCHW', 'OIHW', 'NCHW'))
            return out + b[None, :, None, None]

        def batchnorm(x, g, b, m, v):
            inv = g / jnp.sqrt(v + EPS)
            return x * inv[None, :, None, None] + (b - m * inv)[None, :, None, None]

        def leaky_relu(x):
            return jnp.where(x >= 0, x, SLOPE * x)

        def deform_conv(x, offset, w, b):
            B, C, H, W = x.shape
            Ho, Wo = (offset.shape[2], offset.shape[3])
            KK = K * K
            off = offset.reshape(B, KK, 2, Ho, Wo)
            kh = jnp.repeat(jnp.arange(K), K).astype(x.dtype)
            kw = jnp.tile(jnp.arange(K), K).astype(x.dtype)
            base_y = (jnp.arange(Ho) * STRIDE).astype(x.dtype)
            base_x = (jnp.arange(Wo) * STRIDE).astype(x.dtype)
            py = base_y[None, None, :, None] + kh[None, :, None, None] + off[:, :, 0]
            px = base_x[None, None, None, :] + kw[None, :, None, None] + off[:, :, 1]
            y0 = jnp.floor(py)
            x0 = jnp.floor(px)
            wy = py - y0
            wx = px - x0

            def corner(yc, xc):
                yi = yc.astype(jnp.int32)
                xi = xc.astype(jnp.int32)
                valid = (yi >= 0) & (yi < H) & (xi >= 0) & (xi < W)
                yi = jnp.clip(yi, 0, H - 1)
                xi = jnp.clip(xi, 0, W - 1)
                v = jax.vmap(lambda img, a, c: img[:, a, c])(x, yi, xi)
                return v * valid[:, None].astype(x.dtype)
            v00 = corner(y0, x0)
            v01 = corner(y0, x0 + 1)
            v10 = corner(y0 + 1, x0)
            v11 = corner(y0 + 1, x0 + 1)
            wy_ = wy[:, None]
            wx_ = wx[:, None]
            sampled = v00 * (1 - wy_) * (1 - wx_) + v01 * (1 - wy_) * wx_ + v10 * wy_ * (1 - wx_) + v11 * wy_ * wx_
            out = jnp.einsum('bckhw,ock->bohw', sampled, w.reshape(w.shape[0], C, KK))
            return out + b[None, :, None, None]
        key = jax.random.key(seed)
        ks = jax.random.split(key, 16)
        f32 = jnp.float32
        inp = {'x': jax.random.normal(ks[0], (64, 3, 224, 224), f32), 'stem_w': jax.random.normal(ks[1], (96, 3, 4, 4), f32) * 0.1, 'stem_b': jax.random.normal(ks[2], (96,), f32) * 0.05, 'bn1_g': jax.random.uniform(ks[3], (96,), f32, 0.5, 1.5), 'bn1_b': jax.random.normal(ks[4], (96,), f32) * 0.05, 'bn1_m': jax.random.normal(ks[5], (96,), f32) * 0.05, 'bn1_v': jax.random.uniform(ks[6], (96,), f32, 0.5, 1.5), 'off_w': jax.random.normal(ks[7], (32, 96, 4, 4), f32) * 0.02, 'off_b': jax.random.normal(ks[8], (32,), f32) * 0.02, 'dcn_w': jax.random.normal(ks[9], (192, 96, 4, 4), f32) * 0.05, 'dcn_b': jax.random.normal(ks[10], (192,), f32) * 0.05, 'bn2_g': jax.random.uniform(ks[11], (192,), f32, 0.5, 1.5), 'bn2_b': jax.random.normal(ks[12], (192,), f32) * 0.05, 'bn2_m': jax.random.normal(ks[13], (192,), f32) * 0.05, 'bn2_v': jax.random.uniform(ks[14], (192,), f32, 0.5, 1.5)}
        return inp
    _L0_tok_all = _L0_tok_setup()
    _L0_tok_in = {k: v for k, v in _L0_tok_all.items() if k in ('stem_w', 'stem_b', 'bn1_g', 'bn1_b', 'bn1_m', 'bn1_v', 'off_w', 'off_b', 'dcn_w', 'dcn_b', 'bn2_g', 'bn2_b', 'bn2_m', 'bn2_v')}
    del _L0_tok_all

    def _L0_attn_setup():
        import jax, jax.numpy as jnp
        import numpy as np
        DIM = 192
        NUM_HEADS = 12
        HEAD_DIM = DIM // NUM_HEADS
        HIDDEN = int(DIM * 4.0)
        EPS = 1e-08

        def layer_norm(x, w, b):
            mu = jnp.mean(x, axis=-1, keepdims=True)
            var = jnp.mean(jnp.square(x - mu), axis=-1, keepdims=True)
            return (x - mu) * jax.lax.rsqrt(var + EPS) * w + b

        def linear_attention(x, qkv_w, qkv_b, proj_w, proj_b):
            B, N, C = x.shape
            qkv = (x @ qkv_w + qkv_b).reshape(B, N, 3, NUM_HEADS, HEAD_DIM)
            qkv = qkv.transpose(2, 0, 3, 1, 4)
            q, k, v = (qkv[0], qkv[1], qkv[2])
            q = jax.nn.elu(q) + 1.0
            k = jax.nn.elu(k) + 1.0
            kv = jnp.einsum('bhsd,bhse->bhde', k, v)
            z = 1.0 / jnp.einsum('bhsd,bhd->bhs', q, k.sum(axis=-2))
            out = jnp.einsum('bhde,bhsd,bhs->bhse', kv, q, z)
            out = out.transpose(0, 2, 1, 3).reshape(B, N, C)
            return out @ proj_w + proj_b
        key = jax.random.key(seed)
        ks = jax.random.split(key, 10)
        s = 0.02
        return {'x': jax.random.normal(ks[0], (16, 1024, DIM), dtype=jnp.float32), 'qkv_w': jax.random.normal(ks[1], (DIM, 3 * DIM), dtype=jnp.float32) * s, 'qkv_b': jnp.zeros((3 * DIM,), dtype=jnp.float32), 'proj_w': jax.random.normal(ks[2], (DIM, DIM), dtype=jnp.float32) * s, 'proj_b': jnp.zeros((DIM,), dtype=jnp.float32), 'fc1_w': jax.random.normal(ks[3], (DIM, HIDDEN), dtype=jnp.float32) * s, 'fc1_b': jnp.zeros((HIDDEN,), dtype=jnp.float32), 'fc2_w': jax.random.normal(ks[4], (HIDDEN, DIM), dtype=jnp.float32) * s, 'fc2_b': jnp.zeros((DIM,), dtype=jnp.float32), 'ln1_w': jnp.ones((DIM,), dtype=jnp.float32), 'ln1_b': jnp.zeros((DIM,), dtype=jnp.float32), 'ln2_w': jnp.ones((DIM,), dtype=jnp.float32), 'ln2_b': jnp.zeros((DIM,), dtype=jnp.float32)}
    _L0_attn_all = _L0_attn_setup()
    _L0_attn_in = {k: v for k, v in _L0_attn_all.items() if k in ('qkv_w', 'qkv_b', 'proj_w', 'proj_b', 'fc1_w', 'fc1_b', 'fc2_w', 'fc2_b', 'ln1_w', 'ln1_b', 'ln2_w', 'ln2_b')}
    del _L0_attn_all

    def _L0_ffn_setup():
        import jax, jax.numpy as jnp
        import numpy as np
        B, T, C = (4, 512, 192)
        E, K = (8, 2)

        def _mlp(x, wfc, wproj):
            h = jnp.square(jax.nn.relu(x @ wfc))
            return h @ wproj
        key = jax.random.key(seed)
        ks = jax.random.split(key, 6)
        s = 0.02
        return {'x': jax.random.normal(ks[0], (B, T, C), jnp.float32), 'w_fc_sh': jax.random.normal(ks[1], (C, C), jnp.float32) * s, 'w_proj_sh': jax.random.normal(ks[2], (C, C), jnp.float32) * s, 'w1': jax.random.normal(ks[3], (E, C, C), jnp.float32) * s, 'w2': jax.random.normal(ks[4], (E, C, C), jnp.float32) * s, 'router_w': jax.random.normal(ks[5], (E, C), jnp.float32) * s, 'balance_bias': jnp.zeros((E,), jnp.float32)}
    _L0_ffn_all = _L0_ffn_setup()
    _L0_ffn_in = {k: v for k, v in _L0_ffn_all.items() if k in ('w_fc_sh', 'w_proj_sh', 'w1', 'w2', 'router_w', 'balance_bias')}
    del _L0_ffn_all
    return {'x': x, 'cls_tok': cls_tok, 'L0_tok_stem_w': _L0_tok_in['stem_w'], 'L0_tok_stem_b': _L0_tok_in['stem_b'], 'L0_tok_bn1_g': _L0_tok_in['bn1_g'], 'L0_tok_bn1_b': _L0_tok_in['bn1_b'], 'L0_tok_bn1_m': _L0_tok_in['bn1_m'], 'L0_tok_bn1_v': _L0_tok_in['bn1_v'], 'L0_tok_off_w': _L0_tok_in['off_w'], 'L0_tok_off_b': _L0_tok_in['off_b'], 'L0_tok_dcn_w': _L0_tok_in['dcn_w'], 'L0_tok_dcn_b': _L0_tok_in['dcn_b'], 'L0_tok_bn2_g': _L0_tok_in['bn2_g'], 'L0_tok_bn2_b': _L0_tok_in['bn2_b'], 'L0_tok_bn2_m': _L0_tok_in['bn2_m'], 'L0_tok_bn2_v': _L0_tok_in['bn2_v'], 'L0_attn_qkv_w': _L0_attn_in['qkv_w'], 'L0_attn_qkv_b': _L0_attn_in['qkv_b'], 'L0_attn_proj_w': _L0_attn_in['proj_w'], 'L0_attn_proj_b': _L0_attn_in['proj_b'], 'L0_attn_fc1_w': _L0_attn_in['fc1_w'], 'L0_attn_fc1_b': _L0_attn_in['fc1_b'], 'L0_attn_fc2_w': _L0_attn_in['fc2_w'], 'L0_attn_fc2_b': _L0_attn_in['fc2_b'], 'L0_attn_ln1_w': _L0_attn_in['ln1_w'], 'L0_attn_ln1_b': _L0_attn_in['ln1_b'], 'L0_attn_ln2_w': _L0_attn_in['ln2_w'], 'L0_attn_ln2_b': _L0_attn_in['ln2_b'], 'L0_ffn_w_fc_sh': _L0_ffn_in['w_fc_sh'], 'L0_ffn_w_proj_sh': _L0_ffn_in['w_proj_sh'], 'L0_ffn_w1': _L0_ffn_in['w1'], 'L0_ffn_w2': _L0_ffn_in['w2'], 'L0_ffn_router_w': _L0_ffn_in['router_w'], 'L0_ffn_balance_bias': _L0_ffn_in['balance_bias']}

def reference(x, cls_tok, L0_tok_stem_w, L0_tok_stem_b, L0_tok_bn1_g, L0_tok_bn1_b, L0_tok_bn1_m, L0_tok_bn1_v, L0_tok_off_w, L0_tok_off_b, L0_tok_dcn_w, L0_tok_dcn_b, L0_tok_bn2_g, L0_tok_bn2_b, L0_tok_bn2_m, L0_tok_bn2_v, L0_attn_qkv_w, L0_attn_qkv_b, L0_attn_proj_w, L0_attn_proj_b, L0_attn_fc1_w, L0_attn_fc1_b, L0_attn_fc2_w, L0_attn_fc2_b, L0_attn_ln1_w, L0_attn_ln1_b, L0_attn_ln2_w, L0_attn_ln2_b, L0_ffn_w_fc_sh, L0_ffn_w_proj_sh, L0_ffn_w1, L0_ffn_w2, L0_ffn_router_w, L0_ffn_balance_bias):
    import jax
    import jax.numpy as jnp

    def _L0_tok_ref(x, stem_w, stem_b, bn1_g, bn1_b, bn1_m, bn1_v, off_w, off_b, dcn_w, dcn_b, bn2_g, bn2_b, bn2_m, bn2_v):
        import jax, jax.numpy as jnp
        import numpy as np
        K = 4
        STRIDE = 4
        EPS = 1e-05
        SLOPE = 0.01

        def conv2d(x, w, b, stride):
            out = jax.lax.conv_general_dilated(x, w, (stride, stride), 'VALID', dimension_numbers=('NCHW', 'OIHW', 'NCHW'))
            return out + b[None, :, None, None]

        def batchnorm(x, g, b, m, v):
            inv = g / jnp.sqrt(v + EPS)
            return x * inv[None, :, None, None] + (b - m * inv)[None, :, None, None]

        def leaky_relu(x):
            return jnp.where(x >= 0, x, SLOPE * x)

        def deform_conv(x, offset, w, b):
            B, C, H, W = x.shape
            Ho, Wo = (offset.shape[2], offset.shape[3])
            KK = K * K
            off = offset.reshape(B, KK, 2, Ho, Wo)
            kh = jnp.repeat(jnp.arange(K), K).astype(x.dtype)
            kw = jnp.tile(jnp.arange(K), K).astype(x.dtype)
            base_y = (jnp.arange(Ho) * STRIDE).astype(x.dtype)
            base_x = (jnp.arange(Wo) * STRIDE).astype(x.dtype)
            py = base_y[None, None, :, None] + kh[None, :, None, None] + off[:, :, 0]
            px = base_x[None, None, None, :] + kw[None, :, None, None] + off[:, :, 1]
            y0 = jnp.floor(py)
            x0 = jnp.floor(px)
            wy = py - y0
            wx = px - x0

            def corner(yc, xc):
                yi = yc.astype(jnp.int32)
                xi = xc.astype(jnp.int32)
                valid = (yi >= 0) & (yi < H) & (xi >= 0) & (xi < W)
                yi = jnp.clip(yi, 0, H - 1)
                xi = jnp.clip(xi, 0, W - 1)
                v = jax.vmap(lambda img, a, c: img[:, a, c])(x, yi, xi)
                return v * valid[:, None].astype(x.dtype)
            v00 = corner(y0, x0)
            v01 = corner(y0, x0 + 1)
            v10 = corner(y0 + 1, x0)
            v11 = corner(y0 + 1, x0 + 1)
            wy_ = wy[:, None]
            wx_ = wx[:, None]
            sampled = v00 * (1 - wy_) * (1 - wx_) + v01 * (1 - wy_) * wx_ + v10 * wy_ * (1 - wx_) + v11 * wy_ * wx_
            out = jnp.einsum('bckhw,ock->bohw', sampled, w.reshape(w.shape[0], C, KK))
            return out + b[None, :, None, None]
        h = conv2d(x, stem_w, stem_b, 4)
        h = leaky_relu(batchnorm(h, bn1_g, bn1_b, bn1_m, bn1_v))
        offset = conv2d(h, off_w, off_b, 4)
        h = deform_conv(h, offset, dcn_w, dcn_b)
        h = leaky_relu(batchnorm(h, bn2_g, bn2_b, bn2_m, bn2_v))
        B, C, Ho, Wo = h.shape
        return h.reshape(B, C, Ho * Wo).transpose(0, 2, 1)

    def _L0_attn_ref(x, qkv_w, qkv_b, proj_w, proj_b, fc1_w, fc1_b, fc2_w, fc2_b, ln1_w, ln1_b, ln2_w, ln2_b):
        import jax, jax.numpy as jnp
        import numpy as np
        DIM = 192
        NUM_HEADS = 12
        HEAD_DIM = DIM // NUM_HEADS
        HIDDEN = int(DIM * 4.0)
        EPS = 1e-08

        def layer_norm(x, w, b):
            mu = jnp.mean(x, axis=-1, keepdims=True)
            var = jnp.mean(jnp.square(x - mu), axis=-1, keepdims=True)
            return (x - mu) * jax.lax.rsqrt(var + EPS) * w + b

        def linear_attention(x, qkv_w, qkv_b, proj_w, proj_b):
            B, N, C = x.shape
            qkv = (x @ qkv_w + qkv_b).reshape(B, N, 3, NUM_HEADS, HEAD_DIM)
            qkv = qkv.transpose(2, 0, 3, 1, 4)
            q, k, v = (qkv[0], qkv[1], qkv[2])
            q = jax.nn.elu(q) + 1.0
            k = jax.nn.elu(k) + 1.0
            kv = jnp.einsum('bhsd,bhse->bhde', k, v)
            z = 1.0 / jnp.einsum('bhsd,bhd->bhs', q, k.sum(axis=-2))
            out = jnp.einsum('bhde,bhsd,bhs->bhse', kv, q, z)
            out = out.transpose(0, 2, 1, 3).reshape(B, N, C)
            return out @ proj_w + proj_b
        y = linear_attention(layer_norm(x, ln1_w, ln1_b), qkv_w, qkv_b, proj_w, proj_b)
        x = x + y
        h = layer_norm(x, ln2_w, ln2_b)
        h = jax.nn.gelu(h @ fc1_w + fc1_b, approximate=False) @ fc2_w + fc2_b
        return x + h

    def _L0_ffn_ref(x, w_fc_sh, w_proj_sh, w1, w2, router_w, balance_bias):
        import jax, jax.numpy as jnp
        import numpy as np
        B, T, C = (4, 512, 192)
        E, K = (8, 2)

        def _mlp(x, wfc, wproj):
            h = jnp.square(jax.nn.relu(x @ wfc))
            return h @ wproj
        Bx, Tx, Cx = x.shape
        shared = _mlp(x, w_fc_sh, w_proj_sh)
        xf = x.reshape(-1, Cx)
        logits = xf.astype(jnp.float32) @ router_w.T
        scores = jax.nn.sigmoid(logits)
        _, idx = jax.lax.top_k(scores + balance_bias, K)
        tw = jnp.take_along_axis(scores, idx, axis=-1)
        tw = tw / (tw.sum(-1, keepdims=True) + 1e-20)
        combine = (jax.nn.one_hot(idx, E, dtype=tw.dtype) * tw[..., None]).sum(1)
        h = jnp.square(jax.nn.relu(jnp.einsum('nc,ech->neh', xf, w1)))
        y = jnp.einsum('neh,ehc->nec', h, w2)
        routed = jnp.einsum('nec,ne->nc', y, combine)
        return shared + routed.reshape(Bx, Tx, Cx)
    h = _L0_tok_ref(x, L0_tok_stem_w, L0_tok_stem_b, L0_tok_bn1_g, L0_tok_bn1_b, L0_tok_bn1_m, L0_tok_bn1_v, L0_tok_off_w, L0_tok_off_b, L0_tok_dcn_w, L0_tok_dcn_b, L0_tok_bn2_g, L0_tok_bn2_b, L0_tok_bn2_m, L0_tok_bn2_v)
    h = jnp.concatenate([jnp.broadcast_to(cls_tok, (h.shape[0], 1, h.shape[2])), h], axis=1)
    h = h + _L0_attn_ref(_layernorm(h, axis=-1), L0_attn_qkv_w, L0_attn_qkv_b, L0_attn_proj_w, L0_attn_proj_b, L0_attn_fc1_w, L0_attn_fc1_b, L0_attn_fc2_w, L0_attn_fc2_b, L0_attn_ln1_w, L0_attn_ln1_b, L0_attn_ln2_w, L0_attn_ln2_b)
    h = h + _L0_ffn_ref(_layernorm(h, axis=-1), L0_ffn_w_fc_sh, L0_ffn_w_proj_sh, L0_ffn_w1, L0_ffn_w2, L0_ffn_router_w, L0_ffn_balance_bias)
    return h

_drawn_inputs = setup_inputs


def setup_inputs(seed=0):
    import zlib

    import numpy as np

    out = dict(_drawn_inputs(seed))
    spreads = {'L0_attn_qkv_b': (0.0, 0.428),
     'L0_attn_proj_b': (0.0, 0.1),
     'L0_attn_fc1_b': (0.0, 0.424),
     'L0_attn_fc2_b': (0.0, 0.1),
     'L0_attn_ln1_w': (1.0, 0.6),
     'L0_attn_ln1_b': (0.0, 0.8),
     'L0_attn_ln2_w': (1.0, 0.6),
     'L0_attn_ln2_b': (0.0, 0.8),
     'L0_ffn_balance_bias': (0.0, 0.742)}
    factors = {'L0_ffn_w_fc_sh': 4.012,
     'L0_ffn_w_proj_sh': 3.651,
     'L0_ffn_w1': 5.633,
     'L0_ffn_w2': 5.219,
     'L0_ffn_router_w': 7.061}
    for name, (base, spread) in spreads.items():
        noise = np.random.default_rng([zlib.crc32(name.encode()), seed]).standard_normal(out[name].shape)
        drawn = base * np.exp(spread * noise) if base else spread * noise
        out[name] = jnp.asarray(drawn.astype(out[name].dtype))
    for name, factor in factors.items():
        out[name] = (out[name] * factor).astype(out[name].dtype)
    return out
```

```python
from contextlib import ExitStack

import concourse.bass as bass
from concourse import mybir

F32 = mybir.dt.float32
U32 = mybir.dt.uint32
ALU = mybir.AluOpType
ACT = mybir.ActivationFunctionType

IMAGES, GROUP_IMGS, TILE_IMGS = 32, 4, 2
GROUPS = IMAGES // GROUP_IMGS
TILES = GROUP_IMGS // TILE_IMGS
SIDE = 28
K = 4
OUT_SIDE = SIDE // K
POS = OUT_SIDE * OUT_SIDE
TPOS = TILE_IMGS * POS
TAPS = K * K
C = 96
STEM_K = 3 * K * K + 1
DIM = 192
HALF = DIM // 2
HEADS, HEAD_DIM = 12, 16
HIDDEN = 4 * DIM
EXPERTS = 8
TOKENS = POS + 1
SLOT = 64
CHUNKS = TAPS * C // 128
QUAD = 4
QUADS = TILES * TAPS // QUAD
CORNERS = 4
RING = 4
MOE_CHUNKS = -(-(EXPERTS + 1) * DIM // 128)
ROW = SIDE * 2 * C
SLOPE = 0.01
MARK = 2.0 ** 100
ROUND = 2.0 ** 23

STEM_USE, TURN_USE, OFFSET_USE, SAMPLE_USE = 0, 8, 14, 15
FRONT_USES, FRONT_BANKS = 23, 2
(EMBED, TOKMAJOR, YT, QUERY, KV0, KV1, OUTER0, OUTER1, NUMER, DENOM, PROJ, ZT, FC1, _a, _b, FC2,
 FT) = range(17)
MAIN_USES, MAIN_BANKS = 17, 3
MOE_SEQ = [("r", 0), ("h", 6), ("h", 0), ("y", 8), ("h", 1), ("y", 0), ("h", 2), ("y", 1), ("h", 3),
           ("y", 2), ("y", 3), ("h", 4), ("y", 4), ("h", 5), ("y", 5), ("y", 6), ("y", 7)]
MOE_USES, MOE_BANKS = len(MOE_SEQ), 3
LAST_H = MOE_SEQ.index(("h", 5))
H_ORDER = [n for kind, n in MOE_SEQ if kind == "h"]

GATHERED = (QUADS // RING) * QUAD * 16
TABLE_WRITES = TILES * K * 2
ACT_MAIN, ACT_MOE = 5, 2
DVE_FRONT, DVE_MAIN, DVE_MOE = 12 + 2 * QUADS, 9, 11

M = "moe.step"
PE_ORDER = [
    *[("front.stem", n) for n in range(8)], ("setup",), ("main.embed",),
    *[("front.turn", n) for n in range(6)], ("front.offsets",),
    (M, 0), (M, 1), ("main.tokens",), (M, 2), (M, 3), ("main.yT",), (M, 4),
    ("main.query",), ("main.kv", 0), ("main.kv", 1), (M, 5), ("main.outer", 0), ("main.outer", 1), (M, 6),
    ("main.numer",), ("main.denom",), (M, 7), ("main.proj",), (M, 8), (M, 9), ("front.sample", 0),
    ("main.zT",), (M, 10), ("front.sample", 1), ("main.fc1", 0), ("main.fc1", 1), ("main.fc1", 2),
    (M, 11), ("front.sample", 2), ("main.fc2",), (M, 12), (M, 13), ("front.sample", 3), (M, 14),
    ("front.sample", 4), (M, 15), (M, 16), ("main.fT",),
    ("front.sample", 5), ("front.sample", 6), ("front.sample", 7),
    ("setup_end",)]
ACT_ORDER = [
    *[("front.stem", n) for n in range(8)], ("setup",), ("main.embed",),
    *[("front.turn", n) for n in range(6)],
    (M, 0), (M, 1), ("main.rstd", 0), (M, 2), ("main.yT",), (M, 4),
    ("main.query",), ("main.kv", 0), ("main.kv", 1), (M, 6),
    (M, 8), ("main.rstd", 1), ("front.sample", 0), ("main.zT",), ("front.sample", 1),
    ("main.fc1", 0), ("main.fc1", 1), ("main.fc1", 2), (M, 11), ("front.sample", 2), (M, 13),
    ("front.sample", 3), ("main.rstd", 2), ("front.sample", 4), ("main.fT",),
    ("front.sample", 5), ("front.sample", 6), ("front.sample", 7),
    ("setup_end",)]
DVE_ORDER = [
    *[("front.leaky", n) for n in range(4)], ("main.embed",), ("front.sampling",), ("setup",),
    (M, 0), ("main.tokens",), (M, 3), ("main.query",), ("main.key", 0), ("main.key", 1), (M, 5),
    ("main.outer", 0), ("main.outer", 1), (M, 7), ("main.attend",), ("front.interpolate", 0),
    ("main.proj",), (M, 9), ("front.interpolate", 1), (M, 10), ("front.interpolate", 2),
    (M, 12), ("front.interpolate", 3), ("main.mlp",), (M, 14), ("front.interpolate", 4), (M, 15), (M, 16),
    ("front.interpolate", 5), ("front.interpolate", 6), ("front.interpolate", 7)]


def build(nc, a, out):
    ctx = ExitStack()
    with ctx:
        def sb(name, shape, dt=F32):
            return ctx.enter_context(nc.sbuf_tensor(name, shape, dt))

        def sem(name):
            return ctx.enter_context(nc.semaphore(name))

        table = nc.dram_tensor("corner_table", (GROUP_IMGS * SIDE * SIDE + SIDE, 2 * C), F32,
                               kind="Internal").ap()

        stem_w = sb("stem_w", [STEM_K, C])
        bn1 = sb("bn1", [STEM_K, 4, C])
        off_w = sb("off_w", [128, CHUNKS, 2 * TAPS])
        off_b = sb("off_b", [TPOS, TILES * TAPS, 2])
        base = sb("base", [TPOS, TILES * TAPS, 2])
        img_base = sb("img_base", [TPOS, TILES * TAPS])
        dcn_w = sb("dcn_w", [128, CHUNKS, DIM])
        bn2 = sb("bn2", [HALF, 5, 2])
        bn2_scale = sb("bn2_scale", [HALF, 2])
        bn2_bias = sb("bn2_bias", [HALF, 2])
        qkv_w = sb("qkv_w", [HALF + 1, 2, 3 * DIM])
        proj_w = sb("proj_w", [HALF + 1, 2, DIM])
        fc1_w = sb("fc1_w", [HALF, 2, HIDDEN])
        fc1_b = sb("fc1_b", [128, HIDDEN // 128])
        fc2_w = sb("fc2_w", [128, HIDDEN // 128, DIM])
        fc2_b = sb("fc2_b", [1, DIM])
        ln_cols = sb("ln_cols", [HALF, 4, 2])
        rows = sb("rows", [1, 3 * DIM])
        moe_w1 = sb("moe_w1", [HALF, 2, (EXPERTS + 1) * DIM])
        moe_w2 = sb("moe_w2", [128, MOE_CHUNKS, DIM])
        router_w = sb("router_w", [HALF, 2, EXPERTS])
        balance = sb("balance", [128, EXPERTS])
        cls_cols = sb("cls_cols", [HALF, 2])
        ident = sb("ident", [128, 128])
        head_mask = sb("head_mask", [HALF, HALF])
        ones_row = sb("ones_row", [1, 128])
        consts = sb("consts", [128, 4])
        NEG1, EPS8, EPS5 = (consts[:, j:j + 1] for j in range(3))

        xcol = sb("xcol", [STEM_K, TILES * TAPS * TPOS])
        H = sb("H", [TPOS, TILES, TAPS * C])
        HT = sb("HT", [128, TILES, CHUNKS, TPOS])
        p_yx = sb("p_yx", [TPOS, TILES * TAPS * 2])
        p_int = sb("p_int", [TPOS, TILES * TAPS * 2])
        dist = sb("dist", [TPOS, TILES * TAPS * 2])
        hat = sb("hat", [TPOS, TILES * TAPS, 2, 2])
        idx_f = sb("idx_f", [TPOS, TILES * TAPS])
        idx = sb("idx", [TPOS, TILES * TAPS], U32)
        corner_w = sb("corner_w", [TPOS, TILES * TAPS * CORNERS])
        G = sb("G", [TPOS, RING, QUAD * CORNERS * C])
        S = sb("S", [TPOS, RING, QUAD * C])
        ST = sb("ST", [128, CHUNKS, TILES, TPOS])

        embed = sb("embed", [HALF, 2, GROUP_IMGS, POS])
        xT = sb("xT", [HALF, 2, GROUP_IMGS * SLOT])
        X0 = sb("X0", [128, TILES, DIM])
        stats = sb("stats", [128, TILES, 6])
        mv = sb("mv", [128, TILES, 2])
        var = sb("var", [128, TILES, 2])
        rstd = sb("rstd", [128, TILES, 2])
        U = sb("U", [128, TILES, DIM])
        Y = sb("Y", [128, TILES, DIM])
        yT = sb("yT", [HALF + 1, 2, GROUP_IMGS * SLOT])
        exp_q = sb("exp_q", [HALF, 2, GROUP_IMGS * TOKENS])
        qT = sb("qT", [HALF, 2, GROUP_IMGS * TOKENS])
        exp_k = sb("exp_k", [128, TILES, DIM])
        kS = sb("kS", [128, TILES, DIM])
        vS = sb("vS", [128, TILES, 2, HALF + 1])
        KV = sb("KV", [HALF, GROUP_IMGS * 2, HALF])
        KS = sb("KS", [HALF, GROUP_IMGS * 2, HALF])
        rden = sb("rden", [HALF, 2 * GROUP_IMGS * TOKENS])
        attT = sb("attT", [HALF + 1, 2, GROUP_IMGS * SLOT])
        XR = sb("XR", [128, TILES, DIM])
        zT = sb("zT", [HALF, 2, GROUP_IMGS * SLOT])
        gT = sb("gT", [128, HIDDEN // 128, GROUP_IMGS * SLOT])
        XM = sb("XM", [128, TILES, DIM])

        X1 = sb("X1", [128, TILES, DIM])
        fT = sb("fT", [HALF, 2, GROUP_IMGS * SLOT])
        score = sb("score", [128, TILES * EXPERTS])
        biased = sb("biased", [128, TILES, EXPERTS + 6])
        top8 = sb("top8", [128, TILES, 8])
        chosen = sb("chosen", [128, TILES, 8])
        marked = sb("marked", [128, TILES, EXPERTS + 6])
        comb = sb("comb", [128, TILES, EXPERTS])
        comb_sum = sb("comb_sum", [128, TILES])
        relu = sb("relu", [128, 2, 2, GROUP_IMGS * TOKENS])
        hidT = sb("hidT", [128, MOE_CHUNKS, GROUP_IMGS * SLOT])

        psum = [ctx.enter_context(nc.psum_tensor(f"bank{b}", [128, 512], F32)) for b in range(8)]

        waits_alone = sem("waits_alone")
        loaded_first, loaded_rest = sem("loaded_first"), sem("loaded_rest")
        moved = sem("moved")
        set_dve, set_act = sem("set_dve"), sem("set_act")
        consts_ready, pads_ready, stem_ready = sem("consts_ready"), sem("pads_ready"), sem("stem_ready")
        shifts_ready, folded, qkv_row_ready = sem("shifts_ready"), sem("folded"), sem("qkv_row_ready")
        front_filled = [sem(f"front_filled{b}") for b in range(FRONT_BANKS)]
        front_freed = [sem(f"front_freed{b}") for b in range(FRONT_BANKS)]
        main_filled = [sem(f"main_filled{b}") for b in range(MAIN_BANKS)]
        main_freed = [sem(f"main_freed{b}") for b in range(MAIN_BANKS)]
        moe_filled = [sem(f"moe_filled{b}") for b in range(MOE_BANKS)]
        moe_freed = [sem(f"moe_freed{b}") for b in range(MOE_BANKS)]
        xcol_loaded = sem("xcol_loaded")
        leaky_done = sem("leaky_done")
        indices_ready = sem("indices_ready")
        table_padded = sem("table_padded")
        table_written = sem("table_written")
        gathered = [sem(f"gathered{r}") for r in range(RING)]
        sampled = sem("sampled")
        embed_copied = sem("embed_copied")
        embedded = sem("embedded")
        var_ready, rstd_ready = sem("var_ready"), sem("rstd_ready")
        normed = sem("normed")
        exp_ready = sem("exp_ready")
        hidden_ready = sem("hidden_ready")
        out_written = sem("out_written")
        chain_front, chain_main, chain_moe = sem("chain_front"), sem("chain_main"), sem("chain_moe")
        act_main, act_moe = sem("act_main"), sem("act_moe")

        class Banks:
            def __init__(self, first, count, uses, filled, freed):
                self.first, self.count, self.filled_sem, self.freed_sem = first, count, filled, freed
                self.per = [len(range(b, uses, count)) for b in range(count)]

            def ap(self, n):
                return psum[self.first + n % self.count]

            def before(self, g, n):
                return g * self.per[n % self.count] + n // self.count

            def claim(self, eng, g, n):
                wait(eng, self.freed_sem[n % self.count], self.before(g, n))

            def evicted(self, eng, g, n):
                wait(eng, self.freed_sem[n % self.count], self.before(g, n) + 1)

            def filled(self, eng, g, n):
                wait(eng, self.filled_sem[n % self.count], self.before(g, n) + 1)

            def fill(self, ins, n):
                ins.then_inc(self.filled_sem[n % self.count], 1)

            def free(self, ins, n):
                ins.then_inc(self.freed_sem[n % self.count], 1)

        def wait(eng, s, value):
            if isinstance(value, int) and value <= 0:
                return
            eng.wait_ge(s, value)

        def wait_alone(eng, s, value):
            if isinstance(value, int) and value <= 0:
                return
            eng.wait_ge(s, value)
            eng.sem_inc(waits_alone, 1)

        front = Banks(0, FRONT_BANKS, FRONT_USES, front_filled, front_freed)
        main = Banks(2, MAIN_BANKS, MAIN_USES, main_filled, main_freed)
        moe = Banks(5, MOE_BANKS, MOE_USES, moe_filled, moe_freed)

        class Chain:
            def __init__(self, eng, s, per):
                self.eng, self.s, self.per, self.n = eng, s, per, 0

            def begin(self, g):
                self.g, self.n = g, 0

            def __call__(self, ins, alone=False):
                self.n += 1
                ins.then_inc(self.s, 1)
                (wait_alone if alone else wait)(self.eng, self.s, self.g * self.per + self.n)

            def end(self):
                assert self.n == self.per, (self.n, self.per)

        def tokens(buf, c=None):
            v = buf if c is None else buf[:, c, :]
            return v.rearrange("p (i s) -> p i s", s=SLOT)[:, :, 0:TOKENS]

        def iterations(eng, order, units):
            def iteration(i, stages):
                for stage, *args in order:
                    kind = stage.split(".")[0]
                    if kind.startswith("setup"):
                        if isinstance(i, int) and i == -1:
                            units[stage]()
                    elif kind in stages:
                        units[stage](i + {"front": 1, "main": 0, "moe": -1}[kind], *args)
            iteration(-1, ("front",))
            iteration(0, ("front", "main"))
            with eng.Fori(1, GROUPS - 1) as i:
                iteration(i, ("front", "main", "moe"))
            iteration(GROUPS - 1, ("main", "moe"))
            iteration(GROUPS, ("moe",))

        FIRST = [(stem_w[:], "stem_w"), (bn1[:], "bn1"), (ident[:], "ident")]
        REST = [(off_w[:], "off_w"), (off_b[:], "off_b"), (base[:], "base"), (img_base[:], "img_base"),
                (bn2[:], "bn2"), (dcn_w[:], "dcn_w"), (head_mask[:], "head_mask"), (ln_cols[:], "ln_cols"),
                (cls_cols[:], "cls_cols"), (qkv_w[0:HALF], "qkv_w"), (rows[:], "qkv_b"),
                (proj_w[0:HALF], "proj_w"), (proj_w[HALF:HALF + 1, 1, :], "proj_b"),
                (fc1_w[:], "fc1_w"), (fc1_b[:], "fc1_b"), (fc2_w[:], "fc2_w"), (fc2_b[:], "fc2_b"),
                (router_w[:], "router_w"), (balance[:], "balance"), (moe_w1[:], "moe_w1"),
                (moe_w2[:], "moe_w2")]

        block = ctx.enter_context(nc.Block())

        @block.sync
        def _(sp):
            def load_x(g):
                if isinstance(g, int) and g == 0:
                    return
                front.filled(sp, g - 1, STEM_USE + 7)
                front.filled(sp, g - 1, STEM_USE + 6)
                sp.dma_start(xcol[:, :], a["xcol"][:, bass.ds(g * xcol.shape[1], xcol.shape[1])])\
                    .then_inc(xcol_loaded, 16)

            def write_table(g):
                for r in range(RING):
                    wait(sp, gathered[r], g * GATHERED)
                for t in range(TILES):
                    wait(sp, leaky_done, g * 4 + 2 * t + 2)
                    for kh in range(K):
                        src = H[:, t, kh * K * C:(kh + 1) * K * C].rearrange("p (w c) -> p w c", w=K)
                        for upper in range(2):
                            first = SIDE + t * TILE_IMGS * SIDE * SIDE + (kh - upper) * SIDE
                            dst = bass.AP(table.tensor, first * 2 * C + upper * C,
                                          [[K * ROW, TILE_IMGS * OUT_SIDE], [K * 2 * C, OUT_SIDE],
                                           [2 * C, K], [1, C]])
                            sp.dma_start(dst, src).then_inc(table_written, 16)

            def write_out(g):
                moe.evicted(sp, g, MOE_USES - 1)
                view = out.rearrange("(g t s) n c -> s n g t c", t=TILES, s=TILE_IMGS)
                for s in range(TILE_IMGS):
                    sp.dma_start(view[s][:, bass.ds(g, 1)].rearrange("n g t c -> n (g t) c"),
                                 X1[s * SLOT:s * SLOT + TOKENS, :, :]).then_inc(out_written, 16)

            def setup():
                sp.wait_ge(qkv_row_ready, 1)
                sp.dma_start(qkv_w[HALF:HALF + 1, 1, :], rows[:, :]).then_inc(moved, 16)

            for dst, name in FIRST:
                sp.dma_start(dst, a[name]).then_inc(loaded_first, 16)
            sp.dma_start(xcol[:, :], a["xcol"][:, 0:xcol.shape[1]]).then_inc(xcol_loaded, 16)
            for dst, name in REST:
                sp.dma_start(dst, a[name]).then_inc(loaded_rest, 16)
            sp.wait_ge(pads_ready, 10)
            for r, half in ((0, 0), (GROUP_IMGS * SIDE, 1)):
                sp.dma_start(table[r * SIDE:(r + 1) * SIDE, half * C:(half + 1) * C], gT[0:SIDE, 0, 0:C])\
                    .then_inc(table_padded, 16)
            iterations(sp, [("front.load",), ("front.table",), ("setup",), ("moe.out",)],
                       {"front.load": load_x, "front.table": write_table, "moe.out": write_out,
                        "setup": setup})
            sp.wait_ge(out_written, GROUPS * TILE_IMGS * 16)
            sp.wait_ge(table_written, GROUPS * TABLE_WRITES * 16)

        @block.gpsimd
        def _(pool):
            def gather(g):
                pool.wait_ge(table_written, (g + 1) * TABLE_WRITES * 16)
                wait_alone(pool, indices_ready, g + 1)
                for n in range(QUADS):
                    wait_alone(pool, sampled, g * QUADS + n - RING + 1)
                    for k in range(QUAD):
                        tap = n * QUAD + k
                        nc.gpsimd.indirect_dma_start(
                            out=G[:, n % RING, k * CORNERS * C:(k + 1) * CORNERS * C], out_offset=None,
                            in_=table[:, :],
                            in_offset=bass.IndirectOffsetOnAxis(ap=idx[:, tap:tap + 1], axis=0),
                        ).then_inc(gathered[n % RING], 16)

            for j, (pad, value) in enumerate((
                    (xT[:], 0.0), (attT[0:HALF], 0.0), (attT[HALF:HALF + 1], 1.0), (yT[HALF:HALF + 1], 1.0),
                    (vS[:, :, :, HALF:HALF + 1], 1.0), (ones_row[:], 1.0), (biased[:, :, EXPERTS:], -MARK),
                    (chosen[:, :, 2:], -MARK), (gT[:], 0.0), (hidT[:], 0.0))):
                wait(pool, pads_ready, j)
                nc.gpsimd.memset(pad, value).then_inc(pads_ready, 1)
            pool.wait_ge(pads_ready, 10)
            pool.wait_ge(table_padded, 32)
            iterations(pool, [("front.gather",)], {"front.gather": gather})

        @block.tensor
        def _(pe):
            mm = nc.tensor.matmul

            def stem(g, n):
                if n == 0:
                    pe.wait_ge(xcol_loaded, (g + 1) * 16)
                front.claim(pe, g, STEM_USE + n)
                bank = front.ap(STEM_USE + n)
                for k in range(QUAD):
                    at = (n * QUAD + k) * TPOS
                    ins = mm(bank[0:TPOS, k * C:(k + 1) * C], xcol[:, at:at + TPOS], stem_w[:, :],
                             start=True, stop=True)
                front.fill(ins, STEM_USE + n)

            def turn_stem(g, n):
                t, j = divmod(n, 3)
                if j == 0:
                    pe.wait_ge(leaky_done, g * 4 + 2 * t + 2)
                front.claim(pe, g, TURN_USE + n)
                bank = front.ap(TURN_USE + n)
                for k in range(4):
                    at = (4 * j + k) * 128
                    ins = nc.tensor.transpose(bank[:, k * TPOS:(k + 1) * TPOS], H[:, t, at:at + 128],
                                              ident[0:TPOS, 0:TPOS])
                front.fill(ins, TURN_USE + n)

            def offsets(g):
                front.evicted(pe, g, TURN_USE + 4)
                front.evicted(pe, g, TURN_USE + 5)
                front.claim(pe, g, OFFSET_USE)
                bank = front.ap(OFFSET_USE)
                for t in range(TILES):
                    for c in range(CHUNKS):
                        ins = mm(bank[0:TPOS, t * 32:(t + 1) * 32], HT[:, t, c, :], off_w[:, c, :],
                                 start=(c == 0), stop=(c == CHUNKS - 1))
                front.fill(ins, OFFSET_USE)

            def turn_sample(g, n):
                pe.wait_ge(sampled, g * QUADS + n + 1)
                front.claim(pe, g, SAMPLE_USE + n)
                bank = front.ap(SAMPLE_USE + n)
                for k in range(3):
                    ins = nc.tensor.transpose(bank[:, k * TPOS:(k + 1) * TPOS],
                                              S[:, n % RING, k * 128:(k + 1) * 128],
                                              ident[0:TPOS, 0:TPOS])
                front.fill(ins, SAMPLE_USE + n)

            def embed_patches(g):
                front.evicted(pe, g, SAMPLE_USE + QUADS - 2)
                front.evicted(pe, g, SAMPLE_USE + QUADS - 1)
                main.claim(pe, g, EMBED)
                bank = main.ap(EMBED)
                n = TILES * TPOS
                for m in range(2):
                    for c in range(CHUNKS):
                        ins = mm(bank[0:HALF, m * n:(m + 1) * n], dcn_w[:, c, m * HALF:(m + 1) * HALF],
                                 ST[:, c, :, :].rearrange("p t s -> p (t s)"),
                                 start=(c == 0), stop=(c == CHUNKS - 1))
                main.fill(ins, EMBED)

            def to_tokens(g):
                pe.wait_ge(embedded, g + 1)
                main.claim(pe, g, TOKMAJOR)
                bank = main.ap(TOKMAJOR)
                for t in range(TILES):
                    for c in range(2):
                        at = t * DIM + c * HALF
                        ins = nc.tensor.transpose(bank[:, at:at + HALF], xT[:, c, t * 128:(t + 1) * 128],
                                                  ident[0:HALF, 0:HALF])
                main.fill(ins, TOKMAJOR)

            def to_features(g, use, norm):
                pe.wait_ge(normed, g * 3 + norm + 1)
                main.claim(pe, g, use)
                bank = main.ap(use)
                for t in range(TILES):
                    for c in range(2):
                        at = c * 256 + t * 128
                        ins = nc.tensor.transpose(bank[0:HALF, at:at + 128],
                                                  Y[:, t, c * HALF:(c + 1) * HALF], ident[:, :])
                main.fill(ins, use)

            def chunk(c, buf):
                return buf[0:HALF + c, c, :]

            def query(g):
                main.evicted(pe, g, YT)
                main.claim(pe, g, QUERY)
                bank = main.ap(QUERY)
                n = GROUP_IMGS * TOKENS
                for m in range(2):
                    for c in range(2):
                        ins = mm(bank[0:HALF, m * n:(m + 1) * n],
                                 chunk(c, qkv_w)[:, m * HALF:(m + 1) * HALF], tokens(chunk(c, yT)),
                                 start=(c == 0), stop=(c == 1))
                main.fill(ins, QUERY)

            def key_value(g, t):
                main.claim(pe, g, KV0 + t)
                bank = main.ap(KV0 + t)
                for c in range(2):
                    ins = mm(bank[:, 0:2 * DIM], chunk(c, yT)[:, t * 128:(t + 1) * 128],
                             chunk(c, qkv_w)[:, DIM:], start=(c == 0), stop=(c == 1))
                main.fill(ins, KV0 + t)

            def outer(g, s):
                if s == 0:
                    main.evicted(pe, g, KV0)
                    main.evicted(pe, g, KV1)
                main.claim(pe, g, OUTER0 + s)
                bank = main.ap(OUTER0 + s)
                w = HALF + 1
                p = slice(s * SLOT, s * SLOT + TOKENS)
                for t in range(TILES):
                    for c in range(2):
                        at = (t * 2 + c) * w
                        ins = mm(bank[0:HALF, at:at + w], kS[p, t, c * HALF:(c + 1) * HALF], vS[p, t, c, :],
                                 start=True, stop=True)
                main.fill(ins, OUTER0 + s)

            def attend(g, use):
                table_ = {NUMER: KV, DENOM: KS}[use]
                if use == NUMER:
                    main.evicted(pe, g, QUERY)
                    main.evicted(pe, g, OUTER0)
                    main.evicted(pe, g, OUTER1)
                main.claim(pe, g, use)
                bank = main.ap(use)
                for c in range(2):
                    for i in range(GROUP_IMGS):
                        at = (c * GROUP_IMGS + i) * TOKENS
                        t, s = divmod(i, TILE_IMGS)
                        ins = mm(bank[0:HALF, at:at + TOKENS], table_[:, (s * TILES + t) * 2 + c, :],
                                 qT[:, c, i * TOKENS:(i + 1) * TOKENS], start=True, stop=True)
                main.fill(ins, use)

            def project(g):
                main.evicted(pe, g, NUMER)
                main.claim(pe, g, PROJ)
                bank = main.ap(PROJ)
                for t in range(TILES):
                    for c in range(2):
                        ins = mm(bank[:, t * DIM:(t + 1) * DIM], chunk(c, attT)[:, t * 128:(t + 1) * 128],
                                 chunk(c, proj_w), start=(c == 0), stop=(c == 1))
                main.fill(ins, PROJ)

            def fc1(g, n):
                main.evicted(pe, g, ZT)
                main.claim(pe, g, FC1 + n)
                bank = main.ap(FC1 + n)
                w = GROUP_IMGS * TOKENS
                for k in range(2):
                    m = (2 * n + k) * 128
                    for c in range(2):
                        ins = mm(bank[:, k * w:(k + 1) * w], fc1_w[:, c, m:m + 128], tokens(zT, c),
                                 start=(c == 0), stop=(c == 1))
                main.fill(ins, FC1 + n)

            def fc2(g):
                for n in range(3):
                    main.evicted(pe, g, FC1 + n)
                main.claim(pe, g, FC2)
                bank = main.ap(FC2)
                for t in range(TILES):
                    dst = bank[:, t * DIM:(t + 1) * DIM]
                    mm(dst, ones_row[:, :], fc2_b[:, :], start=True, stop=False)
                    for m in range(HIDDEN // 128):
                        ins = mm(dst, gT[:, m, t * 128:(t + 1) * 128], fc2_w[:, m, :],
                                 start=False, stop=(m == HIDDEN // 128 - 1))
                main.fill(ins, FC2)

            def router(g, n):
                main.evicted(pe, g, FT)
                moe.claim(pe, g, n)
                bank = moe.ap(n)
                for t in range(TILES):
                    for c in range(2):
                        ins = mm(bank[:, t * EXPERTS:(t + 1) * EXPERTS], fT[:, c, t * 128:(t + 1) * 128],
                                 router_w[:, c, :], start=(c == 0), stop=(c == 1))
                moe.fill(ins, n)

            def hidden(g, n, pair):
                moe.claim(pe, g, n)
                bank = moe.ap(n)
                w = GROUP_IMGS * TOKENS
                for k in range(2):
                    at = (2 * pair + k) * 128
                    rows_ = min(128, (EXPERTS + 1) * DIM - at)
                    for c in range(2):
                        ins = mm(bank[0:rows_, k * w:(k + 1) * w], moe_w1[:, c, at:at + rows_],
                                 tokens(fT, c), start=(c == 0), stop=(c == 1))
                moe.fill(ins, n)

            def expert_out(g, n, e):
                parts = [(e * DIM // 128, slice(0, 128)), (e * DIM // 128 + 1, slice(0, 64))] if e % 2 == 0 \
                    else [(e * DIM // 128, slice(64, 128)), (e * DIM // 128 + 1, slice(0, 128))]
                pair = max(H_ORDER.index(c // 2) for c, _ in parts)
                pe.wait_ge(hidden_ready, g * len(H_ORDER) + pair + 1)
                moe.claim(pe, g, n)
                bank = moe.ap(n)
                for t in range(TILES):
                    for j, (c, p) in enumerate(parts):
                        ins = mm(bank[:, t * DIM:(t + 1) * DIM], hidT[p, c, t * 128:(t + 1) * 128],
                                 moe_w2[p, c, :], start=(j == 0), stop=(j == 1))
                moe.fill(ins, n)

            def moe_step(g, n):
                kind, k = MOE_SEQ[n]
                router(g, n) if kind == "r" else (hidden if kind == "h" else expert_out)(g, n, k)

            def setup():
                pe.wait_ge(loaded_rest, 16 * len(REST))
                pe.wait_ge(pads_ready, 10)
                for h in range(2):
                    for c in range(2):
                        ins = mm(psum[2 + h][0:1, 0:288], ln_cols[:, 1, c:c + 1],
                                 qkv_w[0:HALF, c, h * 288:(h + 1) * 288], start=(c == 0), stop=(c == 1))
                for m in range(HIDDEN // 128):
                    for c in range(2):
                        ins = mm(psum[4][:, m:m + 1], fc1_w[:, c, m * 128:(m + 1) * 128],
                                 ln_cols[:, 3, c:c + 1], start=(c == 0), stop=(c == 1))
                ins.then_inc(shifts_ready, 1)

            def setup_end():
                pe.wait_ge(folded, 1)
                pe.wait_ge(moved, 16)

            pe.wait_ge(loaded_first, 16 * len(FIRST))
            pe.wait_ge(stem_ready, 1)
            iterations(pe, PE_ORDER, {
                "setup": setup, "setup_end": setup_end,
                "front.stem": stem, "front.turn": turn_stem, "front.offsets": offsets,
                "front.sample": turn_sample, "main.embed": embed_patches, "main.tokens": to_tokens,
                "main.yT": lambda g: to_features(g, YT, 0), "main.zT": lambda g: to_features(g, ZT, 1),
                "main.fT": lambda g: to_features(g, FT, 2), "main.query": query, "main.kv": key_value,
                "main.outer": outer, "main.numer": lambda g: attend(g, NUMER),
                "main.denom": lambda g: attend(g, DENOM), "main.proj": project, "main.fc1": fc1,
                "main.fc2": fc2, "moe.step": moe_step})

        @block.scalar
        def _(act):
            A = nc.scalar.activation
            link_main, link_moe = Chain(act, act_main, ACT_MAIN), Chain(act, act_moe, ACT_MOE)
            w = GROUP_IMGS * TOKENS

            def stem(g, n):
                if n == 0:
                    wait(act, table_written, g * TABLE_WRITES * 16)
                front.filled(act, g, STEM_USE + n)
                t, q = divmod(n, 4)
                front.free(A(H[:, t, q * QUAD * C:(q + 1) * QUAD * C],
                             front.ap(STEM_USE + n)[0:TPOS, 0:QUAD * C], ACT.Copy), STEM_USE + n)

            def turn_stem(g, n):
                front.filled(act, g, TURN_USE + n)
                t, j = divmod(n, 3)
                front.free(A(HT[:, t, 4 * j:4 * j + 4, :].rearrange("p c s -> p (c s)"),
                             front.ap(TURN_USE + n)[:, 0:4 * TPOS], ACT.Copy), TURN_USE + n)

            def turn_sample(g, n):
                if n == 0 and not (isinstance(g, int) and g == 0):
                    main.filled(act, g - 1, EMBED)
                front.filled(act, g, SAMPLE_USE + n)
                t, q = divmod(n, 4)
                front.free(A(ST[:, 3 * q:3 * q + 3, t, :],
                             front.ap(SAMPLE_USE + n)[:, 0:3 * TPOS].rearrange("p (c s) -> p c s", c=3),
                             ACT.Copy), SAMPLE_USE + n)

            def embed_copy(g):
                main.filled(act, g, EMBED)
                wait(act, embedded, g)
                link_main.begin(g)
                n = TILES * TPOS
                for m in range(2):
                    ins = A(embed[:, m, :, :].rearrange("p i s -> p (i s)"),
                            main.ap(EMBED)[0:HALF, m * n:(m + 1) * n], ACT.Identity,
                            bias=bn2_bias[:, m:m + 1], scale=bn2_scale[:, m:m + 1])
                    if m == 0:
                        ins.then_inc(embed_copied, 1)
                main.free(ins, EMBED)

            def inverse_root(g, norm):
                act.wait_ge(var_ready, g * 3 + norm + 1)
                n = 4 if norm == 0 else 2
                v = var[:].rearrange("p a b -> p (a b)")[:, 0:n]
                link_main(A(v, v, ACT.Ln))
                A(rstd[:].rearrange("p a b -> p (a b)")[:, 0:n], v, ACT.Exp, scale=-0.5)\
                    .then_inc(rstd_ready, 1)

            def evict_features(g, use, dst):
                main.filled(act, g, use)
                if use == FT and not (isinstance(g, int) and g == 0):
                    moe.filled(act, g - 1, LAST_H)
                main.free(A(dst[0:HALF].rearrange("p c s -> p (c s)"), main.ap(use)[0:HALF, :], ACT.Copy),
                          use)

            def exp_query(g):
                main.filled(act, g, QUERY)
                A(exp_q[:].rearrange("p c s -> p (c s)"), main.ap(QUERY)[0:HALF, 0:2 * w], ACT.Exp,
                  bias=NEG1[0:HALF]).then_inc(exp_ready, 1)

            def key_value(g, t):
                main.filled(act, g, KV0 + t)
                bank = main.ap(KV0 + t)
                link_main(A(vS[:, t, :, 0:HALF], bank[:, DIM:2 * DIM].rearrange("p (c f) -> p c f", c=2),
                            ACT.Copy))
                A(exp_k[:, t, :], bank[:, 0:DIM], ACT.Exp, bias=NEG1).then_inc(exp_ready, 1)

            def gelu(g, n):
                main.filled(act, g, FC1 + n)
                for k in range(2):
                    m = 2 * n + k
                    ins = A(tokens(gT, m),
                            main.ap(FC1 + n)[:, k * w:(k + 1) * w].rearrange("p (i s) -> p i s", s=TOKENS),
                            ACT.Gelu, bias=fc1_b[:, m:m + 1])
                main.free(ins, FC1 + n)

            def moe_step(g, n):
                kind, pair = MOE_SEQ[n]
                if kind == "y":
                    return
                moe.filled(act, g, n)
                if kind == "r":
                    link_moe.begin(g)
                    moe.free(A(score[:, :], moe.ap(n)[:, 0:TILES * EXPERTS], ACT.Exp, scale=-1.0), n)
                    return
                if pair == H_ORDER[0] and not (isinstance(g, int) and g == 0):
                    moe.filled(act, g - 1, MOE_USES - 1)
                tmp = relu[:, H_ORDER.index(pair) % 2]
                chunks = [2] if pair < 6 else [1, 1]
                at, last = 0, None
                for k, width in enumerate(chunks):
                    r = 64 if k else 128
                    src = moe.ap(n)[0:r, k * w:(k + width) * w]
                    ins = A(tmp[0:r, k:k + width, :].rearrange("p c s -> p (c s)"), src, ACT.Relu)
                    if k < len(chunks) - 1:
                        link_moe(ins)
                moe.free(ins, n)
                moe.evicted(act, g, n)
                for k, width in enumerate(chunks):
                    r = 64 if k else 128
                    c = 2 * pair + k
                    dst = hidT[0:r, c:c + width, :].rearrange("p c (i s) -> p c i s", s=SLOT)[:, :, :, 0:TOKENS]
                    ins = A(dst, tmp[0:r, k:k + width, :].rearrange("p c (i s) -> p c i s", s=TOKENS),
                            ACT.Square)
                    if k < len(chunks) - 1:
                        link_moe(ins)
                ins.then_inc(hidden_ready, 1)

            act.wait_ge(consts_ready, 3)
            act.wait_ge(loaded_first, 16 * len(FIRST))
            A(bn1[:, 3, :], bn1[:, 3, :], ACT.Ln, bias=EPS5[0:STEM_K]).then_inc(set_act, 1)
            act.wait_ge(set_act, 1)
            A(bn1[:, 3, :], bn1[:, 3, :], ACT.Exp, scale=-0.5).then_inc(set_act, 1)

            def setup():
                act.wait_ge(loaded_rest, 16 * len(REST))
                act.wait_ge(pads_ready, 10)
                A(bn2[:, 4, :], bn2[:, 4, :], ACT.Ln, bias=EPS5[0:HALF]).then_inc(set_act, 1)
                act.wait_ge(set_act, 3)
                A(bn2[:, 4, :], bn2[:, 4, :], ACT.Exp, scale=-0.5).then_inc(set_act, 1)

            def setup_end():
                act.wait_ge(folded, 1)

            iterations(act, ACT_ORDER, {
                "setup": setup, "setup_end": setup_end,
                "front.stem": stem, "front.turn": turn_stem, "front.sample": turn_sample,
                "main.embed": embed_copy, "main.rstd": inverse_root,
                "main.yT": lambda g: evict_features(g, YT, yT), "main.zT": lambda g: evict_features(g, ZT, zT),
                "main.fT": lambda g: evict_features(g, FT, fT), "main.query": exp_query,
                "main.kv": key_value, "main.fc1": gelu, "moe.step": moe_step})

        @block.vector
        def _(dve):
            v = nc.vector
            link_front = Chain(dve, chain_front, DVE_FRONT)
            link_main = Chain(dve, chain_main, DVE_MAIN)
            link_moe = Chain(dve, chain_moe, DVE_MOE)
            half_taps = TAPS * C // 2

            def leaky(g, n):
                front.evicted(dve, g, STEM_USE + 2 * n)
                front.evicted(dve, g, STEM_USE + 2 * n + 1)
                h = H[:, n // 2, (n % 2) * half_taps:(n % 2 + 1) * half_taps]
                v.scalar_tensor_tensor(out=h, in0=h, scalar=SLOPE, in1=h, op0=ALU.mult, op1=ALU.max)\
                    .then_inc(leaky_done, 1)

            def sampling(g):
                link_front.begin(g)
                if isinstance(g, int) and g == 0:
                    dve.wait_ge(loaded_rest, 16 * len(REST))
                front.filled(dve, g, OFFSET_USE)
                n = TILES * TAPS * 2
                ins = v.tensor_tensor(p_yx[:], front.ap(OFFSET_USE)[0:TPOS, 0:n],
                                      off_b[:].rearrange("p t y -> p (t y)"), ALU.add)
                front.free(ins, OFFSET_USE)
                front.evicted(dve, g, OFFSET_USE)
                link_front(v.tensor_tensor(p_yx[:], p_yx[:], base[:].rearrange("p t y -> p (t y)"), ALU.add))
                link_front(v.tensor_scalar(p_int[:], p_yx[:], 0.5, SIDE - 1.5, ALU.max, ALU.min))
                link_front(v.tensor_scalar(p_int[:], p_int[:], -0.5, ROUND, ALU.add, ALU.add))
                link_front(v.tensor_scalar(p_int[:], p_int[:], -ROUND, None, ALU.add))
                corner = p_int[:].rearrange("p (t y) -> p t y", y=2)
                link_front(v.scalar_tensor_tensor(out=idx_f[:], in0=corner[:, :, 0], scalar=float(SIDE),
                                                  in1=corner[:, :, 1], op0=ALU.mult, op1=ALU.add))
                for r in range(RING):
                    wait(dve, gathered[r], g * GATHERED)
                v.tensor_tensor(idx[:], idx_f[:], img_base[:], ALU.add).then_inc(indices_ready, 1)
                hats = hat[:].rearrange("p t y k -> p (t y) k")
                link_front(v.tensor_tensor(dist[:], p_yx[:], p_int[:], ALU.subtract))
                for k in range(2):
                    link_front(v.scalar_tensor_tensor(out=hats[:, :, k], in0=dist[:], scalar=-1.0, in1=dist[:],
                                                      op0=ALU.mult, op1=ALU.min))
                    if k == 0:
                        link_front(v.tensor_scalar(dist[:], dist[:], -1.0, None, ALU.add))
                flat = hat[:].rearrange("p t y k -> p (t y k)")
                link_front(v.tensor_scalar(flat, flat, 1.0, 0.0, ALU.add, ALU.max))
                cw = corner_w[:].rearrange("p (t x y) -> p t x y", x=2, y=2)
                m = TILES * TAPS
                for x in range(2):
                    link_front(v.tensor_tensor(cw[:, :, x, :], hat[:, :, 1, x:x + 1].to_broadcast([TPOS, m, 2]),
                                               hat[:, :, 0, :], ALU.mult))

            def interpolate(g, n):
                dve.wait_ge(gathered[n % RING], g * GATHERED + (n // RING + 1) * QUAD * 16)
                if n >= RING:
                    front.filled(dve, g, SAMPLE_USE + n - RING)
                elif not (isinstance(g, int) and g == 0):
                    front.filled(dve, g - 1, SAMPLE_USE + n + QUADS - RING)
                m = QUAD * CORNERS
                quad = G[:, n % RING, :]
                q = quad.rearrange("p (m c) -> p m c", c=C)
                link_front(v.tensor_tensor(
                    q, q, corner_w[:, n * m:(n + 1) * m].unsqueeze(2).to_broadcast([TPOS, m, C]), ALU.mult))
                half = quad.rearrange("p (k x r) -> p k x r", x=2, r=2 * C)
                link_front(v.tensor_tensor(half[:, :, 0, :], half[:, :, 0, :], half[:, :, 1, :], ALU.add))
                four = quad.rearrange("p (k y c) -> p k y c", y=CORNERS, c=C)
                v.tensor_tensor(S[:, n % RING, :].rearrange("p (k c) -> p k c", c=C), four[:, :, 0, :],
                                four[:, :, 1, :], ALU.add).then_inc(sampled, 1)

            def embed_leaky(g):
                link_main.begin(g)
                dve.wait_ge(embed_copied, g + 1)
                main.evicted(dve, g, EMBED)
                dst = xT[:].rearrange("p c (i s) -> p (c i) s", s=SLOT)[:, :, 1:TOKENS]
                src = embed[:].rearrange("p c i s -> p (c i) s")
                v.scalar_tensor_tensor(out=dst, in0=src, scalar=SLOPE, in1=src, op0=ALU.mult, op1=ALU.max)\
                    .then_inc(embedded, 1)

            def moments(src):
                for t in range(TILES):
                    ins = v.bn_stats(stats[:, t, :], src[:, t, :])
                link_main(ins, alone=True)
                for t in range(TILES):
                    ins = v.bn_aggr(mv[:, t, :], stats[:, t, :])
                link_main(ins)

            def normalise(dst, src, scale):
                for t in range(TILES):
                    ins = v.tensor_scalar(dst[:, t, :], src[:, t, :], mv[:, t, 0:1], scale(t),
                                          ALU.subtract, ALU.mult)
                return ins

            def norm_tokens(g):
                main.filled(dve, g, TOKMAJOR)
                ins = v.tensor_copy(X0[:].rearrange("p t c -> p (t c)"), main.ap(TOKMAJOR)[:, 0:TILES * DIM])
                main.free(ins, TOKMAJOR)
                main.evicted(dve, g, TOKMAJOR)
                moments(X0)
                link_main(v.tensor_scalar(var[:, :, 0], mv[:, :, 1], 1e-5, None, ALU.add))
                v_ = v.scalar_tensor_tensor(out=var[:, :, 1], in0=var[:, :, 0], scalar=1e-8,
                                            in1=mv[:, :, 1], op0=ALU.mult, op1=ALU.add)
                v_.then_inc(var_ready, 1)
                dve.wait_ge(rstd_ready, g * 3 + 1)
                normalise(Y, X0, lambda t: rstd[:, t, 1:2]).then_inc(normed, 1)
                link_main(normalise(U, X0, lambda t: rstd[:, t, 0:1]))

            def norm_again(g, src, norm, eps):
                moments(src)
                v.tensor_scalar(var[:].rearrange("p a b -> p (a b)")[:, 0:2], mv[:, :, 1], eps, None,
                                ALU.add).then_inc(var_ready, 1)
                dve.wait_ge(rstd_ready, g * 3 + norm + 1)
                r = rstd[:].rearrange("p a b -> p (a b)")
                normalise(Y, src, lambda t: r[:, t:t + 1]).then_inc(normed, 1)

            def elu(g, use, n, dst, e, src):
                dve.wait_ge(exp_ready, g * 3 + n + 1)
                main.free(v.scalar_tensor_tensor(out=dst, in0=e, scalar=1.0, in1=src, op0=ALU.min,
                                                 op1=ALU.max), use)

            def query(g):
                elu(g, QUERY, 0, qT[:].rearrange("p c s -> p (c s)"), exp_q[:].rearrange("p c s -> p (c s)"),
                    main.ap(QUERY)[0:HALF, 0:2 * GROUP_IMGS * TOKENS])

            def key(g, t):
                elu(g, KV0 + t, 1 + t, kS[:, t, :], exp_k[:, t, :], main.ap(KV0 + t)[:, 0:DIM])

            def outer(g, s):
                main.filled(dve, g, OUTER0 + s)
                m = TILES * 2
                kv = main.ap(OUTER0 + s)[0:HALF, 0:m * (HALF + 1)].rearrange("p (m f) -> p m f", m=m)
                mask = head_mask[:].unsqueeze(1).to_broadcast([HALF, m, HALF])
                v.tensor_tensor(KV[:, s * m:(s + 1) * m, :], kv[:, :, 0:HALF], mask, ALU.mult)
                ins = v.tensor_tensor(KS[:, s * m:(s + 1) * m, :],
                                      kv[:, :, HALF:HALF + 1].to_broadcast([HALF, m, HALF]), mask, ALU.mult)
                main.free(ins, OUTER0 + s)

            def attend(g):
                main.filled(dve, g, DENOM)
                n = 2 * GROUP_IMGS * TOKENS
                main.free(v.reciprocal(rden[:, :], main.ap(DENOM)[0:HALF, 0:n]), DENOM)
                main.evicted(dve, g, DENOM)
                dst = attT[0:HALF].rearrange("p c (i s) -> p (c i) s", s=SLOT)[:, :, 0:TOKENS]
                m = 2 * GROUP_IMGS
                ins = v.tensor_tensor(dst, main.ap(NUMER)[0:HALF, 0:n].rearrange("p (m s) -> p m s", m=m),
                                      rden[:].rearrange("p (m s) -> p m s", m=m), ALU.mult)
                main.free(ins, NUMER)

            def project(g):
                main.filled(dve, g, PROJ)
                flat = [b[:].rearrange("p t c -> p (t c)") for b in (XR, U, X0)]
                ins = v.tensor_tensor(flat[0], flat[1], main.ap(PROJ)[:, 0:TILES * DIM], ALU.add)
                main.free(ins, PROJ)
                main.evicted(dve, g, PROJ)
                norm_again(g, XR, 1, 1e-8)
                link_main(v.tensor_tensor(flat[2], flat[2], flat[0], ALU.add))

            def mlp_out(g):
                main.filled(dve, g, FC2)
                flat = [b[:].rearrange("p t c -> p (t c)") for b in (XM, X0)]
                ins = v.tensor_tensor(flat[0], flat[1], main.ap(FC2)[:, 0:TILES * DIM], ALU.add)
                main.free(ins, FC2)
                main.evicted(dve, g, FC2)
                norm_again(g, XM, 2, 1e-5)
                link_main.end()

            def choose(g, n):
                moe.evicted(dve, g, n)
                link_moe.begin(g)
                link_moe(v.tensor_scalar(score[:], score[:], 1.0, None, ALU.add))
                link_moe(v.reciprocal(score[:], score[:]))
                s3 = score[:].rearrange("p (t e) -> p t e", t=TILES)
                link_moe(v.tensor_tensor(biased[:, :, 0:EXPERTS], s3,
                                         balance[:].unsqueeze(1).to_broadcast([128, TILES, EXPERTS]), ALU.add),
                         alone=True)
                for t in range(TILES):
                    ins = v.max(out=top8[:, t, :], in_=biased[:, t, 0:EXPERTS])
                link_moe(ins)
                link_moe(v.tensor_copy(chosen[:, :, 0:2], top8[:, :, 0:2]), alone=True)
                for t in range(TILES):
                    ins = v.match_replace(out=marked[:, t, :], in_to_replace=chosen[:, t, :],
                                          in_values=biased[:, t, :], imm_value=MARK)
                link_moe(ins)
                for t in range(TILES):
                    ins = v.scalar_tensor_tensor(out=comb[:, t, :], in0=marked[:, t, 0:EXPERTS], scalar=MARK,
                                                 in1=s3[:, t, :], op0=ALU.is_equal, op1=ALU.mult,
                                                 accum_out=comb_sum[:, t:t + 1])
                    link_moe(ins)
                link_moe(v.tensor_scalar(comb_sum[:], comb_sum[:], 1e-20, None, ALU.add))
                link_moe(v.reciprocal(comb_sum[:], comb_sum[:]))
                link_moe(v.tensor_tensor(comb[:], comb[:],
                                         comb_sum[:].unsqueeze(2).to_broadcast([128, TILES, EXPERTS]),
                                         ALU.mult))

            def expert_sum(g, n, e):
                moe.filled(dve, g, n)
                if e == EXPERTS:
                    wait(dve, out_written, g * TILE_IMGS * 16)
                    flat = [b[:].rearrange("p t c -> p (t c)") for b in (X1, XM)]
                    ins = v.tensor_tensor(flat[0], flat[1], moe.ap(n)[:, 0:TILES * DIM], ALU.add)
                else:
                    for t in range(TILES):
                        ins = v.scalar_tensor_tensor(
                            out=X1[:, t, :], in0=moe.ap(n)[:, t * DIM:(t + 1) * DIM], scalar=comb[:, t, e:e + 1],
                            in1=X1[:, t, :], op0=ALU.mult, op1=ALU.add)
                moe.free(ins, n)
                moe.evicted(dve, g, n)
                if n == MOE_USES - 1:
                    link_moe.end()

            def moe_step(g, n):
                kind, k = MOE_SEQ[n]
                if kind == "r":
                    choose(g, n)
                elif kind == "y":
                    expert_sum(g, n, k)

            for j, value in enumerate((-1.0, 1e-8, 1e-5)):
                v.memset(consts[:, j:j + 1], value).then_inc(consts_ready, 1)
            step = Chain(dve, set_dve, 0)
            step.begin(0)
            dve.wait_ge(loaded_first, 16 * len(FIRST))
            dve.wait_ge(set_act, 2)
            step(v.tensor_tensor(bn1[:, 0, :], bn1[:, 0, :], bn1[:, 3, :], ALU.mult))
            step(v.tensor_tensor(stem_w[0:1, :], stem_w[0:1, :], bn1[0:1, 2, :], ALU.subtract))
            step(v.tensor_tensor(stem_w[:, :], stem_w[:, :], bn1[:, 0, :], ALU.mult))
            v.tensor_tensor(stem_w[0:1, :], stem_w[0:1, :], bn1[0:1, 1, :], ALU.add).then_inc(stem_ready, 1)

            def setup():
                dve.wait_ge(pads_ready, 10)
                dve.wait_ge(set_act, 4)
                step(v.tensor_tensor(bn2_scale[:], bn2[:, 1, :], bn2[:, 4, :], ALU.mult))
                step(v.tensor_tensor(bn2_bias[:], bn2[:, 0, :], bn2[:, 3, :], ALU.subtract))
                step(v.tensor_tensor(bn2_bias[:], bn2_bias[:], bn2_scale[:], ALU.mult))
                step(v.tensor_tensor(bn2_bias[:], bn2_bias[:], bn2[:, 2, :], ALU.add))
                for c in range(2):
                    for i in range(GROUP_IMGS):
                        ins = v.tensor_copy(xT[:, c, i * SLOT:i * SLOT + 1], cls_cols[:, c:c + 1])
                step(ins)
                dve.wait_ge(shifts_ready, 1)
                for h in range(2):
                    part = rows[:, h * 288:(h + 1) * 288]
                    ins = v.tensor_tensor(part, part, psum[2 + h][0:1, 0:288], ALU.add)
                step(ins)
                v.tensor_scalar(rows[:, 0:2 * DIM], rows[:, 0:2 * DIM], 1.0, None, ALU.add)\
                    .then_inc(qkv_row_ready, 1)
                step(v.tensor_tensor(fc1_b[:], fc1_b[:], psum[4][:, 0:HIDDEN // 128], ALU.add))
                for c in range(2):
                    step(v.tensor_scalar(qkv_w[0:HALF, c, :], qkv_w[0:HALF, c, :], ln_cols[:, 0, c:c + 1], None,
                                         ALU.mult))
                    ins = v.tensor_scalar(fc1_w[:, c, :], fc1_w[:, c, :], ln_cols[:, 2, c:c + 1], None, ALU.mult)
                    step(ins) if c == 0 else ins.then_inc(folded, 1)

            iterations(dve, DVE_ORDER, {
                "setup": setup,
                "front.leaky": leaky, "front.sampling": sampling, "front.interpolate": interpolate,
                "main.embed": embed_leaky, "main.tokens": norm_tokens, "main.query": query, "main.key": key,
                "main.outer": outer, "main.attend": attend, "main.proj": project, "main.mlp": mlp_out,
                "moe.step": moe_step})


def kernel(**inputs):
    import numpy as np
    import concourse.bacc as bacc
    from concourse.bass_utils import run_bass_kernel_spmd

    x = {k.removeprefix("L0_"): np.asarray(v) for k, v in inputs.items()}

    def chunks(w, p):
        return w.reshape(-1, p, w.shape[-1]).transpose(1, 0, 2)

    def cols(*vs):
        return np.stack([v.reshape(2, HALF).T for v in vs], 1)

    img = x["x"].reshape(GROUPS, TILES, TILE_IMGS, 3, OUT_SIDE, K, K, OUT_SIDE, K, K)
    patches = img.transpose(3, 6, 9, 0, 1, 5, 8, 2, 4, 7).reshape(STEM_K - 1, -1)
    taps = lambda w: w.transpose(2, 3, 1, 0).reshape(TAPS * C, -1)
    experts1 = np.concatenate([x["ffn_w1"].transpose(1, 0, 2).reshape(DIM, -1), x["ffn_w_fc_sh"]], 1)
    experts2 = np.concatenate([x["ffn_w2"].reshape(-1, DIM), x["ffn_w_proj_sh"]], 0)
    experts2 = np.concatenate([experts2, np.zeros((-len(experts2) % 128, DIM), np.float32)], 0)
    k = np.arange(K)
    at = np.stack(np.meshgrid(np.arange(OUT_SIDE) * K, np.arange(OUT_SIDE) * K, indexing="ij"), -1)
    tap = np.stack(np.meshgrid(k, k, indexing="ij"), -1).reshape(1, TAPS, 2)
    base = np.tile(at.reshape(POS, 1, 2) + tap, (TILE_IMGS, TILES, 1))
    image = np.arange(TILES).reshape(1, TILES, 1) * TILE_IMGS + np.repeat(np.arange(TILE_IMGS), POS).reshape(-1, 1, 1)
    img_base = np.broadcast_to(image * SIDE * SIDE, (TPOS, TILES, TAPS))
    head = np.arange(HALF) // HEAD_DIM
    a = {
        "xcol": np.concatenate([np.ones((1, patches.shape[1]), np.float32), patches], 0),
        "stem_w": np.concatenate([x["tok_stem_b"][None], x["tok_stem_w"].reshape(C, -1).T], 0),
        "bn1": np.broadcast_to(np.stack([x["tok_bn1_" + n] for n in "gbmv"]), (STEM_K, 4, C)),
        "ident": np.eye(128, dtype=np.float32),
        "off_w": chunks(taps(x["tok_off_w"]), 128),
        "off_b": np.broadcast_to(np.tile(x["tok_off_b"].reshape(TAPS, 2), (TILES, 1)), (TPOS, TILES * TAPS, 2)),
        "base": base.astype(np.float32),
        "img_base": (img_base.reshape(TPOS, -1) + SIDE).astype(np.float32),
        "bn2": cols(x["tok_dcn_b"], *[x["tok_bn2_" + n] for n in "gbmv"]),
        "dcn_w": chunks(taps(x["tok_dcn_w"]), 128),
        "head_mask": (head[:, None] == head[None]).astype(np.float32),
        "ln_cols": cols(*[x["attn_" + n] for n in ("ln1_w", "ln1_b", "ln2_w", "ln2_b")]),
        "cls_cols": x["cls_tok"].reshape(2, HALF).T,
        "qkv_w": chunks(x["attn_qkv_w"], HALF),
        "qkv_b": x["attn_qkv_b"][None],
        "proj_w": chunks(x["attn_proj_w"], HALF),
        "proj_b": x["attn_proj_b"][None],
        "fc1_w": chunks(x["attn_fc1_w"], HALF),
        "fc1_b": x["attn_fc1_b"].reshape(-1, 128).T,
        "fc2_w": chunks(x["attn_fc2_w"], 128),
        "fc2_b": x["attn_fc2_b"][None],
        "router_w": chunks(x["ffn_router_w"].T, HALF),
        "balance": np.broadcast_to(x["ffn_balance_bias"], (128, EXPERTS)),
        "moe_w1": chunks(experts1, HALF),
        "moe_w2": chunks(experts2, 128),
    }
    nc = bacc.Bacc("TRN2", target_bir_lowering=False, num_devices=1)
    arrays = {f"in_{n}": np.ascontiguousarray(v) for n, v in a.items()}
    args = {n: nc.dram_tensor(f"in_{n}", v.shape, F32, kind="ExternalInput").ap() for n, v in a.items()}
    out = nc.dram_tensor("out", (IMAGES, TOKENS, DIM), F32, kind="ExternalOutput").ap()
    build(nc, args, out)
    return run_bass_kernel_spmd(nc, [arrays], core_ids=[0]).results[0]["out"]
```

```python
from contextlib import ExitStack

import concourse.bass as bass
from concourse import mybir

F32 = mybir.dt.float32
U32 = mybir.dt.uint32
ALU = mybir.AluOpType
ACT = mybir.ActivationFunctionType

IMAGES, GROUP_IMGS, TILE_IMGS = 32, 4, 2
GROUPS = IMAGES // GROUP_IMGS
TILES = GROUP_IMGS // TILE_IMGS
SIDE = 28
K = 4
OUT_SIDE = SIDE // K
POS = OUT_SIDE * OUT_SIDE
TPOS = TILE_IMGS * POS
TAPS = K * K
C = 96
STEM_K = 3 * K * K + 1
DIM = 192
HALF = DIM // 2
HEADS, HEAD_DIM = 12, 16
HIDDEN = 4 * DIM
EXPERTS = 8
TOKENS = POS + 1
SLOT = 64
CHUNKS = TAPS * C // 128
QUAD = 4
QUADS = TILES * TAPS // QUAD
CORNERS = 4
RING = 4
MOE_CHUNKS = -(-(EXPERTS + 1) * DIM // 128)
ROW = SIDE * 2 * C
SLOPE = 0.01
MARK = 2.0 ** 100
ROUND = 2.0 ** 23

STEM_USE, TURN_USE, OFFSET_USE = 0, 8, 14
FRONT_USES, FRONT_BANKS = 15, 2
EMBED, TOKMAJOR, YT, QUERY, KV0, KV1, OUTER0, OUTER1, NUMER, DENOM, PROJ, ZT, FC1, _a, _b, FC2 = range(16)
MAIN_USES, MAIN_BANKS = 16, 3
GATHERED = (QUADS // RING) * QUAD * 16
TABLE_WRITES = K * 2
PADS = 10
ACT_MAIN, ACT_MOE = 5, 2
DVE_FRONT, DVE_GATHER, DVE_MAIN, DVE_MOE = 12, 2 * QUADS, 10, 11

PE_ORDERS = ["""
    setup.start main.embed main.tokens front.stem:0 front.stem:1 front.stem:2 front.stem:3
    main.yT front.stem:4 main.query main.kv:0 front.stem:5 main.kv:1 front.stem:6 front.stem:7
    main.outer:0 main.outer:1 main.numer gather.sample:0 main.denom main.proj gather.sample:1
    front.turn:0 front.turn:1 front.turn:2 gather.sample:2 front.turn:3 gather.sample:3
    front.turn:4 main.zT front.turn:5 main.fc1:0 main.fc1:1 main.fc1:2 gather.sample:4
    front.offsets gather.sample:5 main.fc2 gather.sample:6 gather.sample:7 setup.end""", """
    front.stem:0 front.stem:1 main.embed front.stem:2 gather.sample:0 front.stem:3 moe.f
    front.stem:4 gather.sample:1 main.tokens front.stem:5 front.stem:6 moe.r moe.h:1 moe.h:6
    main.yT moe.h:0 main.query main.kv:0 main.kv:1 front.stem:7 moe.h:4 main.outer:0
    main.outer:1 moe.y:8 front.turn:0 gather.sample:2 main.numer main.denom front.turn:1
    front.turn:2 moe.h:3 moe.h:5 gather.sample:3 moe.y:1 main.proj front.turn:3 moe.y:5 moe.h:2
    front.turn:4 front.turn:5 moe.y:7 main.zT moe.y:6 main.fc1:0 gather.sample:4 main.fc1:1
    main.fc1:2 front.offsets gather.sample:5 moe.y:4 moe.y:0 main.fc2 gather.sample:6 moe.y:3
    gather.sample:7 moe.y:2"""]
ACT_ORDERS = ["""
    setup.start main.embed front.stem:0 front.stem:1 main.rstd:0 front.stem:2 front.stem:3
    main.yT main.query front.stem:4 main.kv:0 main.kv:1 front.stem:5 front.stem:6
    gather.sample:0 front.stem:7 gather.sample:1 front.turn:0 front.turn:1 front.turn:2
    gather.sample:2 main.rstd:1 front.turn:3 main.zT front.turn:4 main.fc1:0 front.turn:5
    main.fc1:1 gather.sample:3 main.fc1:2 gather.sample:4 gather.sample:5 gather.sample:6
    gather.sample:7 main.rstd:2 setup.end""", """
    front.stem:0 front.stem:1 main.embed front.stem:2 gather.sample:0 front.stem:3 moe.f
    front.stem:4 moe.r main.rstd:0 moe.h:1 main.yT gather.sample:1 moe.h:6 main.query
    front.stem:5 main.kv:0 main.kv:1 front.stem:6 moe.h:0 front.stem:7 gather.sample:2
    front.turn:0 moe.h:4 moe.h:3 front.turn:1 front.turn:2 moe.h:5 front.turn:3 main.rstd:1
    moe.h:2 main.zT gather.sample:3 main.fc1:0 gather.sample:4 front.turn:4 main.fc1:1
    front.turn:5 main.fc1:2 gather.sample:5 gather.sample:6 gather.sample:7 main.rstd:2"""]
DVE_ORDERS = ["""
    setup.start main.embed main.tokens front.leaky:0 main.tokens_end gather.interpolate:0
    gather.interpolate:1 main.query front.leaky:1 main.key:0 main.key:1 front.leaky:2
    main.outer:0 main.outer:1 gather.interpolate:2 main.attend gather.interpolate:3 main.proj
    front.leaky:3 main.proj_end gather.interpolate:4 gather.interpolate:5 gather.interpolate:6
    gather.interpolate:7 front.sampling main.mlp main.mlp_end""", """
    front.leaky:0 gather.interpolate:0 gather.interpolate:1 main.embed main.tokens front.leaky:1
    main.tokens_end moe.r gather.interpolate:2 main.query main.key:0 main.key:1 front.leaky:2
    main.outer:0 main.outer:1 gather.interpolate:3 moe.y:8 main.attend front.leaky:3 moe.y:1
    main.proj moe.y:5 main.proj_end gather.interpolate:4 gather.interpolate:5 moe.y:7 moe.y:6
    gather.interpolate:6 gather.interpolate:7 front.sampling moe.y:4 moe.y:0 main.mlp moe.y:3
    main.mlp_end moe.y:2"""]
MOE_SEQ = [entry[4:] for entry in PE_ORDERS[1].split() if entry.startswith("moe.")]
MOE_USES, MOE_BANKS = len(MOE_SEQ), 2
H_ORDER = [int(entry[2:]) for entry in MOE_SEQ if entry.startswith("h")]
STAGE_LAG = {"load": 3, "front": 2, "gather": 1, "main": 0, "moe": -1}


def build(nc, a, out):
    ctx = ExitStack()
    with ctx:
        def sb(name, shape, dt=F32):
            return ctx.enter_context(nc.sbuf_tensor(name, shape, dt))

        def sem(name):
            return ctx.enter_context(nc.semaphore(name))

        table = nc.dram_tensor("corner_table", (GROUP_IMGS * SIDE * SIDE + SIDE, 2 * C), F32,
                               kind="Internal").ap()

        stem_w = sb("stem_w", [STEM_K, C])
        bn1 = sb("bn1", [STEM_K, 4, C])
        off_w = sb("off_w", [128, CHUNKS, 2 * TAPS])
        off_b = sb("off_b", [TPOS, TILES * TAPS, 2])
        base = sb("base", [TPOS, TILES * TAPS, 2])
        img_base = sb("img_base", [TPOS, TILES * TAPS])
        dcn_w = sb("dcn_w", [128, CHUNKS, DIM])
        bn2 = sb("bn2", [HALF, 5, 2])
        bn2_scale = sb("bn2_scale", [HALF, 2])
        bn2_bias = sb("bn2_bias", [HALF, 2])
        qkv_w = sb("qkv_w", [HALF + 1, 2, 3 * DIM])
        proj_w = sb("proj_w", [HALF + 1, 2, DIM])
        fc1_w = sb("fc1_w", [HALF, 2, HIDDEN])
        fc1_b = sb("fc1_b", [128, HIDDEN // 128])
        fc2_w = sb("fc2_w", [128, HIDDEN // 128, DIM])
        fc2_b = sb("fc2_b", [128, DIM])
        ln_cols = sb("ln_cols", [HALF, 4, 2])
        rows = sb("rows", [1, 3 * DIM])
        moe_w1 = sb("moe_w1", [HALF, 2, (EXPERTS + 1) * DIM])
        moe_w2 = sb("moe_w2", [128, MOE_CHUNKS, DIM])
        router_w = sb("router_w", [HALF, 2, EXPERTS])
        balance = sb("balance", [128, EXPERTS])
        cls_cols = sb("cls_cols", [HALF, 2])
        ident = sb("ident", [128, 128])
        head_mask = sb("head_mask", [HALF, HALF])
        zeros = sb("zeros", [SIDE, C])
        consts = sb("consts", [128, 4])
        NEG1, EPS8, EPS5 = (consts[:, j:j + 1] for j in range(3))

        xcol = sb("xcol", [STEM_K, TILES * TAPS * TPOS])
        H = sb("H", [TPOS, TILES, TAPS * C])
        HT = sb("HT", [128, TILES, CHUNKS, TPOS])
        p_yx = sb("p_yx", [TPOS, TILES * TAPS * 2])
        p_int = sb("p_int", [TPOS, TILES * TAPS * 2])
        dist = sb("dist", [TPOS, TILES * TAPS * 2])
        hat = sb("hat", [TPOS, TILES * TAPS, 2, 2])
        idx_f = sb("idx_f", [TPOS, TILES * TAPS])
        idx = sb("idx", [TPOS, TILES * TAPS], U32)
        corner_w = sb("corner_w", [TPOS, TILES * TAPS * CORNERS])
        G = sb("G", [TPOS, RING, QUAD * CORNERS * C])
        S = sb("S", [TPOS, RING, QUAD * C])
        ST = sb("ST", [128, CHUNKS, TILES, TPOS])

        embed = sb("embed", [HALF, 2, GROUP_IMGS, POS])
        xT = sb("xT", [HALF, 2, GROUP_IMGS * SLOT])
        X0 = sb("X0", [128, TILES, DIM])
        stats = sb("stats", [128, TILES, 6])
        mv = sb("mv", [128, TILES, 2])
        var = sb("var", [128, TILES, 2])
        rstd = sb("rstd", [128, TILES, 2])
        U = sb("U", [128, TILES, DIM])
        Y = sb("Y", [128, TILES, DIM])
        yT = sb("yT", [HALF + 1, 2, GROUP_IMGS * SLOT])
        exp_q = sb("exp_q", [HALF, 2, GROUP_IMGS * TOKENS])
        qT = sb("qT", [HALF, 2, GROUP_IMGS * TOKENS])
        exp_k = sb("exp_k", [128, TILES, DIM])
        kS = sb("kS", [128, TILES, DIM])
        vS = sb("vS", [128, TILES, 2, HALF + 1])
        KV = sb("KV", [HALF, GROUP_IMGS * 2, HALF])
        KS = sb("KS", [HALF, GROUP_IMGS * 2, HALF])
        rden = sb("rden", [HALF, 2 * GROUP_IMGS * TOKENS])
        attT = sb("attT", [HALF + 1, 2, GROUP_IMGS * SLOT])
        XR = sb("XR", [128, TILES, DIM])
        zT = sb("zT", [HALF, 2, GROUP_IMGS * SLOT])
        gT = sb("gT", [128, HIDDEN // 128, GROUP_IMGS * SLOT])
        XM = sb("XM", [128, TILES, DIM])

        X1 = sb("X1", [128, TILES, DIM])
        fT = sb("fT", [HALF, 2, GROUP_IMGS * SLOT])
        score = sb("score", [128, TILES * EXPERTS])
        biased = sb("biased", [128, TILES, EXPERTS + 6])
        top8 = sb("top8", [128, TILES, 8])
        chosen = sb("chosen", [128, TILES, 8])
        marked = sb("marked", [128, TILES, EXPERTS + 6])
        comb = sb("comb", [128, TILES, EXPERTS])
        comb_sum = sb("comb_sum", [128, TILES])
        relu = sb("relu", [128, 2, 2, GROUP_IMGS * TOKENS])
        hidT = sb("hidT", [128, MOE_CHUNKS, GROUP_IMGS * SLOT])

        psum = [ctx.enter_context(nc.psum_tensor(f"bank{b}", [128, 512], F32)) for b in range(8)]

        waits_alone = sem("waits_alone")
        loaded_first, loaded_second, loaded_rest = (sem(f"loaded_{n}") for n in ("first", "second", "rest"))
        moved = sem("moved")
        set_dve, set_act = sem("set_dve"), sem("set_act")
        consts_ready, pads_ready, stem_ready = sem("consts_ready"), sem("pads_ready"), sem("stem_ready")
        shifts_ready, folded, qkv_row_ready = sem("shifts_ready"), sem("folded"), sem("qkv_row_ready")
        front_filled = [sem(f"front_filled{b}") for b in range(FRONT_BANKS)]
        front_freed = [sem(f"front_freed{b}") for b in range(FRONT_BANKS)]
        sample_filled, sample_freed = [sem("sample_filled")], [sem("sample_freed")]
        main_filled = [sem(f"main_filled{b}") for b in range(MAIN_BANKS)]
        main_freed = [sem(f"main_freed{b}") for b in range(MAIN_BANKS)]
        moe_filled = [sem(f"moe_filled{b}") for b in range(MOE_BANKS)]
        moe_freed = [sem(f"moe_freed{b}") for b in range(MOE_BANKS)]
        xcol_loaded = sem("xcol_loaded")
        leaky_done = sem("leaky_done")
        indices_ready = sem("indices_ready")
        table_padded = sem("table_padded")
        table_written = [sem(f"table_written{t}") for t in range(TILES)]
        gathered = [sem(f"gathered{r}") for r in range(RING)]
        sampled = sem("sampled")
        embed_copied = sem("embed_copied")
        embedded = sem("embedded")
        var_ready, rstd_ready = sem("var_ready"), sem("rstd_ready")
        normed = sem("normed")
        exp_ready = sem("exp_ready")
        hidden_ready = sem("hidden_ready")
        out_written = sem("out_written")
        chain_front, chain_gather = sem("chain_front"), sem("chain_gather")
        chain_main, chain_moe = sem("chain_main"), sem("chain_moe")
        act_main, act_moe = sem("act_main"), sem("act_moe")

        class Banks:
            def __init__(self, first, count, uses, filled, freed):
                self.first, self.count, self.filled_sem, self.freed_sem = first, count, filled, freed
                self.per = [len(range(b, uses, count)) for b in range(count)]

            def ap(self, n):
                return psum[self.first + n % self.count]

            def before(self, g, n):
                return g * self.per[n % self.count] + n // self.count

            def claim(self, eng, g, n):
                wait(eng, self.freed_sem[n % self.count], self.before(g, n))

            def evicted(self, eng, g, n):
                wait(eng, self.freed_sem[n % self.count], self.before(g, n) + 1)

            def filled(self, eng, g, n):
                wait(eng, self.filled_sem[n % self.count], self.before(g, n) + 1)

            def fill(self, ins, n):
                ins.then_inc(self.filled_sem[n % self.count], 1)

            def free(self, ins, n):
                ins.then_inc(self.freed_sem[n % self.count], 1)

        def wait(eng, s, value):
            if isinstance(value, int) and value <= 0:
                return
            eng.wait_ge(s, value)

        def wait_alone(eng, s, value):
            if isinstance(value, int) and value <= 0:
                return
            eng.wait_ge(s, value)
            eng.sem_inc(waits_alone, 1)

        front = Banks(0, FRONT_BANKS, FRONT_USES, front_filled, front_freed)
        sample = Banks(2, 1, QUADS, sample_filled, sample_freed)
        main = Banks(3, MAIN_BANKS, MAIN_USES, main_filled, main_freed)
        moe = Banks(6, MOE_BANKS, MOE_USES, moe_filled, moe_freed)

        def moe_use(kind, n=None):
            return MOE_SEQ.index(kind if n is None else f"{kind}:{n}")

        class Chain:
            def __init__(self, eng, s, per):
                self.eng, self.s, self.per, self.n = eng, s, per, 0

            def begin(self, g):
                self.g, self.n = g, 0

            def __call__(self, ins, alone=False):
                self.n += 1
                ins.then_inc(self.s, 1)
                (wait_alone if alone else wait)(self.eng, self.s, self.g * self.per + self.n)

            def end(self):
                assert self.n == self.per, (self.n, self.per)

        def tokens(buf, c=None):
            v = buf if c is None else buf[:, c, :]
            return v.rearrange("p (i s) -> p i s", s=SLOT)[:, :, 0:TOKENS]

        def iterations(eng, orders, units, loop_end=GROUPS - 2):
            def iteration(i):
                peeled = isinstance(i, int)
                for entry in orders[0 if peeled and i <= 0 else -1].split():
                    name, _, n = entry.partition(":")
                    stage = name.split(".")[0]
                    if stage == "setup":
                        if peeled and i == -1:
                            units[name]()
                    elif not peeled or 0 <= i + STAGE_LAG[stage] < GROUPS:
                        units[name](i + STAGE_LAG[stage], *([int(n)] if n else []))
            for i in range(-2, 1):
                iteration(i)
            with eng.Fori(1, loop_end) as i:
                iteration(i)
            for i in range(loop_end, GROUPS + 1):
                iteration(i)

        FIRST = [(stem_w[:], "stem_w"), (bn1[:], "bn1")]
        SECOND = [(ident[:], "ident"), (off_w[:], "off_w"), (off_b[:], "off_b"), (base[:], "base"),
                  (img_base[:], "img_base")]
        REST = [(bn2[:], "bn2"), (dcn_w[:], "dcn_w"), (head_mask[:], "head_mask"), (ln_cols[:], "ln_cols"),
                (cls_cols[:], "cls_cols"), (qkv_w[0:HALF], "qkv_w"), (rows[:], "qkv_b"),
                (proj_w[0:HALF], "proj_w"), (proj_w[HALF:HALF + 1, 1, :], "proj_b"),
                (fc1_w[:], "fc1_w"), (fc1_b[:], "fc1_b"), (fc2_w[:], "fc2_w"), (fc2_b[:], "fc2_b"),
                (router_w[:], "router_w"), (balance[:], "balance"), (moe_w1[:], "moe_w1"),
                (moe_w2[:], "moe_w2")]

        block = ctx.enter_context(nc.Block())

        @block.sync
        def _(sp):
            def load_early(g):
                if isinstance(g, int) and g <= 3:
                    load(g)

            def load_x(g):
                if not (isinstance(g, int) and g <= 3):
                    load(g)

            def load(g):
                front.filled(sp, g - 1, STEM_USE + 7)
                front.filled(sp, g - 1, STEM_USE + 6)
                sp.dma_start(xcol[:, :], a["xcol"][:, bass.ds(g * xcol.shape[1], xcol.shape[1])])\
                    .then_inc(xcol_loaded, 16)

            def write_table(g):
                for r in range(RING):
                    wait(sp, gathered[r], g * GATHERED)
                for t in range(TILES):
                    wait(sp, leaky_done, g * 4 + 2 * t + 2)
                    for kh in range(K):
                        src = H[:, t, kh * K * C:(kh + 1) * K * C].rearrange("p (w c) -> p w c", w=K)
                        for upper in range(2):
                            first = SIDE + t * TILE_IMGS * SIDE * SIDE + (kh - upper) * SIDE
                            dst = bass.AP(table.tensor, first * 2 * C + upper * C,
                                          [[K * ROW, TILE_IMGS * OUT_SIDE], [K * 2 * C, OUT_SIDE],
                                           [2 * C, K], [1, C]])
                            sp.dma_start(dst, src).then_inc(table_written[t], 16)

            def write_out(g):
                moe.evicted(sp, g, MOE_USES - 1)
                view = out.rearrange("(g t s) n c -> s n g t c", t=TILES, s=TILE_IMGS)
                for s in range(TILE_IMGS):
                    sp.dma_start(view[s][:, bass.ds(g, 1)].rearrange("n g t c -> n (g t) c"),
                                 X1[s * SLOT:s * SLOT + TOKENS, :, :]).then_inc(out_written, 16)

            def setup():
                sp.wait_ge(qkv_row_ready, 1)
                sp.dma_start(qkv_w[HALF:HALF + 1, 1, :], rows[:, :]).then_inc(moved, 16)

            for dst, name in FIRST:
                sp.dma_start(dst, a[name]).then_inc(loaded_first, 16)
            sp.dma_start(xcol[:, :], a["xcol"][:, 0:xcol.shape[1]]).then_inc(xcol_loaded, 16)
            for dst, name in SECOND:
                sp.dma_start(dst, a[name]).then_inc(loaded_second, 16)
            sp.wait_ge(pads_ready, 1)
            for r, half in ((0, 0), (GROUP_IMGS * SIDE, 1)):
                sp.dma_start(table[r * SIDE:(r + 1) * SIDE, half * C:(half + 1) * C], zeros[:, :])\
                    .then_inc(table_padded, 16)
            for dst, name in REST:
                sp.dma_start(dst, a[name]).then_inc(loaded_rest, 16)
            iterations(sp, ["setup.start load.early front.table load.x moe.out"],
                       {"load.x": load_x, "load.early": load_early, "front.table": write_table, "moe.out": write_out,
                        "setup.start": setup}, loop_end=GROUPS - 3)
            sp.wait_ge(out_written, GROUPS * TILE_IMGS * 16)
            for t in range(TILES):
                sp.wait_ge(table_written[t], GROUPS * TABLE_WRITES * 16)

        @block.gpsimd
        def _(pool):
            def gather(g):
                wait_alone(pool, indices_ready, g + 1)
                for n in range(QUADS):
                    if n % (QUADS // TILES) == 0:
                        wait_alone(pool, table_written[n * TILES // QUADS], (g + 1) * TABLE_WRITES * 16)
                    wait_alone(pool, sampled, g * QUADS + n - RING + 1)
                    for k in range(QUAD):
                        tap = n * QUAD + k
                        nc.gpsimd.indirect_dma_start(
                            out=G[:, n % RING, k * CORNERS * C:(k + 1) * CORNERS * C], out_offset=None,
                            in_=table[:, :],
                            in_offset=bass.IndirectOffsetOnAxis(ap=idx[:, tap:tap + 1], axis=0),
                        ).then_inc(gathered[n % RING], 16)

            for j, (pad, value) in enumerate((
                    (zeros[:], 0.0), (xT[:], 0.0), (attT[0:HALF], 0.0), (attT[HALF:HALF + 1], 1.0), (yT[HALF:HALF + 1], 1.0),
                    (vS[:, :, :, HALF:HALF + 1], 1.0), (biased[:, :, EXPERTS:], -MARK),
                    (chosen[:, :, 2:], -MARK), (gT[:], 0.0), (hidT[:], 0.0))):
                wait(pool, pads_ready, j)
                nc.gpsimd.memset(pad, value).then_inc(pads_ready, 1)
            pool.wait_ge(pads_ready, PADS)
            pool.wait_ge(table_padded, 32)
            iterations(pool, ["gather.taps"], {"gather.taps": gather})

        @block.tensor
        def _(pe):
            mm = nc.tensor.matmul

            def stem(g, n):
                if n == 0:
                    pe.wait_ge(xcol_loaded, (g + 1) * 16)
                front.claim(pe, g, STEM_USE + n)
                bank = front.ap(STEM_USE + n)
                for k in range(QUAD):
                    at = (n * QUAD + k) * TPOS
                    ins = mm(bank[0:TPOS, k * C:(k + 1) * C], xcol[:, at:at + TPOS], stem_w[:, :],
                             start=True, stop=True)
                front.fill(ins, STEM_USE + n)

            def turn_stem(g, n):
                if isinstance(g, int) and g == n == 0:
                    pe.wait_ge(loaded_second, 16 * len(SECOND))
                t, j = divmod(n, 3)
                if j == 0:
                    pe.wait_ge(leaky_done, g * 4 + 2 * t + 2)
                front.claim(pe, g, TURN_USE + n)
                bank = front.ap(TURN_USE + n)
                for k in range(4):
                    at = (4 * j + k) * 128
                    ins = nc.tensor.transpose(bank[:, k * TPOS:(k + 1) * TPOS], H[:, t, at:at + 128],
                                              ident[0:TPOS, 0:TPOS])
                front.fill(ins, TURN_USE + n)

            def offsets(g):
                front.evicted(pe, g, TURN_USE + 4)
                front.evicted(pe, g, TURN_USE + 5)
                front.claim(pe, g, OFFSET_USE)
                bank = front.ap(OFFSET_USE)
                for t in range(TILES):
                    for c in range(CHUNKS):
                        ins = mm(bank[0:TPOS, t * 32:(t + 1) * 32], HT[:, t, c, :], off_w[:, c, :],
                                 start=(c == 0), stop=(c == CHUNKS - 1))
                front.fill(ins, OFFSET_USE)

            def turn_sample(g, n):
                pe.wait_ge(sampled, g * QUADS + n + 1)
                sample.claim(pe, g, n)
                bank = sample.ap(n)
                for k in range(3):
                    ins = nc.tensor.transpose(bank[:, k * TPOS:(k + 1) * TPOS],
                                              S[:, n % RING, k * 128:(k + 1) * 128],
                                              ident[0:TPOS, 0:TPOS])
                sample.fill(ins, n)

            def embed_patches(g):
                sample.evicted(pe, g, QUADS - 2)
                sample.evicted(pe, g, QUADS - 1)
                main.claim(pe, g, EMBED)
                bank = main.ap(EMBED)
                n = TILES * TPOS
                for m in range(2):
                    for c in range(CHUNKS):
                        ins = mm(bank[0:HALF, m * n:(m + 1) * n], dcn_w[:, c, m * HALF:(m + 1) * HALF],
                                 ST[:, c, :, :].rearrange("p t s -> p (t s)"),
                                 start=(c == 0), stop=(c == CHUNKS - 1))
                main.fill(ins, EMBED)

            def to_tokens(g):
                pe.wait_ge(embedded, g + 1)
                main.claim(pe, g, TOKMAJOR)
                bank = main.ap(TOKMAJOR)
                for t in range(TILES):
                    for c in range(2):
                        at = t * DIM + c * HALF
                        ins = nc.tensor.transpose(bank[:, at:at + HALF], xT[:, c, t * 128:(t + 1) * 128],
                                                  ident[0:HALF, 0:HALF])
                main.fill(ins, TOKMAJOR)

            def to_features(g, banks, use, norm):
                pe.wait_ge(normed, g * 3 + norm + 1)
                banks.claim(pe, g, use)
                bank = banks.ap(use)
                for t in range(TILES):
                    for c in range(2):
                        at = c * 256 + t * 128
                        ins = nc.tensor.transpose(bank[0:HALF, at:at + 128],
                                                  Y[:, t, c * HALF:(c + 1) * HALF], ident[:, :])
                banks.fill(ins, use)

            def chunk(c, buf):
                return buf[0:HALF + c, c, :]

            def query(g):
                main.evicted(pe, g, YT)
                main.claim(pe, g, QUERY)
                bank = main.ap(QUERY)
                n = GROUP_IMGS * TOKENS
                for m in range(2):
                    for c in range(2):
                        ins = mm(bank[0:HALF, m * n:(m + 1) * n],
                                 chunk(c, qkv_w)[:, m * HALF:(m + 1) * HALF], tokens(chunk(c, yT)),
                                 start=(c == 0), stop=(c == 1))
                main.fill(ins, QUERY)

            def key_value(g, t):
                main.claim(pe, g, KV0 + t)
                bank = main.ap(KV0 + t)
                for c in range(2):
                    ins = mm(bank[:, 0:2 * DIM], chunk(c, yT)[:, t * 128:(t + 1) * 128],
                             chunk(c, qkv_w)[:, DIM:], start=(c == 0), stop=(c == 1))
                main.fill(ins, KV0 + t)

            def outer(g, s):
                if s == 0:
                    main.evicted(pe, g, KV0)
                    main.evicted(pe, g, KV1)
                main.claim(pe, g, OUTER0 + s)
                bank = main.ap(OUTER0 + s)
                w = HALF + 1
                p = slice(s * SLOT, s * SLOT + TOKENS)
                for t in range(TILES):
                    for c in range(2):
                        at = (t * 2 + c) * w
                        ins = mm(bank[0:HALF, at:at + w], kS[p, t, c * HALF:(c + 1) * HALF], vS[p, t, c, :],
                                 start=True, stop=True)
                main.fill(ins, OUTER0 + s)

            def attend(g, use):
                table_ = {NUMER: KV, DENOM: KS}[use]
                if use == NUMER:
                    main.evicted(pe, g, QUERY)
                    main.evicted(pe, g, OUTER0)
                    main.evicted(pe, g, OUTER1)
                main.claim(pe, g, use)
                bank = main.ap(use)
                for c in range(2):
                    for i in range(GROUP_IMGS):
                        at = (c * GROUP_IMGS + i) * TOKENS
                        t, s = divmod(i, TILE_IMGS)
                        ins = mm(bank[0:HALF, at:at + TOKENS], table_[:, (s * TILES + t) * 2 + c, :],
                                 qT[:, c, i * TOKENS:(i + 1) * TOKENS], start=True, stop=True)
                main.fill(ins, use)

            def project(g):
                main.evicted(pe, g, NUMER)
                main.claim(pe, g, PROJ)
                bank = main.ap(PROJ)
                for t in range(TILES):
                    for c in range(2):
                        ins = mm(bank[:, t * DIM:(t + 1) * DIM], chunk(c, attT)[:, t * 128:(t + 1) * 128],
                                 chunk(c, proj_w), start=(c == 0), stop=(c == 1))
                main.fill(ins, PROJ)

            def fc1(g, n):
                main.evicted(pe, g, ZT)
                main.claim(pe, g, FC1 + n)
                bank = main.ap(FC1 + n)
                w = GROUP_IMGS * TOKENS
                for k in range(2):
                    m = (2 * n + k) * 128
                    for c in range(2):
                        ins = mm(bank[:, k * w:(k + 1) * w], fc1_w[:, c, m:m + 128], tokens(zT, c),
                                 start=(c == 0), stop=(c == 1))
                main.fill(ins, FC1 + n)

            def fc2(g):
                for n in range(3):
                    main.evicted(pe, g, FC1 + n)
                main.claim(pe, g, FC2)
                bank = main.ap(FC2)
                for t in range(TILES):
                    dst = bank[:, t * DIM:(t + 1) * DIM]
                    for m in range(HIDDEN // 128):
                        ins = mm(dst, gT[:, m, t * 128:(t + 1) * 128], fc2_w[:, m, :],
                                 start=(m == 0), stop=(m == HIDDEN // 128 - 1))
                main.fill(ins, FC2)

            def router(g):
                n = moe_use("r")
                moe.evicted(pe, g, 0)
                moe.claim(pe, g, n)
                bank = moe.ap(n)
                for t in range(TILES):
                    for c in range(2):
                        ins = mm(bank[:, t * EXPERTS:(t + 1) * EXPERTS], fT[:, c, t * 128:(t + 1) * 128],
                                 router_w[:, c, :], start=(c == 0), stop=(c == 1))
                moe.fill(ins, n)

            def hidden(g, pair):
                n = moe_use("h", pair)
                moe.claim(pe, g, n)
                bank = moe.ap(n)
                w = GROUP_IMGS * TOKENS
                for k in range(2):
                    at = (2 * pair + k) * 128
                    rows_ = min(128, (EXPERTS + 1) * DIM - at)
                    for c in range(2):
                        ins = mm(bank[0:rows_, k * w:(k + 1) * w], moe_w1[:, c, at:at + rows_],
                                 tokens(fT, c), start=(c == 0), stop=(c == 1))
                moe.fill(ins, n)

            def expert_out(g, e):
                n = moe_use("y", e)
                parts = [(e * DIM // 128, slice(0, 128)), (e * DIM // 128 + 1, slice(0, 64))] if e % 2 == 0 \
                    else [(e * DIM // 128, slice(64, 128)), (e * DIM // 128 + 1, slice(0, 128))]
                pair = max(H_ORDER.index(c // 2) for c, _ in parts)
                pe.wait_ge(hidden_ready, g * len(H_ORDER) + pair + 1)
                moe.claim(pe, g, n)
                bank = moe.ap(n)
                for t in range(TILES):
                    for j, (c, p) in enumerate(parts):
                        ins = mm(bank[:, t * DIM:(t + 1) * DIM], hidT[p, c, t * 128:(t + 1) * 128],
                                 moe_w2[p, c, :], start=(j == 0), stop=(j == 1))
                moe.fill(ins, n)

            def setup():
                pe.wait_ge(loaded_rest, 16 * len(REST))
                pe.wait_ge(pads_ready, PADS)
                for h in range(2):
                    for c in range(2):
                        ins = mm(main.ap(h)[0:1, 0:288], ln_cols[:, 1, c:c + 1],
                                 qkv_w[0:HALF, c, h * 288:(h + 1) * 288], start=(c == 0), stop=(c == 1))
                for m in range(HIDDEN // 128):
                    for c in range(2):
                        ins = mm(main.ap(2)[:, m:m + 1], fc1_w[:, c, m * 128:(m + 1) * 128],
                                 ln_cols[:, 3, c:c + 1], start=(c == 0), stop=(c == 1))
                ins.then_inc(shifts_ready, 1)

            def setup_end():
                pe.wait_ge(folded, 1)
                pe.wait_ge(moved, 16)

            pe.wait_ge(loaded_first, 16 * len(FIRST))
            pe.wait_ge(stem_ready, 1)
            iterations(pe, PE_ORDERS, {
                "setup.start": setup, "setup.end": setup_end,
                "front.stem": stem, "front.turn": turn_stem, "front.offsets": offsets,
                "gather.sample": turn_sample, "main.embed": embed_patches, "main.tokens": to_tokens,
                "main.yT": lambda g: to_features(g, main, YT, 0),
                "main.zT": lambda g: to_features(g, main, ZT, 1), "main.query": query,
                "main.kv": key_value, "main.outer": outer, "main.numer": lambda g: attend(g, NUMER),
                "main.denom": lambda g: attend(g, DENOM), "main.proj": project, "main.fc1": fc1,
                "main.fc2": fc2, "moe.f": lambda g: to_features(g, moe, moe_use("f"), 2),
                "moe.r": router, "moe.h": hidden, "moe.y": expert_out})

        @block.scalar
        def _(act):
            A = nc.scalar.activation
            link_main, link_moe = Chain(act, act_main, ACT_MAIN), Chain(act, act_moe, ACT_MOE)
            w = GROUP_IMGS * TOKENS

            def stem(g, n):
                t, q = divmod(n, 4)
                if q == 0:
                    wait(act, table_written[t], g * TABLE_WRITES * 16)
                front.filled(act, g, STEM_USE + n)
                front.free(A(H[:, t, q * QUAD * C:(q + 1) * QUAD * C],
                             front.ap(STEM_USE + n)[0:TPOS, 0:QUAD * C], ACT.Copy), STEM_USE + n)

            def turn_stem(g, n):
                front.filled(act, g, TURN_USE + n)
                t, j = divmod(n, 3)
                front.free(A(HT[:, t, 4 * j:4 * j + 4, :].rearrange("p c s -> p (c s)"),
                             front.ap(TURN_USE + n)[:, 0:4 * TPOS], ACT.Copy), TURN_USE + n)

            def turn_sample(g, n):
                if n == 0 and not (isinstance(g, int) and g == 0):
                    main.filled(act, g - 1, EMBED)
                sample.filled(act, g, n)
                t, q = divmod(n, 4)
                sample.free(A(ST[:, 3 * q:3 * q + 3, t, :],
                             sample.ap(n)[:, 0:3 * TPOS].rearrange("p (c s) -> p c s", c=3),
                             ACT.Copy), n)

            def embed_copy(g):
                main.filled(act, g, EMBED)
                wait(act, embedded, g)
                link_main.begin(g)
                n = TILES * TPOS
                for m in range(2):
                    ins = A(embed[:, m, :, :].rearrange("p i s -> p (i s)"),
                            main.ap(EMBED)[0:HALF, m * n:(m + 1) * n], ACT.Identity,
                            bias=bn2_bias[:, m:m + 1], scale=bn2_scale[:, m:m + 1])
                    if m == 0:
                        ins.then_inc(embed_copied, 1)
                main.free(ins, EMBED)

            def inverse_root(g, norm):
                act.wait_ge(var_ready, g * 3 + norm + 1)
                n = 4 if norm == 0 else 2
                v = var[:].rearrange("p a b -> p (a b)")[:, 0:n]
                link_main(A(v, v, ACT.Ln))
                A(rstd[:].rearrange("p a b -> p (a b)")[:, 0:n], v, ACT.Exp, scale=-0.5)\
                    .then_inc(rstd_ready, 1)

            def evict_features(g, banks, use, dst):
                banks.filled(act, g, use)
                if dst is fT:
                    moe.filled(act, g - 1, MOE_USES - 1)
                banks.free(A(dst[0:HALF].rearrange("p c s -> p (c s)"), banks.ap(use)[0:HALF, :], ACT.Copy),
                           use)

            def exp_query(g):
                main.filled(act, g, QUERY)
                A(exp_q[:].rearrange("p c s -> p (c s)"), main.ap(QUERY)[0:HALF, 0:2 * w], ACT.Exp,
                  bias=NEG1[0:HALF]).then_inc(exp_ready, 1)

            def key_value(g, t):
                main.filled(act, g, KV0 + t)
                bank = main.ap(KV0 + t)
                link_main(A(vS[:, t, :, 0:HALF], bank[:, DIM:2 * DIM].rearrange("p (c f) -> p c f", c=2),
                            ACT.Copy))
                A(exp_k[:, t, :], bank[:, 0:DIM], ACT.Exp, bias=NEG1).then_inc(exp_ready, 1)

            def gelu(g, n):
                main.filled(act, g, FC1 + n)
                for k in range(2):
                    m = 2 * n + k
                    ins = A(tokens(gT, m),
                            main.ap(FC1 + n)[:, k * w:(k + 1) * w].rearrange("p (i s) -> p i s", s=TOKENS),
                            ACT.Gelu, bias=fc1_b[:, m:m + 1])
                main.free(ins, FC1 + n)
                if n == 2:
                    nc.scalar.preload_act_table_set("natural_log_exp_and_others")

            def router_exp(g):
                n = moe_use("r")
                moe.filled(act, g, n)
                link_moe.begin(g)
                moe.free(A(score[:, :], moe.ap(n)[:, 0:TILES * EXPERTS], ACT.Exp, scale=-1.0), n)

            def relu_squared(g, pair):
                n = moe_use("h", pair)
                moe.filled(act, g, n)
                if pair == H_ORDER[0] and not (isinstance(g, int) and g == 0):
                    moe.filled(act, g - 1, MOE_USES - 1)
                tmp = relu[:, H_ORDER.index(pair) % 2]
                chunks = [2] if pair < 6 else [1, 1]
                at, last = 0, None
                for k, width in enumerate(chunks):
                    r = 64 if k else 128
                    src = moe.ap(n)[0:r, k * w:(k + width) * w]
                    ins = A(tmp[0:r, k:k + width, :].rearrange("p c s -> p (c s)"), src, ACT.Relu)
                    if k < len(chunks) - 1:
                        link_moe(ins)
                moe.free(ins, n)
                moe.evicted(act, g, n)
                for k, width in enumerate(chunks):
                    r = 64 if k else 128
                    c = 2 * pair + k
                    dst = hidT[0:r, c:c + width, :].rearrange("p c (i s) -> p c i s", s=SLOT)[:, :, :, 0:TOKENS]
                    ins = A(dst, tmp[0:r, k:k + width, :].rearrange("p c (i s) -> p c i s", s=TOKENS),
                            ACT.Square)
                    if k < len(chunks) - 1:
                        link_moe(ins)
                ins.then_inc(hidden_ready, 1)

            nc.scalar.preload_act_table_set("natural_log_exp_and_others")
            act.wait_ge(consts_ready, 3)
            act.wait_ge(loaded_first, 16 * len(FIRST))
            A(bn1[:, 3, :], bn1[:, 3, :], ACT.Ln, bias=EPS5[0:STEM_K]).then_inc(set_act, 1)
            act.wait_ge(set_act, 1)
            A(bn1[:, 3, :], bn1[:, 3, :], ACT.Exp, scale=-0.5).then_inc(set_act, 1)

            def setup():
                act.wait_ge(loaded_rest, 16 * len(REST))
                act.wait_ge(pads_ready, PADS)
                A(bn2[:, 4, :], bn2[:, 4, :], ACT.Ln, bias=EPS5[0:HALF]).then_inc(set_act, 1)
                act.wait_ge(set_act, 3)
                A(bn2[:, 4, :], bn2[:, 4, :], ACT.Exp, scale=-0.5).then_inc(set_act, 1)

            def setup_end():
                act.wait_ge(folded, 1)

            iterations(act, ACT_ORDERS, {
                "setup.start": setup, "setup.end": setup_end,
                "front.stem": stem, "front.turn": turn_stem, "gather.sample": turn_sample,
                "main.embed": embed_copy, "main.rstd": inverse_root,
                "main.yT": lambda g: evict_features(g, main, YT, yT),
                "main.zT": lambda g: evict_features(g, main, ZT, zT), "main.query": exp_query,
                "main.kv": key_value, "main.fc1": gelu,
                "moe.f": lambda g: evict_features(g, moe, moe_use("f"), fT),
                "moe.r": router_exp, "moe.h": relu_squared})

        @block.vector
        def _(dve):
            v = nc.vector
            link_front = Chain(dve, chain_front, DVE_FRONT)
            link_gather = Chain(dve, chain_gather, DVE_GATHER)
            link_main = Chain(dve, chain_main, DVE_MAIN)
            link_moe = Chain(dve, chain_moe, DVE_MOE)
            half_taps = TAPS * C // 2

            def leaky(g, n):
                front.evicted(dve, g, STEM_USE + 2 * n)
                front.evicted(dve, g, STEM_USE + 2 * n + 1)
                h = H[:, n // 2, (n % 2) * half_taps:(n % 2 + 1) * half_taps]
                v.scalar_tensor_tensor(out=h, in0=h, scalar=SLOPE, in1=h, op0=ALU.mult, op1=ALU.max)\
                    .then_inc(leaky_done, 1)

            def sampling(g):
                link_front.begin(g)
                if isinstance(g, int) and g == 0:
                    dve.wait_ge(loaded_second, 16 * len(SECOND))
                front.filled(dve, g, OFFSET_USE)
                n = TILES * TAPS * 2
                ins = v.tensor_tensor(p_yx[:], front.ap(OFFSET_USE)[0:TPOS, 0:n],
                                      off_b[:].rearrange("p t y -> p (t y)"), ALU.add)
                front.free(ins, OFFSET_USE)
                front.evicted(dve, g, OFFSET_USE)
                link_front(v.tensor_tensor(p_yx[:], p_yx[:], base[:].rearrange("p t y -> p (t y)"), ALU.add))
                link_front(v.tensor_scalar(p_int[:], p_yx[:], 0.5, SIDE - 1.5, ALU.max, ALU.min))
                link_front(v.tensor_scalar(p_int[:], p_int[:], -0.5, ROUND, ALU.add, ALU.add))
                link_front(v.tensor_scalar(p_int[:], p_int[:], -ROUND, None, ALU.add))
                corner = p_int[:].rearrange("p (t y) -> p t y", y=2)
                link_front(v.scalar_tensor_tensor(out=idx_f[:], in0=corner[:, :, 0], scalar=float(SIDE),
                                                  in1=corner[:, :, 1], op0=ALU.mult, op1=ALU.add))
                for r in range(RING):
                    wait(dve, gathered[r], g * GATHERED)
                v.tensor_tensor(idx[:], idx_f[:], img_base[:], ALU.add).then_inc(indices_ready, 1)
                hats = hat[:].rearrange("p t y k -> p (t y) k")
                link_front(v.tensor_tensor(dist[:], p_yx[:], p_int[:], ALU.subtract))
                for k in range(2):
                    link_front(v.scalar_tensor_tensor(out=hats[:, :, k], in0=dist[:], scalar=-1.0, in1=dist[:],
                                                      op0=ALU.mult, op1=ALU.min))
                    if k == 0:
                        link_front(v.tensor_scalar(dist[:], dist[:], -1.0, None, ALU.add))
                flat = hat[:].rearrange("p t y k -> p (t y k)")
                link_front(v.tensor_scalar(flat, flat, 1.0, 0.0, ALU.add, ALU.max))
                wait(dve, sampled, g * QUADS)
                cw = corner_w[:].rearrange("p (t x y) -> p t x y", x=2, y=2)
                m = TILES * TAPS
                for x in range(2):
                    link_front(v.tensor_tensor(cw[:, :, x, :], hat[:, :, 1, x:x + 1].to_broadcast([TPOS, m, 2]),
                                               hat[:, :, 0, :], ALU.mult))

            def interpolate(g, n):
                if n == 0:
                    link_gather.begin(g)
                dve.wait_ge(gathered[n % RING], g * GATHERED + (n // RING + 1) * QUAD * 16)
                if n >= RING:
                    sample.filled(dve, g, n - RING)
                elif not (isinstance(g, int) and g == 0):
                    sample.filled(dve, g - 1, n + QUADS - RING)
                m = QUAD * CORNERS
                quad = G[:, n % RING, :]
                q = quad.rearrange("p (m c) -> p m c", c=C)
                link_gather(v.tensor_tensor(
                    q, q, corner_w[:, n * m:(n + 1) * m].unsqueeze(2).to_broadcast([TPOS, m, C]), ALU.mult))
                half = quad.rearrange("p (k x r) -> p k x r", x=2, r=2 * C)
                link_gather(v.tensor_tensor(half[:, :, 0, :], half[:, :, 0, :], half[:, :, 1, :], ALU.add))
                four = quad.rearrange("p (k y c) -> p k y c", y=CORNERS, c=C)
                v.tensor_tensor(S[:, n % RING, :].rearrange("p (k c) -> p k c", c=C), four[:, :, 0, :],
                                four[:, :, 1, :], ALU.add).then_inc(sampled, 1)

            def embed_leaky(g):
                link_main.begin(g)
                dve.wait_ge(embed_copied, g + 1)
                main.evicted(dve, g, EMBED)
                dst = xT[:].rearrange("p c (i s) -> p (c i) s", s=SLOT)[:, :, 1:TOKENS]
                src = embed[:].rearrange("p c i s -> p (c i) s")
                v.scalar_tensor_tensor(out=dst, in0=src, scalar=SLOPE, in1=src, op0=ALU.mult, op1=ALU.max)\
                    .then_inc(embedded, 1)

            def moments(src):
                for t in range(TILES):
                    ins = v.bn_stats(stats[:, t, :], src[:, t, :])
                link_main(ins, alone=True)
                for t in range(TILES):
                    ins = v.bn_aggr(mv[:, t, :], stats[:, t, :])
                link_main(ins)

            def normalise(dst, src, scale):
                for t in range(TILES):
                    ins = v.tensor_scalar(dst[:, t, :], src[:, t, :], mv[:, t, 0:1], scale(t),
                                          ALU.subtract, ALU.mult)
                return ins

            def norm_tokens(g):
                main.filled(dve, g, TOKMAJOR)
                ins = v.tensor_copy(X0[:].rearrange("p t c -> p (t c)"), main.ap(TOKMAJOR)[:, 0:TILES * DIM])
                main.free(ins, TOKMAJOR)
                main.evicted(dve, g, TOKMAJOR)
                moments(X0)
                link_main(v.tensor_scalar(var[:, :, 0], mv[:, :, 1], 1e-5, None, ALU.add))
                v_ = v.scalar_tensor_tensor(out=var[:, :, 1], in0=var[:, :, 0], scalar=1e-8,
                                            in1=mv[:, :, 1], op0=ALU.mult, op1=ALU.add)
                v_.then_inc(var_ready, 1)

            def norm_tokens_end(g):
                dve.wait_ge(rstd_ready, g * 3 + 1)
                if not (isinstance(g, int) and g == 0):
                    moe.filled(dve, g - 1, moe_use("f"))
                normalise(Y, X0, lambda t: rstd[:, t, 1:2]).then_inc(normed, 1)
                link_main(normalise(U, X0, lambda t: rstd[:, t, 0:1]))

            def variance(src, eps):
                moments(src)
                v.tensor_scalar(var[:].rearrange("p a b -> p (a b)")[:, 0:2], mv[:, :, 1], eps, None,
                                ALU.add).then_inc(var_ready, 1)

            def norm_again(g, src, norm):
                dve.wait_ge(rstd_ready, g * 3 + norm + 1)
                r = rstd[:].rearrange("p a b -> p (a b)")
                normalise(Y, src, lambda t: r[:, t:t + 1]).then_inc(normed, 1)

            def elu(g, use, n, dst, e, src):
                dve.wait_ge(exp_ready, g * 3 + n + 1)
                main.free(v.scalar_tensor_tensor(out=dst, in0=e, scalar=1.0, in1=src, op0=ALU.min,
                                                 op1=ALU.max), use)

            def query(g):
                elu(g, QUERY, 0, qT[:].rearrange("p c s -> p (c s)"), exp_q[:].rearrange("p c s -> p (c s)"),
                    main.ap(QUERY)[0:HALF, 0:2 * GROUP_IMGS * TOKENS])

            def key(g, t):
                elu(g, KV0 + t, 1 + t, kS[:, t, :], exp_k[:, t, :], main.ap(KV0 + t)[:, 0:DIM])

            def outer(g, s):
                main.filled(dve, g, OUTER0 + s)
                m = TILES * 2
                kv = main.ap(OUTER0 + s)[0:HALF, 0:m * (HALF + 1)].rearrange("p (m f) -> p m f", m=m)
                mask = head_mask[:].unsqueeze(1).to_broadcast([HALF, m, HALF])
                v.tensor_tensor(KV[:, s * m:(s + 1) * m, :], kv[:, :, 0:HALF], mask, ALU.mult)
                ins = v.tensor_tensor(KS[:, s * m:(s + 1) * m, :],
                                      kv[:, :, HALF:HALF + 1].to_broadcast([HALF, m, HALF]), mask, ALU.mult)
                main.free(ins, OUTER0 + s)

            def attend(g):
                main.filled(dve, g, DENOM)
                n = 2 * GROUP_IMGS * TOKENS
                main.free(v.reciprocal(rden[:, :], main.ap(DENOM)[0:HALF, 0:n]), DENOM)
                main.evicted(dve, g, DENOM)
                dst = attT[0:HALF].rearrange("p c (i s) -> p (c i) s", s=SLOT)[:, :, 0:TOKENS]
                m = 2 * GROUP_IMGS
                ins = v.tensor_tensor(dst, main.ap(NUMER)[0:HALF, 0:n].rearrange("p (m s) -> p m s", m=m),
                                      rden[:].rearrange("p (m s) -> p m s", m=m), ALU.mult)
                main.free(ins, NUMER)

            def project(g):
                main.filled(dve, g, PROJ)
                flat = [b[:].rearrange("p t c -> p (t c)") for b in (XR, U, X0)]
                ins = v.tensor_tensor(flat[0], flat[1], main.ap(PROJ)[:, 0:TILES * DIM], ALU.add)
                main.free(ins, PROJ)
                main.evicted(dve, g, PROJ)
                variance(XR, 1e-8)

            def project_end(g):
                norm_again(g, XR, 1)
                flat = [b[:].rearrange("p t c -> p (t c)") for b in (XR, U, X0)]
                link_main(v.tensor_tensor(flat[2], flat[2], flat[0], ALU.add))
                link_main(v.tensor_tensor(X0[:], X0[:], fc2_b[:].unsqueeze(1).to_broadcast([128, TILES, DIM]),
                                          ALU.add))

            def mlp_out(g):
                main.filled(dve, g, FC2)
                flat = [b[:].rearrange("p t c -> p (t c)") for b in (XM, X0)]
                ins = v.tensor_tensor(flat[0], flat[1], main.ap(FC2)[:, 0:TILES * DIM], ALU.add)
                main.free(ins, FC2)
                main.evicted(dve, g, FC2)
                variance(XM, 1e-5)

            def mlp_end(g):
                norm_again(g, XM, 2)
                link_main.end()

            def choose(g):
                moe.evicted(dve, g, moe_use("r"))
                link_moe.begin(g)
                link_moe(v.tensor_scalar(score[:], score[:], 1.0, None, ALU.add))
                link_moe(v.reciprocal(score[:], score[:]))
                s3 = score[:].rearrange("p (t e) -> p t e", t=TILES)
                link_moe(v.tensor_tensor(biased[:, :, 0:EXPERTS], s3,
                                         balance[:].unsqueeze(1).to_broadcast([128, TILES, EXPERTS]), ALU.add),
                         alone=True)
                for t in range(TILES):
                    ins = v.max(out=top8[:, t, :], in_=biased[:, t, 0:EXPERTS])
                link_moe(ins)
                link_moe(v.tensor_copy(chosen[:, :, 0:2], top8[:, :, 0:2]), alone=True)
                for t in range(TILES):
                    ins = v.match_replace(out=marked[:, t, :], in_to_replace=chosen[:, t, :],
                                          in_values=biased[:, t, :], imm_value=MARK)
                link_moe(ins)
                for t in range(TILES):
                    ins = v.scalar_tensor_tensor(out=comb[:, t, :], in0=marked[:, t, 0:EXPERTS], scalar=MARK,
                                                 in1=s3[:, t, :], op0=ALU.is_equal, op1=ALU.mult,
                                                 accum_out=comb_sum[:, t:t + 1])
                    link_moe(ins)
                link_moe(v.tensor_scalar(comb_sum[:], comb_sum[:], 1e-20, None, ALU.add))
                link_moe(v.reciprocal(comb_sum[:], comb_sum[:]))
                link_moe(v.tensor_tensor(comb[:], comb[:],
                                         comb_sum[:].unsqueeze(2).to_broadcast([128, TILES, EXPERTS]),
                                         ALU.mult))

            def expert_sum(g, e):
                n = moe_use("y", e)
                moe.filled(dve, g, n)
                if e == EXPERTS:
                    wait(dve, out_written, g * TILE_IMGS * 16)
                    flat = [b[:].rearrange("p t c -> p (t c)") for b in (X1, XM)]
                    ins = v.tensor_tensor(flat[0], flat[1], moe.ap(n)[:, 0:TILES * DIM], ALU.add)
                else:
                    for t in range(TILES):
                        ins = v.scalar_tensor_tensor(
                            out=X1[:, t, :], in0=moe.ap(n)[:, t * DIM:(t + 1) * DIM], scalar=comb[:, t, e:e + 1],
                            in1=X1[:, t, :], op0=ALU.mult, op1=ALU.add)
                moe.free(ins, n)
                moe.evicted(dve, g, n)
                if n == MOE_USES - 1:
                    link_moe.end()

            for j, value in enumerate((-1.0, 1e-8, 1e-5)):
                v.memset(consts[:, j:j + 1], value).then_inc(consts_ready, 1)
            step = Chain(dve, set_dve, 0)
            step.begin(0)
            dve.wait_ge(loaded_first, 16 * len(FIRST))
            dve.wait_ge(set_act, 2)
            step(v.tensor_tensor(bn1[:, 0, :], bn1[:, 0, :], bn1[:, 3, :], ALU.mult))
            step(v.tensor_tensor(stem_w[0:1, :], stem_w[0:1, :], bn1[0:1, 2, :], ALU.subtract))
            step(v.tensor_tensor(stem_w[:, :], stem_w[:, :], bn1[:, 0, :], ALU.mult))
            v.tensor_tensor(stem_w[0:1, :], stem_w[0:1, :], bn1[0:1, 1, :], ALU.add).then_inc(stem_ready, 1)

            def setup():
                dve.wait_ge(pads_ready, PADS)
                dve.wait_ge(set_act, 4)
                step(v.tensor_tensor(bn2_scale[:], bn2[:, 1, :], bn2[:, 4, :], ALU.mult))
                step(v.tensor_tensor(bn2_bias[:], bn2[:, 0, :], bn2[:, 3, :], ALU.subtract))
                step(v.tensor_tensor(bn2_bias[:], bn2_bias[:], bn2_scale[:], ALU.mult))
                step(v.tensor_tensor(bn2_bias[:], bn2_bias[:], bn2[:, 2, :], ALU.add))
                for c in range(2):
                    for i in range(GROUP_IMGS):
                        ins = v.tensor_copy(xT[:, c, i * SLOT:i * SLOT + 1], cls_cols[:, c:c + 1])
                step(ins)
                dve.wait_ge(shifts_ready, 1)
                for h in range(2):
                    part = rows[:, h * 288:(h + 1) * 288]
                    ins = v.tensor_tensor(part, part, main.ap(h)[0:1, 0:288], ALU.add)
                step(ins)
                v.tensor_scalar(rows[:, 0:2 * DIM], rows[:, 0:2 * DIM], 1.0, None, ALU.add)\
                    .then_inc(qkv_row_ready, 1)
                step(v.tensor_tensor(fc1_b[:], fc1_b[:], main.ap(2)[:, 0:HIDDEN // 128], ALU.add))
                for c in range(2):
                    step(v.tensor_scalar(qkv_w[0:HALF, c, :], qkv_w[0:HALF, c, :], ln_cols[:, 0, c:c + 1], None,
                                         ALU.mult))
                    ins = v.tensor_scalar(fc1_w[:, c, :], fc1_w[:, c, :], ln_cols[:, 2, c:c + 1], None, ALU.mult)
                    step(ins) if c == 0 else ins.then_inc(folded, 1)

            iterations(dve, DVE_ORDERS, {
                "setup.start": setup, "front.leaky": leaky, "front.sampling": sampling,
                "gather.interpolate": interpolate, "main.embed": embed_leaky, "main.tokens": norm_tokens,
                "main.query": query, "main.key": key, "main.outer": outer, "main.attend": attend,
                "main.proj": project, "main.mlp": mlp_out, "main.tokens_end": norm_tokens_end,
                "main.proj_end": project_end, "main.mlp_end": mlp_end, "moe.r": choose, "moe.y": expert_sum})


def kernel(**inputs):
    import numpy as np
    import concourse.bacc as bacc
    from concourse.bass_utils import run_bass_kernel_spmd

    x = {k.removeprefix("L0_"): np.asarray(v) for k, v in inputs.items()}

    def chunks(w, p):
        return w.reshape(-1, p, w.shape[-1]).transpose(1, 0, 2)

    def cols(*vs):
        return np.stack([v.reshape(2, HALF).T for v in vs], 1)

    img = x["x"].reshape(GROUPS, TILES, TILE_IMGS, 3, OUT_SIDE, K, K, OUT_SIDE, K, K)
    patches = img.transpose(3, 6, 9, 0, 1, 5, 8, 2, 4, 7).reshape(STEM_K - 1, -1)
    taps = lambda w: w.transpose(2, 3, 1, 0).reshape(TAPS * C, -1)
    experts1 = np.concatenate([x["ffn_w1"].transpose(1, 0, 2).reshape(DIM, -1), x["ffn_w_fc_sh"]], 1)
    experts2 = np.concatenate([x["ffn_w2"].reshape(-1, DIM), x["ffn_w_proj_sh"]], 0)
    experts2 = np.concatenate([experts2, np.zeros((-len(experts2) % 128, DIM), np.float32)], 0)
    k = np.arange(K)
    at = np.stack(np.meshgrid(np.arange(OUT_SIDE) * K, np.arange(OUT_SIDE) * K, indexing="ij"), -1)
    tap = np.stack(np.meshgrid(k, k, indexing="ij"), -1).reshape(1, TAPS, 2)
    base = np.tile(at.reshape(POS, 1, 2) + tap, (TILE_IMGS, TILES, 1))
    image = np.arange(TILES).reshape(1, TILES, 1) * TILE_IMGS + np.repeat(np.arange(TILE_IMGS), POS).reshape(-1, 1, 1)
    img_base = np.broadcast_to(image * SIDE * SIDE, (TPOS, TILES, TAPS))
    head = np.arange(HALF) // HEAD_DIM
    a = {
        "xcol": np.concatenate([np.ones((1, patches.shape[1]), np.float32), patches], 0),
        "stem_w": np.concatenate([x["tok_stem_b"][None], x["tok_stem_w"].reshape(C, -1).T], 0),
        "bn1": np.broadcast_to(np.stack([x["tok_bn1_" + n] for n in "gbmv"]), (STEM_K, 4, C)),
        "ident": np.eye(128, dtype=np.float32),
        "off_w": chunks(taps(x["tok_off_w"]), 128),
        "off_b": np.broadcast_to(np.tile(x["tok_off_b"].reshape(TAPS, 2), (TILES, 1)), (TPOS, TILES * TAPS, 2)),
        "base": base.astype(np.float32),
        "img_base": (img_base.reshape(TPOS, -1) + SIDE).astype(np.float32),
        "bn2": cols(x["tok_dcn_b"], *[x["tok_bn2_" + n] for n in "gbmv"]),
        "dcn_w": chunks(taps(x["tok_dcn_w"]), 128),
        "head_mask": (head[:, None] == head[None]).astype(np.float32),
        "ln_cols": cols(*[x["attn_" + n] for n in ("ln1_w", "ln1_b", "ln2_w", "ln2_b")]),
        "cls_cols": x["cls_tok"].reshape(2, HALF).T,
        "qkv_w": chunks(x["attn_qkv_w"], HALF),
        "qkv_b": x["attn_qkv_b"][None],
        "proj_w": chunks(x["attn_proj_w"], HALF),
        "proj_b": x["attn_proj_b"][None],
        "fc1_w": chunks(x["attn_fc1_w"], HALF),
        "fc1_b": x["attn_fc1_b"].reshape(-1, 128).T,
        "fc2_w": chunks(x["attn_fc2_w"], 128),
        "fc2_b": np.broadcast_to(x["attn_fc2_b"], (128, DIM)),
        "router_w": chunks(x["ffn_router_w"].T, HALF),
        "balance": np.broadcast_to(x["ffn_balance_bias"], (128, EXPERTS)),
        "moe_w1": chunks(experts1, HALF),
        "moe_w2": chunks(experts2, 128),
    }
    nc = bacc.Bacc("TRN2", target_bir_lowering=False, num_devices=1)
    arrays = {f"in_{n}": np.ascontiguousarray(v) for n, v in a.items()}
    args = {n: nc.dram_tensor(f"in_{n}", v.shape, F32, kind="ExternalInput").ap() for n, v in a.items()}
    out = nc.dram_tensor("out", (IMAGES, TOKENS, DIM), F32, kind="ExternalOutput").ap()
    build(nc, args, out)
    return run_bass_kernel_spmd(nc, [arrays], core_ids=[0]).results[0]["out"]
```

```python
from contextlib import ExitStack

import concourse.bass as bass
from concourse import mybir

F32 = mybir.dt.float32
U32 = mybir.dt.uint32
ALU = mybir.AluOpType
ACT = mybir.ActivationFunctionType

IMAGES, GROUP_IMGS, TILE_IMGS = 32, 4, 2
GROUPS = IMAGES // GROUP_IMGS
TILES = GROUP_IMGS // TILE_IMGS
SIDE = 28
K = 4
OUT_SIDE = SIDE // K
POS = OUT_SIDE * OUT_SIDE
TPOS = TILE_IMGS * POS
TAPS = K * K
C = 96
STEM_K = 3 * K * K + 1
DIM = 192
HALF = DIM // 2
HEADS, HEAD_DIM = 12, 16
HALF_HEADS = HEADS // 2
KV_COLS = HALF + HALF_HEADS
HIDDEN = 4 * DIM
EXPERTS = 8
TOKENS = POS + 1
SLOT = 64
CHUNKS = TAPS * C // 128
QUAD = 4
QUADS = TILES * TAPS // QUAD
CORNERS = 4
RING = 4
MOE_CHUNKS = -(-(EXPERTS + 1) * DIM // 128)
ROW = SIDE * 2 * C
SLOPE = 0.01
MARK = 2.0 ** 100
ROUND = 2.0 ** 23

FRONT_USES, FRONT_BANKS = 16, 2
EMBED, TOKMAJOR, YT, QUERY, KV0, KV1, OUTER0, OUTER1, ATTEND, AT, PROJ, ZT, FC1, _a, _b, FC2 = range(16)
MAIN_USES, MAIN_BANKS = 16, 3

GATHERED = (QUADS // RING) * QUAD * 16
TABLE_WRITES = K * 2
PADS = 10
ACT_MAIN, ACT_MOE = 5, 2
DVE_FRONT, DVE_GATHER, DVE_MAIN, DVE_MOE = 12 * TILES, 2 * QUADS, 11, 11

PE_ORDERS = ["""
    setup.start main.embed front.stem:0 main.tokens front.stem:1 gather.sample:0 front.stem:2
    front.stem:3 gather.sample:1 main.yT main.query main.kv:0 main.kv:1 front.turn:0
    front.turn:1 main.outer:0 main.outer:1 front.turn:2 main.attend front.offsets:0 main.aT
    gather.sample:2 main.proj front.stem:4 gather.sample:3 front.stem:5 front.stem:6
    front.stem:7 main.zT main.fc1:0 main.fc1:1 front.turn:3 gather.sample:4 main.fc1:2
    front.turn:4 gather.sample:5 front.turn:5 main.fc2 front.offsets:1 gather.sample:6
    gather.sample:7 setup.end""", """
    moe.f main.embed moe.r front.stem:0 moe.h:3 moe.h:2 main.tokens front.stem:1 gather.sample:0
    moe.h:4 front.stem:2 front.stem:3 moe.h:6 moe.h:0 main.yT front.turn:0 moe.h:1 main.query
    main.kv:0 main.kv:1 front.turn:1 moe.y:8 front.turn:2 main.outer:0 main.outer:1 moe.h:5
    gather.sample:1 main.attend front.offsets:0 moe.y:3 main.aT front.stem:4 gather.sample:2
    main.proj moe.y:5 front.stem:5 gather.sample:3 moe.y:1 front.stem:6 moe.y:4 main.zT
    front.stem:7 gather.sample:4 main.fc1:0 main.fc1:1 front.turn:3 front.turn:4 main.fc1:2
    moe.y:2 moe.y:7 gather.sample:5 main.fc2 front.turn:5 gather.sample:6 moe.y:0
    front.offsets:1 gather.sample:7 moe.y:6"""]
ACT_ORDERS = ["""
    setup.start main.embed front.stem:0 front.stem:1 main.rstd:0 gather.sample:0 front.stem:2
    main.yT front.stem:3 main.query main.kv:0 gather.sample:1 main.kv:1 front.turn:0
    front.turn:1 front.turn:2 main.aT gather.sample:2 front.stem:4 main.rstd:1 front.stem:5
    front.stem:6 front.stem:7 gather.sample:3 main.zT main.fc1:0 front.turn:3 main.fc1:1
    gather.sample:4 main.fc1:2 front.turn:4 front.turn:5 gather.sample:5 main.rstd:2
    gather.sample:6 gather.sample:7 setup.end""", """
    moe.f main.embed moe.r moe.h:3 moe.h:2 front.stem:0 front.stem:1 moe.h:4 main.rstd:0
    front.stem:2 front.stem:3 moe.h:6 main.yT gather.sample:0 front.turn:0 moe.h:0 main.query
    main.kv:0 main.kv:1 moe.h:1 front.turn:1 front.turn:2 moe.h:5 gather.sample:1 main.aT
    front.stem:4 gather.sample:2 main.rstd:1 gather.sample:3 front.stem:5 main.zT front.stem:6
    gather.sample:4 front.stem:7 main.fc1:0 main.fc1:1 front.turn:3 front.turn:4 main.fc1:2
    gather.sample:5 gather.sample:6 front.turn:5 main.rstd:2 gather.sample:7"""]
DVE_ORDERS = ["""
    gather.interpolate:0 gather.interpolate:1 setup.start main.embed main.tokens main.tokens_end
    front.leaky:0 front.leaky:1 gather.interpolate:2 main.query main.key:0 main.key:1
    main.outer:0 main.outer:1 gather.interpolate:3 main.attend front.sampling:0 main.proj
    main.proj_end gather.interpolate:4 front.leaky:2 front.leaky:3 gather.interpolate:5
    gather.interpolate:6 gather.interpolate:7 main.mlp main.mlp_end front.sampling:1""", """
    gather.interpolate:0 gather.interpolate:1 main.embed gather.interpolate:2 main.tokens
    front.leaky:0 main.tokens_end front.leaky:1 moe.r gather.interpolate:3 main.query main.key:0
    main.key:1 moe.y:8 main.outer:0 main.outer:1 gather.interpolate:4 main.attend
    front.sampling:0 moe.y:3 main.proj moe.y:5 main.proj_end moe.y:1 front.leaky:2 moe.y:4
    front.leaky:3 gather.interpolate:5 gather.interpolate:6 gather.interpolate:7 moe.y:2 moe.y:7
    main.mlp moe.y:0 main.mlp_end front.sampling:1 moe.y:6"""]
MOE_SEQ = [entry[4:] for entry in PE_ORDERS[1].split() if entry.startswith("moe.")]
MOE_USES, MOE_BANKS = len(MOE_SEQ), 2
H_ORDER = [int(entry[2:]) for entry in MOE_SEQ if entry.startswith("h")]

STAGE_LAG = {"load": 3, "front": 2, "gather": 1, "main": 0, "moe": -1}


def build(nc, a, out):
    ctx = ExitStack()
    with ctx:
        def sb(name, shape, dt=F32):
            return ctx.enter_context(nc.sbuf_tensor(name, shape, dt))

        def sem(name):
            return ctx.enter_context(nc.semaphore(name))

        table = [nc.dram_tensor(f"corner_table{t}", (TILE_IMGS * SIDE * SIDE + SIDE, 2 * C), F32,
                                kind="Internal").ap() for t in range(TILES)]

        stem_w = sb("stem_w", [STEM_K, C])
        bn1 = sb("bn1", [STEM_K, 4, C])
        off_w = sb("off_w", [128, CHUNKS, 2 * TAPS])
        off_b = sb("off_b", [TPOS, TILES * TAPS, 2])
        base = sb("base", [TPOS, TILES * TAPS, 2])
        img_base = sb("img_base", [TPOS, TILES * TAPS])
        dcn_w = sb("dcn_w", [128, CHUNKS, DIM])
        bn2 = sb("bn2", [HALF, 5, 2])
        bn2_scale = sb("bn2_scale", [HALF, 2])
        bn2_bias = sb("bn2_bias", [HALF, 2])
        qkv_w = sb("qkv_w", [HALF + 1, 2, 3 * DIM])
        proj_w = sb("proj_w", [HALF + 1, 2, DIM])
        fc1_w = sb("fc1_w", [HALF, 2, HIDDEN])
        fc1_b = sb("fc1_b", [128, HIDDEN // 128])
        fc2_w = sb("fc2_w", [128, HIDDEN // 128, DIM])
        fc2_b = sb("fc2_b", [128, DIM])
        ln_cols = sb("ln_cols", [HALF, 4, 2])
        rows = sb("rows", [1, 3 * DIM])
        moe_w1 = sb("moe_w1", [HALF, 2, (EXPERTS + 1) * DIM])
        moe_w2 = sb("moe_w2", [128, MOE_CHUNKS, DIM])
        router_w = sb("router_w", [HALF, 2, EXPERTS])
        balance = sb("balance", [128, EXPERTS])
        cls_cols = sb("cls_cols", [HALF, 2])
        ident = sb("ident", [128, 128])
        head_mask = sb("head_mask", [HALF, KV_COLS])
        zeros = sb("zeros", [SIDE, C])
        consts = sb("consts", [128, 4])
        NEG1, EPS8, EPS5 = (consts[:, j:j + 1] for j in range(3))

        xcol = sb("xcol", [STEM_K, TILES * TAPS * TPOS])
        H = sb("H", [TPOS, TILES, TAPS * C])
        HT = sb("HT", [128, TILES, CHUNKS, TPOS])
        p_yx = sb("p_yx", [TPOS, TILES * TAPS * 2])
        p_int = sb("p_int", [TPOS, TILES * TAPS * 2])
        dist = sb("dist", [TPOS, TILES * TAPS * 2])
        hat = sb("hat", [TPOS, TILES * TAPS, 2, 2])
        idx_f = sb("idx_f", [TPOS, TILES * TAPS])
        idx = sb("idx", [TPOS, TILES * TAPS], U32)
        corner_w = sb("corner_w", [TPOS, TILES * TAPS * CORNERS])
        G = sb("G", [TPOS, RING, QUAD * CORNERS * C])
        S = sb("S", [TPOS, RING, QUAD * C])
        ST = sb("ST", [128, CHUNKS, TILES, TPOS])

        embed = sb("embed", [HALF, 2, GROUP_IMGS, POS])
        xT = sb("xT", [HALF, 2, GROUP_IMGS * SLOT])
        X0 = sb("X0", [128, TILES, DIM])
        stats = sb("stats", [128, TILES, 6])
        mv = sb("mv", [128, TILES, 2])
        var = sb("var", [128, TILES, 2])
        rstd = sb("rstd", [128, TILES, 2])
        U = sb("U", [128, TILES, DIM])
        Y = sb("Y", [128, TILES, DIM])
        yT = sb("yT", [HALF + 1, 2, GROUP_IMGS * SLOT])
        exp_q = sb("exp_q", [HALF, 2 * GROUP_IMGS, TOKENS])
        qT = sb("qT", [HALF, 2, GROUP_IMGS * SLOT])
        exp_k = sb("exp_k", [128, TILES, DIM])
        kS = sb("kS", [128, TILES, DIM])
        vS = sb("vS", [128, TILES, 2, HALF + 1])
        KV = sb("KV", [HALF, GROUP_IMGS * 2, KV_COLS])
        rden = sb("rden", [128, TILES * 2, HALF_HEADS])
        attT = sb("attT", [HALF + 1, 2, GROUP_IMGS * SLOT])
        XR = sb("XR", [128, TILES, DIM])
        zT = sb("zT", [HALF, 2, GROUP_IMGS * SLOT])
        gT = sb("gT", [128, HIDDEN // 128, GROUP_IMGS * SLOT])
        XM = sb("XM", [128, TILES, DIM])

        X1 = sb("X1", [128, TILES, DIM])
        fT = sb("fT", [HALF, 2, GROUP_IMGS * SLOT])
        score = sb("score", [128, TILES * EXPERTS])
        biased = sb("biased", [128, TILES, EXPERTS + 6])
        top8 = sb("top8", [128, TILES, 8])
        chosen = sb("chosen", [128, TILES, 8])
        marked = sb("marked", [128, TILES, EXPERTS + 6])
        comb = sb("comb", [128, TILES, EXPERTS])
        comb_sum = sb("comb_sum", [128, TILES])
        relu = sb("relu", [128, 2, 2, GROUP_IMGS * TOKENS])
        hidT = sb("hidT", [128, MOE_CHUNKS, GROUP_IMGS * SLOT])

        psum = [ctx.enter_context(nc.psum_tensor(f"bank{b}", [128, 512], F32)) for b in range(8)]

        waits_alone = sem("waits_alone")
        loaded_first, loaded_second, loaded_rest = (sem(f"loaded_{n}") for n in ("first", "second", "rest"))
        loaded_late = sem("loaded_late")
        moved = sem("moved")
        set_dve, set_act = sem("set_dve"), sem("set_act")
        consts_ready, pads_ready, stem_ready = sem("consts_ready"), sem("pads_ready"), sem("stem_ready")
        shifts_ready, folded, qkv_row_ready = sem("shifts_ready"), sem("folded"), sem("qkv_row_ready")
        front_filled = [sem(f"front_filled{b}") for b in range(FRONT_BANKS)]
        front_freed = [sem(f"front_freed{b}") for b in range(FRONT_BANKS)]
        sample_filled, sample_freed = [sem("sample_filled")], [sem("sample_freed")]
        main_filled = [sem(f"main_filled{b}") for b in range(MAIN_BANKS)]
        main_freed = [sem(f"main_freed{b}") for b in range(MAIN_BANKS)]
        moe_filled = [sem(f"moe_filled{b}") for b in range(MOE_BANKS)]
        moe_freed = [sem(f"moe_freed{b}") for b in range(MOE_BANKS)]
        xcol_loaded = sem("xcol_loaded")
        leaky_done = sem("leaky_done")
        indices_ready = sem("indices_ready")
        table_padded = sem("table_padded")
        table_written = [sem(f"table_written{t}") for t in range(TILES)]
        gathered = [sem(f"gathered{r}") for r in range(RING)]
        sampled = sem("sampled")
        embed_copied = sem("embed_copied")
        embedded = sem("embedded")
        var_ready, rstd_ready = sem("var_ready"), sem("rstd_ready")
        normed = sem("normed")
        exp_ready = sem("exp_ready")
        hidden_ready = sem("hidden_ready")
        out_written = sem("out_written")
        chain_front, chain_gather = sem("chain_front"), sem("chain_gather")
        chain_main, chain_moe = sem("chain_main"), sem("chain_moe")
        act_main, act_moe = sem("act_main"), sem("act_moe")

        class Banks:
            def __init__(self, first, count, uses, filled, freed):
                self.first, self.count, self.filled_sem, self.freed_sem = first, count, filled, freed
                self.per = [len(range(b, uses, count)) for b in range(count)]

            def ap(self, n):
                return psum[self.first + n % self.count]

            def before(self, g, n):
                return g * self.per[n % self.count] + n // self.count

            def claim(self, eng, g, n):
                wait(eng, self.freed_sem[n % self.count], self.before(g, n))

            def evicted(self, eng, g, n):
                wait(eng, self.freed_sem[n % self.count], self.before(g, n) + 1)

            def filled(self, eng, g, n):
                wait(eng, self.filled_sem[n % self.count], self.before(g, n) + 1)

            def fill(self, ins, n):
                ins.then_inc(self.filled_sem[n % self.count], 1)

            def free(self, ins, n):
                ins.then_inc(self.freed_sem[n % self.count], 1)

        def wait(eng, s, value):
            if isinstance(value, int) and value <= 0:
                return
            eng.wait_ge(s, value)

        def wait_alone(eng, s, value):
            if isinstance(value, int) and value <= 0:
                return
            eng.wait_ge(s, value)
            eng.sem_inc(waits_alone, 1)

        front = Banks(0, FRONT_BANKS, FRONT_USES, front_filled, front_freed)
        sample = Banks(2, 1, QUADS, sample_filled, sample_freed)
        main = Banks(3, MAIN_BANKS, MAIN_USES, main_filled, main_freed)
        moe = Banks(6, MOE_BANKS, MOE_USES, moe_filled, moe_freed)

        def moe_use(kind, n=None):
            return MOE_SEQ.index(kind if n is None else f"{kind}:{n}")

        def stem_use(n):
            return n // 4 * 8 + n % 4

        def turn_use(n):
            return n // 3 * 8 + 4 + n % 3

        def offset_use(t):
            return t * 8 + 7

        class Chain:
            def __init__(self, eng, s, per):
                self.eng, self.s, self.per, self.n = eng, s, per, 0

            def begin(self, g):
                self.g, self.n = g, 0

            def __call__(self, ins, alone=False):
                self.n += 1
                ins.then_inc(self.s, 1)
                (wait_alone if alone else wait)(self.eng, self.s, self.g * self.per + self.n)

            def end(self):
                assert self.n == self.per, (self.n, self.per)

        def tokens(buf, c=None):
            v = buf if c is None else buf[:, c, :]
            return v.rearrange("p (i s) -> p i s", s=SLOT)[:, :, 0:TOKENS]

        def iterations(eng, orders, units, loop_end=GROUPS - 2):
            def iteration(i):
                peeled = isinstance(i, int)
                for entry in orders[0 if peeled and i <= 0 else -1].split():
                    name, _, n = entry.partition(":")
                    stage = name.split(".")[0]
                    if stage == "setup":
                        if peeled and i == -1:
                            units[name]()
                    elif not peeled or 0 <= i + STAGE_LAG[stage] < GROUPS:
                        units[name](i + STAGE_LAG[stage], *([int(n)] if n else []))
            for i in range(-2, 2):
                iteration(i)
            with eng.Fori(2, loop_end) as i:
                iteration(i)
            for i in range(loop_end, GROUPS + 1):
                iteration(i)

        FIRST = [(stem_w[:], "stem_w"), (bn1[:], "bn1")]
        SECOND = [(ident[:], "ident"), (off_w[:], "off_w"), (off_b[:], "off_b"), (base[:], "base"),
                  (img_base[:], "img_base")]
        REST = [(bn2[:], "bn2"), (dcn_w[:], "dcn_w"), (head_mask[:], "head_mask"), (ln_cols[:], "ln_cols"),
                (cls_cols[:], "cls_cols"), (qkv_w[0:HALF], "qkv_w"), (rows[:], "qkv_b"),
                (proj_w[0:HALF], "proj_w"), (proj_w[HALF:HALF + 1, 1, :], "proj_b"),
                (fc1_w[:], "fc1_w"), (fc1_b[:], "fc1_b"), (fc2_w[:], "fc2_w"), (fc2_b[:], "fc2_b")]
        LATE = [(router_w[:], "router_w"), (balance[:], "balance"), (moe_w1[:], "moe_w1"),
                (moe_w2[:], "moe_w2")]

        block = ctx.enter_context(nc.Block())

        @block.sync
        def _(sp):
            def load_first(g):
                if isinstance(g, int) and g == 1:
                    load(g)

            def load_early(g):
                if isinstance(g, int) and 2 <= g <= 3:
                    load(g)

            def load_x(g):
                if not (isinstance(g, int) and g <= 3):
                    load(g)

            def load(g):
                front.filled(sp, g - 1, stem_use(7))
                front.filled(sp, g - 1, stem_use(6))
                sp.dma_start(xcol[:, :], a["xcol"][:, bass.ds(g * xcol.shape[1], xcol.shape[1])])\
                    .then_inc(xcol_loaded, 16)

            def write_table(g):
                for r in range(RING):
                    wait(sp, gathered[r], g * GATHERED)
                for t in range(TILES):
                    wait(sp, leaky_done, g * 4 + 2 * t + 2)
                    for kh in range(K):
                        src = H[:, t, kh * K * C:(kh + 1) * K * C].rearrange("p (w c) -> p w c", w=K)
                        for upper in range(2):
                            first = SIDE + (kh - upper) * SIDE
                            dst = bass.AP(table[t].tensor, first * 2 * C + upper * C,
                                          [[K * ROW, TILE_IMGS * OUT_SIDE], [K * 2 * C, OUT_SIDE],
                                           [2 * C, K], [1, C]])
                            sp.dma_start(dst, src).then_inc(table_written[t], 16)

            def write_out(g):
                moe.evicted(sp, g, MOE_USES - 1)
                view = out.rearrange("(g t s) n c -> s n g t c", t=TILES, s=TILE_IMGS)
                for s in range(TILE_IMGS):
                    sp.dma_start(view[s][:, bass.ds(g, 1)].rearrange("n g t c -> n (g t) c"),
                                 X1[s * SLOT:s * SLOT + TOKENS, :, :]).then_inc(out_written, 16)

            def load_late():
                for dst, name in LATE:
                    sp.dma_start(dst, a[name]).then_inc(loaded_late, 16)

            def setup():
                sp.wait_ge(qkv_row_ready, 1)
                sp.dma_start(qkv_w[HALF:HALF + 1, 1, :], rows[:, :]).then_inc(moved, 16)

            for dst, name in FIRST:
                sp.dma_start(dst, a[name]).then_inc(loaded_first, 16)
            sp.dma_start(xcol[:, :], a["xcol"][:, 0:xcol.shape[1]]).then_inc(xcol_loaded, 16)
            for dst, name in SECOND:
                sp.dma_start(dst, a[name]).then_inc(loaded_second, 16)
            sp.wait_ge(pads_ready, 1)
            for t in range(TILES):
                for r, half in ((0, 0), (TILE_IMGS * SIDE, 1)):
                    sp.dma_start(table[t][r * SIDE:(r + 1) * SIDE, half * C:(half + 1) * C], zeros[:, :])\
                        .then_inc(table_padded, 16)
            for dst, name in REST:
                sp.dma_start(dst, a[name]).then_inc(loaded_rest, 16)
            iterations(sp, ["setup.load setup.start load.early front.table load.first load.x moe.out"],
                       {"load.x": load_x, "load.early": load_early, "load.first": load_first, "front.table": write_table, "moe.out": write_out,
                        "setup.start": setup, "setup.load": load_late}, loop_end=GROUPS - 3)
            sp.wait_ge(out_written, GROUPS * TILE_IMGS * 16)
            for t in range(TILES):
                sp.wait_ge(table_written[t], GROUPS * TABLE_WRITES * 16)

        @block.gpsimd
        def _(pool):
            def gather(g):
                for n in range(QUADS):
                    if n % (QUADS // TILES) == 0:
                        wait_alone(pool, indices_ready, g * TILES + n * TILES // QUADS + 1)
                        wait_alone(pool, table_written[n * TILES // QUADS], (g + 1) * TABLE_WRITES * 16)
                    wait_alone(pool, sampled, g * QUADS + n - RING + 1)
                    for k in range(QUAD):
                        tap = n * QUAD + k
                        nc.gpsimd.indirect_dma_start(
                            out=G[:, n % RING, k * CORNERS * C:(k + 1) * CORNERS * C], out_offset=None,
                            in_=table[n * TILES // QUADS][:, :],
                            in_offset=bass.IndirectOffsetOnAxis(ap=idx[:, tap:tap + 1], axis=0),
                        ).then_inc(gathered[n % RING], 16)

            for j, (pad, value) in enumerate((
                    (zeros[:], 0.0), (xT[:], 0.0), (qT[:], 1.0), (attT[HALF:HALF + 1], 1.0), (yT[HALF:HALF + 1], 1.0),
                    (vS[:, :, :, HALF:HALF + 1], 1.0), (biased[:, :, EXPERTS:], -MARK),
                    (chosen[:, :, 2:], -MARK), (gT[:], 0.0), (hidT[:], 0.0))):
                wait(pool, pads_ready, j)
                nc.gpsimd.memset(pad, value).then_inc(pads_ready, 1)
            pool.wait_ge(pads_ready, PADS)
            pool.wait_ge(table_padded, TILES * 32)
            iterations(pool, ["gather.taps"], {"gather.taps": gather})

        @block.tensor
        def _(pe):
            mm = nc.tensor.matmul

            def stem(g, n):
                if n == 0:
                    pe.wait_ge(xcol_loaded, (g + 1) * 16)
                front.claim(pe, g, stem_use(n))
                bank = front.ap(stem_use(n))
                for k in range(QUAD):
                    at = (n * QUAD + k) * TPOS
                    ins = mm(bank[0:TPOS, k * C:(k + 1) * C], xcol[:, at:at + TPOS], stem_w[:, :],
                             start=True, stop=True)
                front.fill(ins, stem_use(n))

            def turn_stem(g, n):
                if isinstance(g, int) and g == n == 0:
                    pe.wait_ge(loaded_second, 16 * len(SECOND))
                t, j = divmod(n, 3)
                if j == 0:
                    pe.wait_ge(leaky_done, g * 4 + 2 * t + 2)
                front.claim(pe, g, turn_use(n))
                bank = front.ap(turn_use(n))
                for k in range(4):
                    at = (4 * j + k) * 128
                    ins = nc.tensor.transpose(bank[:, k * TPOS:(k + 1) * TPOS], H[:, t, at:at + 128],
                                              ident[0:TPOS, 0:TPOS])
                front.fill(ins, turn_use(n))

            def offsets(g, t):
                for j in range(3):
                    front.evicted(pe, g, turn_use(3 * t + j))
                front.claim(pe, g, offset_use(t))
                for c in range(CHUNKS):
                    ins = mm(front.ap(offset_use(t))[0:TPOS, 0:2 * TAPS], HT[:, t, c, :], off_w[:, c, :],
                             start=(c == 0), stop=(c == CHUNKS - 1))
                front.fill(ins, offset_use(t))

            def turn_sample(g, n):
                pe.wait_ge(sampled, g * QUADS + n + 1)
                sample.claim(pe, g, n)
                bank = sample.ap(n)
                for k in range(3):
                    ins = nc.tensor.transpose(bank[:, k * TPOS:(k + 1) * TPOS],
                                              S[:, n % RING, k * 128:(k + 1) * 128],
                                              ident[0:TPOS, 0:TPOS])
                sample.fill(ins, n)

            def embed_patches(g):
                sample.evicted(pe, g, QUADS - 2)
                sample.evicted(pe, g, QUADS - 1)
                main.claim(pe, g, EMBED)
                bank = main.ap(EMBED)
                n = TILES * TPOS
                for m in range(2):
                    for c in range(CHUNKS):
                        ins = mm(bank[0:HALF, m * n:(m + 1) * n], dcn_w[:, c, m * HALF:(m + 1) * HALF],
                                 ST[:, c, :, :].rearrange("p t s -> p (t s)"),
                                 start=(c == 0), stop=(c == CHUNKS - 1))
                main.fill(ins, EMBED)

            def to_tokens(g):
                pe.wait_ge(embedded, g + 1)
                main.claim(pe, g, TOKMAJOR)
                bank = main.ap(TOKMAJOR)
                for t in range(TILES):
                    for c in range(2):
                        at = t * DIM + c * HALF
                        ins = nc.tensor.transpose(bank[:, at:at + HALF], xT[:, c, t * 128:(t + 1) * 128],
                                                  ident[0:HALF, 0:HALF])
                main.fill(ins, TOKMAJOR)

            def norm_to_features(g, banks, use, norm):
                pe.wait_ge(normed, g * 3 + norm + 1)
                to_features(g, banks, use)

            def attention_to_features(g):
                main.evicted(pe, g, ATTEND)
                to_features(g, main, AT)

            def to_features(g, banks, use):
                banks.claim(pe, g, use)
                bank = banks.ap(use)
                for t in range(TILES):
                    for c in range(2):
                        at = c * 256 + t * 128
                        ins = nc.tensor.transpose(bank[0:HALF, at:at + 128],
                                                  Y[:, t, c * HALF:(c + 1) * HALF], ident[:, :])
                banks.fill(ins, use)

            def chunk(c, buf):
                return buf[0:HALF + c, c, :]

            def query(g):
                main.evicted(pe, g, YT)
                main.claim(pe, g, QUERY)
                bank = main.ap(QUERY)
                n = GROUP_IMGS * TOKENS
                for m in range(2):
                    for c in range(2):
                        ins = mm(bank[0:HALF, m * n:(m + 1) * n],
                                 chunk(c, qkv_w)[:, m * HALF:(m + 1) * HALF], tokens(chunk(c, yT)),
                                 start=(c == 0), stop=(c == 1))
                main.fill(ins, QUERY)

            def key_value(g, t):
                main.claim(pe, g, KV0 + t)
                bank = main.ap(KV0 + t)
                for c in range(2):
                    ins = mm(bank[:, 0:2 * DIM], chunk(c, yT)[:, t * 128:(t + 1) * 128],
                             chunk(c, qkv_w)[:, DIM:], start=(c == 0), stop=(c == 1))
                main.fill(ins, KV0 + t)

            def outer(g, s):
                if s == 0:
                    main.evicted(pe, g, KV0)
                    main.evicted(pe, g, KV1)
                main.claim(pe, g, OUTER0 + s)
                bank = main.ap(OUTER0 + s)
                w = HALF + 1
                p = slice(s * SLOT, s * SLOT + TOKENS)
                for t in range(TILES):
                    for c in range(2):
                        at = (t * 2 + c) * w
                        ins = mm(bank[0:HALF, at:at + w], kS[p, t, c * HALF:(c + 1) * HALF], vS[p, t, c, :],
                                 start=True, stop=True)
                main.fill(ins, OUTER0 + s)

            def attend(g):
                main.evicted(pe, g, QUERY)
                main.evicted(pe, g, OUTER0)
                main.evicted(pe, g, OUTER1)
                main.claim(pe, g, ATTEND)
                bank = main.ap(ATTEND)
                for i in range(GROUP_IMGS):
                    t, s = divmod(i, TILE_IMGS)
                    for c in range(2):
                        at = (t * 2 + c) * KV_COLS
                        ins = mm(bank[s * SLOT:(s + 1) * SLOT, at:at + KV_COLS],
                                 qT[:, c, i * SLOT:(i + 1) * SLOT], KV[:, (s * TILES + t) * 2 + c, :],
                                 start=True, stop=True)
                main.fill(ins, ATTEND)

            def project(g):
                main.evicted(pe, g, AT)
                main.claim(pe, g, PROJ)
                bank = main.ap(PROJ)
                for t in range(TILES):
                    for c in range(2):
                        ins = mm(bank[:, t * DIM:(t + 1) * DIM], chunk(c, attT)[:, t * 128:(t + 1) * 128],
                                 chunk(c, proj_w), start=(c == 0), stop=(c == 1))
                main.fill(ins, PROJ)

            def fc1(g, n):
                main.evicted(pe, g, ZT)
                main.claim(pe, g, FC1 + n)
                bank = main.ap(FC1 + n)
                w = GROUP_IMGS * TOKENS
                for k in range(2):
                    m = (2 * n + k) * 128
                    for c in range(2):
                        ins = mm(bank[:, k * w:(k + 1) * w], fc1_w[:, c, m:m + 128], tokens(zT, c),
                                 start=(c == 0), stop=(c == 1))
                main.fill(ins, FC1 + n)

            def fc2(g):
                for n in range(3):
                    main.evicted(pe, g, FC1 + n)
                main.claim(pe, g, FC2)
                bank = main.ap(FC2)
                for t in range(TILES):
                    dst = bank[:, t * DIM:(t + 1) * DIM]
                    for m in range(HIDDEN // 128):
                        ins = mm(dst, gT[:, m, t * 128:(t + 1) * 128], fc2_w[:, m, :],
                                 start=(m == 0), stop=(m == HIDDEN // 128 - 1))
                main.fill(ins, FC2)

            def router(g):
                n = moe_use("r")
                moe.evicted(pe, g, 0)
                moe.claim(pe, g, n)
                bank = moe.ap(n)
                for t in range(TILES):
                    for c in range(2):
                        ins = mm(bank[:, t * EXPERTS:(t + 1) * EXPERTS], fT[:, c, t * 128:(t + 1) * 128],
                                 router_w[:, c, :], start=(c == 0), stop=(c == 1))
                moe.fill(ins, n)

            def hidden(g, pair):
                n = moe_use("h", pair)
                moe.claim(pe, g, n)
                bank = moe.ap(n)
                w = GROUP_IMGS * TOKENS
                for k in range(2):
                    at = (2 * pair + k) * 128
                    rows_ = min(128, (EXPERTS + 1) * DIM - at)
                    for c in range(2):
                        ins = mm(bank[0:rows_, k * w:(k + 1) * w], moe_w1[:, c, at:at + rows_],
                                 tokens(fT, c), start=(c == 0), stop=(c == 1))
                moe.fill(ins, n)

            def expert_out(g, e):
                n = moe_use("y", e)
                parts = [(e * DIM // 128, slice(0, 128)), (e * DIM // 128 + 1, slice(0, 64))] if e % 2 == 0 \
                    else [(e * DIM // 128, slice(64, 128)), (e * DIM // 128 + 1, slice(0, 128))]
                pair = max(H_ORDER.index(c // 2) for c, _ in parts)
                pe.wait_ge(hidden_ready, g * len(H_ORDER) + pair + 1)
                moe.claim(pe, g, n)
                bank = moe.ap(n)
                for t in range(TILES):
                    for j, (c, p) in enumerate(parts):
                        ins = mm(bank[:, t * DIM:(t + 1) * DIM], hidT[p, c, t * 128:(t + 1) * 128],
                                 moe_w2[p, c, :], start=(j == 0), stop=(j == 1))
                moe.fill(ins, n)

            def setup():
                pe.wait_ge(loaded_rest, 16 * len(REST))
                pe.wait_ge(pads_ready, PADS)
                for h in range(2):
                    for c in range(2):
                        ins = mm(main.ap(h)[0:1, 0:288], ln_cols[:, 1, c:c + 1],
                                 qkv_w[0:HALF, c, h * 288:(h + 1) * 288], start=(c == 0), stop=(c == 1))
                for m in range(HIDDEN // 128):
                    for c in range(2):
                        ins = mm(main.ap(2)[:, m:m + 1], fc1_w[:, c, m * 128:(m + 1) * 128],
                                 ln_cols[:, 3, c:c + 1], start=(c == 0), stop=(c == 1))
                ins.then_inc(shifts_ready, 1)

            def setup_end():
                pe.wait_ge(loaded_late, 16 * len(LATE))
                pe.wait_ge(folded, 1)
                pe.wait_ge(moved, 16)

            pe.wait_ge(loaded_first, 16 * len(FIRST))
            pe.wait_ge(stem_ready, 1)
            iterations(pe, PE_ORDERS, {
                "setup.start": setup, "setup.end": setup_end,
                "front.stem": stem, "front.turn": turn_stem, "front.offsets": offsets,
                "gather.sample": turn_sample, "main.embed": embed_patches, "main.tokens": to_tokens,
                "main.yT": lambda g: norm_to_features(g, main, YT, 0),
                "main.zT": lambda g: norm_to_features(g, main, ZT, 1), "main.query": query,
                "main.kv": key_value, "main.outer": outer, "main.attend": attend,
                "main.aT": attention_to_features, "main.proj": project, "main.fc1": fc1,
                "main.fc2": fc2, "moe.f": lambda g: norm_to_features(g, moe, moe_use("f"), 2),
                "moe.r": router, "moe.h": hidden, "moe.y": expert_out})

        @block.scalar
        def _(act):
            A = nc.scalar.activation
            link_main, link_moe = Chain(act, act_main, ACT_MAIN), Chain(act, act_moe, ACT_MOE)
            w = GROUP_IMGS * TOKENS

            def stem(g, n):
                t, q = divmod(n, 4)
                if q == 0:
                    wait(act, table_written[t], g * TABLE_WRITES * 16)
                front.filled(act, g, stem_use(n))
                front.free(A(H[:, t, q * QUAD * C:(q + 1) * QUAD * C],
                             front.ap(stem_use(n))[0:TPOS, 0:QUAD * C], ACT.Copy), stem_use(n))

            def turn_stem(g, n):
                front.filled(act, g, turn_use(n))
                t, j = divmod(n, 3)
                front.free(A(HT[:, t, 4 * j:4 * j + 4, :].rearrange("p c s -> p (c s)"),
                             front.ap(turn_use(n))[:, 0:4 * TPOS], ACT.Copy), turn_use(n))

            def turn_sample(g, n):
                if n == 0 and not (isinstance(g, int) and g == 0):
                    main.filled(act, g - 1, EMBED)
                sample.filled(act, g, n)
                t, q = divmod(n, 4)
                sample.free(A(ST[:, 3 * q:3 * q + 3, t, :],
                             sample.ap(n)[:, 0:3 * TPOS].rearrange("p (c s) -> p c s", c=3),
                             ACT.Copy), n)

            def embed_copy(g):
                main.filled(act, g, EMBED)
                wait(act, embedded, g)
                link_main.begin(g)
                n = TILES * TPOS
                for m in range(2):
                    ins = A(embed[:, m, :, :].rearrange("p i s -> p (i s)"),
                            main.ap(EMBED)[0:HALF, m * n:(m + 1) * n], ACT.Identity,
                            bias=bn2_bias[:, m:m + 1], scale=bn2_scale[:, m:m + 1])
                    if m == 0:
                        ins.then_inc(embed_copied, 1)
                main.free(ins, EMBED)

            def inverse_root(g, norm):
                act.wait_ge(var_ready, g * 3 + norm + 1)
                n = 4 if norm == 0 else 2
                v = var[:].rearrange("p a b -> p (a b)")[:, 0:n]
                link_main(A(v, v, ACT.Ln))
                A(rstd[:].rearrange("p a b -> p (a b)")[:, 0:n], v, ACT.Exp, scale=-0.5)\
                    .then_inc(rstd_ready, 1)

            def evict_features(g, banks, use, dst):
                banks.filled(act, g, use)
                if dst is fT:
                    moe.filled(act, g - 1, MOE_USES - 1)
                banks.free(A(dst[0:HALF].rearrange("p c s -> p (c s)"), banks.ap(use)[0:HALF, :], ACT.Copy),
                           use)

            def exp_query(g):
                main.filled(act, g, QUERY)
                A(exp_q[:].rearrange("p m s -> p (m s)"), main.ap(QUERY)[0:HALF, 0:2 * w], ACT.Exp,
                  bias=NEG1[0:HALF]).then_inc(exp_ready, 1)

            def key_value(g, t):
                main.filled(act, g, KV0 + t)
                bank = main.ap(KV0 + t)
                link_main(A(vS[:, t, :, 0:HALF], bank[:, DIM:2 * DIM].rearrange("p (c f) -> p c f", c=2),
                            ACT.Copy))
                A(exp_k[:, t, :], bank[:, 0:DIM], ACT.Exp, bias=NEG1).then_inc(exp_ready, 1)

            def gelu(g, n):
                main.filled(act, g, FC1 + n)
                for k in range(2):
                    m = 2 * n + k
                    ins = A(tokens(gT, m),
                            main.ap(FC1 + n)[:, k * w:(k + 1) * w].rearrange("p (i s) -> p i s", s=TOKENS),
                            ACT.Gelu, bias=fc1_b[:, m:m + 1])
                main.free(ins, FC1 + n)
                if n == 2:
                    nc.scalar.preload_act_table_set("natural_log_exp_and_others")

            def router_exp(g):
                n = moe_use("r")
                moe.filled(act, g, n)
                link_moe.begin(g)
                moe.free(A(score[:, :], moe.ap(n)[:, 0:TILES * EXPERTS], ACT.Exp, scale=-1.0), n)

            def relu_squared(g, pair):
                n = moe_use("h", pair)
                moe.filled(act, g, n)
                if pair == H_ORDER[0] and not (isinstance(g, int) and g == 0):
                    moe.filled(act, g - 1, MOE_USES - 1)
                tmp = relu[:, H_ORDER.index(pair) % 2]
                chunks = [2] if pair < 6 else [1, 1]
                at, last = 0, None
                for k, width in enumerate(chunks):
                    r = 64 if k else 128
                    src = moe.ap(n)[0:r, k * w:(k + width) * w]
                    ins = A(tmp[0:r, k:k + width, :].rearrange("p c s -> p (c s)"), src, ACT.Relu)
                    if k < len(chunks) - 1:
                        link_moe(ins)
                moe.free(ins, n)
                moe.evicted(act, g, n)
                for k, width in enumerate(chunks):
                    r = 64 if k else 128
                    c = 2 * pair + k
                    dst = hidT[0:r, c:c + width, :].rearrange("p c (i s) -> p c i s", s=SLOT)[:, :, :, 0:TOKENS]
                    ins = A(dst, tmp[0:r, k:k + width, :].rearrange("p c (i s) -> p c i s", s=TOKENS),
                            ACT.Square)
                    if k < len(chunks) - 1:
                        link_moe(ins)
                ins.then_inc(hidden_ready, 1)

            nc.scalar.preload_act_table_set("natural_log_exp_and_others")
            act.wait_ge(consts_ready, 3)
            act.wait_ge(loaded_first, 16 * len(FIRST))
            A(bn1[:, 3, :], bn1[:, 3, :], ACT.Ln, bias=EPS5[0:STEM_K]).then_inc(set_act, 1)
            act.wait_ge(set_act, 1)
            A(bn1[:, 3, :], bn1[:, 3, :], ACT.Exp, scale=-0.5).then_inc(set_act, 1)

            def setup():
                act.wait_ge(loaded_rest, 16 * len(REST))
                act.wait_ge(pads_ready, PADS)
                A(bn2[:, 4, :], bn2[:, 4, :], ACT.Ln, bias=EPS5[0:HALF]).then_inc(set_act, 1)
                act.wait_ge(set_act, 3)
                A(bn2[:, 4, :], bn2[:, 4, :], ACT.Exp, scale=-0.5).then_inc(set_act, 1)

            def setup_end():
                act.wait_ge(folded, 1)

            iterations(act, ACT_ORDERS, {
                "setup.start": setup, "setup.end": setup_end,
                "front.stem": stem, "front.turn": turn_stem, "gather.sample": turn_sample,
                "main.embed": embed_copy, "main.rstd": inverse_root,
                "main.yT": lambda g: evict_features(g, main, YT, yT),
                "main.zT": lambda g: evict_features(g, main, ZT, zT),
                "main.aT": lambda g: evict_features(g, main, AT, attT), "main.query": exp_query,
                "main.kv": key_value, "main.fc1": gelu,
                "moe.f": lambda g: evict_features(g, moe, moe_use("f"), fT),
                "moe.r": router_exp, "moe.h": relu_squared})

        @block.vector
        def _(dve):
            v = nc.vector
            link_front = Chain(dve, chain_front, DVE_FRONT)
            link_gather = Chain(dve, chain_gather, DVE_GATHER)
            link_main = Chain(dve, chain_main, DVE_MAIN)
            link_moe = Chain(dve, chain_moe, DVE_MOE)
            half_taps = TAPS * C // 2

            def leaky(g, n):
                front.evicted(dve, g, stem_use(2 * n))
                front.evicted(dve, g, stem_use(2 * n + 1))
                h = H[:, n // 2, (n % 2) * half_taps:(n % 2 + 1) * half_taps]
                v.scalar_tensor_tensor(out=h, in0=h, scalar=SLOPE, in1=h, op0=ALU.mult, op1=ALU.max)\
                    .then_inc(leaky_done, 1)

            def sampling(g, t):
                if t == 0:
                    link_front.begin(g)
                    if isinstance(g, int) and g == 0:
                        dve.wait_ge(loaded_second, 16 * len(SECOND))
                front.filled(dve, g, offset_use(t))
                yx, taps = slice(t * TAPS * 2, (t + 1) * TAPS * 2), slice(t * TAPS, (t + 1) * TAPS)
                p, pi, d = p_yx[:, yx], p_int[:, yx], dist[:, yx]
                ins = v.tensor_tensor(p, front.ap(offset_use(t))[0:TPOS, 0:2 * TAPS],
                                      off_b[:, taps, :].rearrange("p t y -> p (t y)"), ALU.add)
                front.free(ins, offset_use(t))
                front.evicted(dve, g, offset_use(t))
                link_front(v.tensor_tensor(p, p, base[:, taps, :].rearrange("p t y -> p (t y)"), ALU.add))
                link_front(v.tensor_scalar(pi, p, 0.5, SIDE - 1.5, ALU.max, ALU.min))
                link_front(v.tensor_scalar(pi, pi, -0.5, ROUND, ALU.add, ALU.add))
                link_front(v.tensor_scalar(pi, pi, -ROUND, None, ALU.add))
                corner = pi.rearrange("p (t y) -> p t y", y=2)
                link_front(v.scalar_tensor_tensor(out=idx_f[:, taps], in0=corner[:, :, 0], scalar=float(SIDE),
                                                  in1=corner[:, :, 1], op0=ALU.mult, op1=ALU.add))
                later = TILES - 1 - t
                for r in range(RING):
                    wait(dve, gathered[r], g * GATHERED - later * (GATHERED // TILES))
                v.tensor_tensor(idx[:, taps], idx_f[:, taps], img_base[:, taps], ALU.add)\
                    .then_inc(indices_ready, 1)
                hats = hat[:, taps, :, :].rearrange("p t y k -> p (t y) k")
                link_front(v.tensor_tensor(d, p, pi, ALU.subtract))
                for k in range(2):
                    link_front(v.scalar_tensor_tensor(out=hats[:, :, k], in0=d, scalar=-1.0, in1=d,
                                                      op0=ALU.mult, op1=ALU.min))
                    if k == 0:
                        link_front(v.tensor_scalar(d, d, -1.0, None, ALU.add))
                flat = hat[:, taps, :, :].rearrange("p t y k -> p (t y k)")
                link_front(v.tensor_scalar(flat, flat, 1.0, 0.0, ALU.add, ALU.max))
                wait(dve, sampled, g * QUADS - later * (QUADS // TILES))
                cw = corner_w[:].rearrange("p (t x y) -> p t x y", x=2, y=2)
                for x in range(2):
                    link_front(v.tensor_tensor(cw[:, taps, x, :],
                                               hat[:, taps, 1, x:x + 1].to_broadcast([TPOS, TAPS, 2]),
                                               hat[:, taps, 0, :], ALU.mult))

            def interpolate(g, n):
                if n == 0:
                    link_gather.begin(g)
                dve.wait_ge(gathered[n % RING], g * GATHERED + (n // RING + 1) * QUAD * 16)
                if n >= RING:
                    sample.filled(dve, g, n - RING)
                elif not (isinstance(g, int) and g == 0):
                    sample.filled(dve, g - 1, n + QUADS - RING)
                m = QUAD * CORNERS
                quad = G[:, n % RING, :]
                q = quad.rearrange("p (m c) -> p m c", c=C)
                link_gather(v.tensor_tensor(
                    q, q, corner_w[:, n * m:(n + 1) * m].unsqueeze(2).to_broadcast([TPOS, m, C]), ALU.mult))
                half = quad.rearrange("p (k x r) -> p k x r", x=2, r=2 * C)
                link_gather(v.tensor_tensor(half[:, :, 0, :], half[:, :, 0, :], half[:, :, 1, :], ALU.add))
                four = quad.rearrange("p (k y c) -> p k y c", y=CORNERS, c=C)
                v.tensor_tensor(S[:, n % RING, :].rearrange("p (k c) -> p k c", c=C), four[:, :, 0, :],
                                four[:, :, 1, :], ALU.add).then_inc(sampled, 1)

            def embed_leaky(g):
                link_main.begin(g)
                dve.wait_ge(embed_copied, g + 1)
                main.evicted(dve, g, EMBED)
                dst = xT[:].rearrange("p c (i s) -> p (c i) s", s=SLOT)[:, :, 1:TOKENS]
                src = embed[:].rearrange("p c i s -> p (c i) s")
                v.scalar_tensor_tensor(out=dst, in0=src, scalar=SLOPE, in1=src, op0=ALU.mult, op1=ALU.max)\
                    .then_inc(embedded, 1)

            def moments(src):
                for t in range(TILES):
                    ins = v.bn_stats(stats[:, t, :], src[:, t, :])
                link_main(ins, alone=True)
                for t in range(TILES):
                    ins = v.bn_aggr(mv[:, t, :], stats[:, t, :])
                link_main(ins)

            def normalise(dst, src, scale):
                for t in range(TILES):
                    ins = v.tensor_scalar(dst[:, t, :], src[:, t, :], mv[:, t, 0:1], scale(t),
                                          ALU.subtract, ALU.mult)
                return ins

            def norm_tokens(g):
                main.filled(dve, g, TOKMAJOR)
                ins = v.tensor_copy(X0[:].rearrange("p t c -> p (t c)"), main.ap(TOKMAJOR)[:, 0:TILES * DIM])
                main.free(ins, TOKMAJOR)
                main.evicted(dve, g, TOKMAJOR)
                moments(X0)
                link_main(v.tensor_scalar(var[:, :, 0], mv[:, :, 1], 1e-5, None, ALU.add))
                v_ = v.scalar_tensor_tensor(out=var[:, :, 1], in0=var[:, :, 0], scalar=1e-8,
                                            in1=mv[:, :, 1], op0=ALU.mult, op1=ALU.add)
                v_.then_inc(var_ready, 1)

            def norm_tokens_end(g):
                dve.wait_ge(rstd_ready, g * 3 + 1)
                if not (isinstance(g, int) and g == 0):
                    moe.filled(dve, g - 1, moe_use("f"))
                normalise(Y, X0, lambda t: rstd[:, t, 1:2]).then_inc(normed, 1)
                link_main(normalise(U, X0, lambda t: rstd[:, t, 0:1]))

            def variance(src, eps):
                moments(src)
                v.tensor_scalar(var[:].rearrange("p a b -> p (a b)")[:, 0:2], mv[:, :, 1], eps, None,
                                ALU.add).then_inc(var_ready, 1)

            def norm_again(g, src, norm):
                dve.wait_ge(rstd_ready, g * 3 + norm + 1)
                r = rstd[:].rearrange("p a b -> p (a b)")
                normalise(Y, src, lambda t: r[:, t:t + 1]).then_inc(normed, 1)

            def elu(g, use, n, dst, e, src):
                dve.wait_ge(exp_ready, g * 3 + n + 1)
                main.free(v.scalar_tensor_tensor(out=dst, in0=e, scalar=1.0, in1=src, op0=ALU.min,
                                                 op1=ALU.max), use)

            def query(g):
                m = 2 * GROUP_IMGS
                elu(g, QUERY, 0, qT[:].rearrange("p c (i s) -> p (c i) s", s=SLOT)[:, :, 0:TOKENS], exp_q[:],
                    main.ap(QUERY)[0:HALF, 0:m * TOKENS].rearrange("p (m s) -> p m s", m=m))

            def key(g, t):
                elu(g, KV0 + t, 1 + t, kS[:, t, :], exp_k[:, t, :], main.ap(KV0 + t)[:, 0:DIM])

            def outer(g, s):
                main.filled(dve, g, OUTER0 + s)
                m = TILES * 2
                kv = main.ap(OUTER0 + s)[0:HALF, 0:m * (HALF + 1)].rearrange("p (m f) -> p m f", m=m)
                mask = head_mask[:].unsqueeze(1)
                v.tensor_tensor(KV[:, s * m:(s + 1) * m, 0:HALF], kv[:, :, 0:HALF],
                                mask[:, :, 0:HALF].to_broadcast([HALF, m, HALF]), ALU.mult)
                ins = v.tensor_tensor(KV[:, s * m:(s + 1) * m, HALF:],
                                      kv[:, :, HALF:HALF + 1].to_broadcast([HALF, m, HALF_HEADS]),
                                      mask[:, :, HALF:].to_broadcast([HALF, m, HALF_HEADS]), ALU.mult)
                main.free(ins, OUTER0 + s)

            def attend(g):
                main.filled(dve, g, ATTEND)
                m = TILES * 2
                sums = main.ap(ATTEND)[:, 0:m * KV_COLS].rearrange("p (m f) -> p m f", m=m)
                link_main(v.reciprocal(rden[:], sums[:, :, HALF:]))
                ins = v.tensor_tensor(Y[:].rearrange("p t (c h d) -> p (t c) h d", c=2, d=HEAD_DIM),
                                      sums[:, :, 0:HALF].rearrange("p m (h d) -> p m h d", d=HEAD_DIM),
                                      rden[:].unsqueeze(3).to_broadcast([128, m, HALF_HEADS, HEAD_DIM]),
                                      ALU.mult)
                main.free(ins, ATTEND)

            def project(g):
                main.filled(dve, g, PROJ)
                flat = [b[:].rearrange("p t c -> p (t c)") for b in (XR, U, X0)]
                ins = v.tensor_tensor(flat[0], flat[1], main.ap(PROJ)[:, 0:TILES * DIM], ALU.add)
                main.free(ins, PROJ)
                main.evicted(dve, g, PROJ)
                variance(XR, 1e-8)

            def project_end(g):
                norm_again(g, XR, 1)
                flat = [b[:].rearrange("p t c -> p (t c)") for b in (XR, U, X0)]
                link_main(v.tensor_tensor(flat[2], flat[2], flat[0], ALU.add))
                link_main(v.tensor_tensor(X0[:], X0[:], fc2_b[:].unsqueeze(1).to_broadcast([128, TILES, DIM]),
                                          ALU.add))

            def mlp_out(g):
                main.filled(dve, g, FC2)
                flat = [b[:].rearrange("p t c -> p (t c)") for b in (XM, X0)]
                ins = v.tensor_tensor(flat[0], flat[1], main.ap(FC2)[:, 0:TILES * DIM], ALU.add)
                main.free(ins, FC2)
                main.evicted(dve, g, FC2)
                variance(XM, 1e-5)

            def mlp_end(g):
                norm_again(g, XM, 2)
                link_main.end()

            def choose(g):
                moe.evicted(dve, g, moe_use("r"))
                link_moe.begin(g)
                link_moe(v.tensor_scalar(score[:], score[:], 1.0, None, ALU.add))
                link_moe(v.reciprocal(score[:], score[:]))
                s3 = score[:].rearrange("p (t e) -> p t e", t=TILES)
                link_moe(v.tensor_tensor(biased[:, :, 0:EXPERTS], s3,
                                         balance[:].unsqueeze(1).to_broadcast([128, TILES, EXPERTS]), ALU.add),
                         alone=True)
                for t in range(TILES):
                    ins = v.max(out=top8[:, t, :], in_=biased[:, t, 0:EXPERTS])
                link_moe(ins)
                link_moe(v.tensor_copy(chosen[:, :, 0:2], top8[:, :, 0:2]), alone=True)
                for t in range(TILES):
                    ins = v.match_replace(out=marked[:, t, :], in_to_replace=chosen[:, t, :],
                                          in_values=biased[:, t, :], imm_value=MARK)
                link_moe(ins)
                for t in range(TILES):
                    ins = v.scalar_tensor_tensor(out=comb[:, t, :], in0=marked[:, t, 0:EXPERTS], scalar=MARK,
                                                 in1=s3[:, t, :], op0=ALU.is_equal, op1=ALU.mult,
                                                 accum_out=comb_sum[:, t:t + 1])
                    link_moe(ins)
                link_moe(v.tensor_scalar(comb_sum[:], comb_sum[:], 1e-20, None, ALU.add))
                link_moe(v.reciprocal(comb_sum[:], comb_sum[:]))
                link_moe(v.tensor_tensor(comb[:], comb[:],
                                         comb_sum[:].unsqueeze(2).to_broadcast([128, TILES, EXPERTS]),
                                         ALU.mult))

            def expert_sum(g, e):
                n = moe_use("y", e)
                moe.filled(dve, g, n)
                if e == EXPERTS:
                    wait(dve, out_written, g * TILE_IMGS * 16)
                    flat = [b[:].rearrange("p t c -> p (t c)") for b in (X1, XM)]
                    ins = v.tensor_tensor(flat[0], flat[1], moe.ap(n)[:, 0:TILES * DIM], ALU.add)
                else:
                    for t in range(TILES):
                        ins = v.scalar_tensor_tensor(
                            out=X1[:, t, :], in0=moe.ap(n)[:, t * DIM:(t + 1) * DIM], scalar=comb[:, t, e:e + 1],
                            in1=X1[:, t, :], op0=ALU.mult, op1=ALU.add)
                moe.free(ins, n)
                moe.evicted(dve, g, n)
                if n == MOE_USES - 1:
                    link_moe.end()

            for j, value in enumerate((-1.0, 1e-8, 1e-5)):
                v.memset(consts[:, j:j + 1], value).then_inc(consts_ready, 1)
            step = Chain(dve, set_dve, 0)
            step.begin(0)
            dve.wait_ge(loaded_first, 16 * len(FIRST))
            dve.wait_ge(set_act, 2)
            step(v.tensor_tensor(bn1[:, 0, :], bn1[:, 0, :], bn1[:, 3, :], ALU.mult))
            step(v.tensor_tensor(stem_w[0:1, :], stem_w[0:1, :], bn1[0:1, 2, :], ALU.subtract))
            step(v.tensor_tensor(stem_w[:, :], stem_w[:, :], bn1[:, 0, :], ALU.mult))
            v.tensor_tensor(stem_w[0:1, :], stem_w[0:1, :], bn1[0:1, 1, :], ALU.add).then_inc(stem_ready, 1)

            def setup():
                dve.wait_ge(pads_ready, PADS)
                dve.wait_ge(set_act, 4)
                step(v.tensor_tensor(bn2_scale[:], bn2[:, 1, :], bn2[:, 4, :], ALU.mult))
                step(v.tensor_tensor(bn2_bias[:], bn2[:, 0, :], bn2[:, 3, :], ALU.subtract))
                step(v.tensor_tensor(bn2_bias[:], bn2_bias[:], bn2_scale[:], ALU.mult))
                step(v.tensor_tensor(bn2_bias[:], bn2_bias[:], bn2[:, 2, :], ALU.add))
                for c in range(2):
                    for i in range(GROUP_IMGS):
                        ins = v.tensor_copy(xT[:, c, i * SLOT:i * SLOT + 1], cls_cols[:, c:c + 1])
                step(ins)
                dve.wait_ge(shifts_ready, 1)
                for h in range(2):
                    part = rows[:, h * 288:(h + 1) * 288]
                    ins = v.tensor_tensor(part, part, main.ap(h)[0:1, 0:288], ALU.add)
                step(ins)
                v.tensor_scalar(rows[:, 0:2 * DIM], rows[:, 0:2 * DIM], 1.0, None, ALU.add)\
                    .then_inc(qkv_row_ready, 1)
                step(v.tensor_tensor(fc1_b[:], fc1_b[:], main.ap(2)[:, 0:HIDDEN // 128], ALU.add))
                for c in range(2):
                    step(v.tensor_scalar(qkv_w[0:HALF, c, :], qkv_w[0:HALF, c, :], ln_cols[:, 0, c:c + 1], None,
                                         ALU.mult))
                    ins = v.tensor_scalar(fc1_w[:, c, :], fc1_w[:, c, :], ln_cols[:, 2, c:c + 1], None, ALU.mult)
                    step(ins) if c == 0 else ins.then_inc(folded, 1)

            iterations(dve, DVE_ORDERS, {
                "setup.start": setup, "front.leaky": leaky, "front.sampling": sampling,
                "gather.interpolate": interpolate, "main.embed": embed_leaky, "main.tokens": norm_tokens,
                "main.query": query, "main.key": key, "main.outer": outer, "main.attend": attend,
                "main.proj": project, "main.mlp": mlp_out, "main.tokens_end": norm_tokens_end,
                "main.proj_end": project_end, "main.mlp_end": mlp_end, "moe.r": choose, "moe.y": expert_sum})


def kernel(**inputs):
    import numpy as np
    import concourse.bacc as bacc
    from concourse.bass_utils import run_bass_kernel_spmd

    x = {k.removeprefix("L0_"): np.asarray(v) for k, v in inputs.items()}

    def chunks(w, p):
        return w.reshape(-1, p, w.shape[-1]).transpose(1, 0, 2)

    def cols(*vs):
        return np.stack([v.reshape(2, HALF).T for v in vs], 1)

    img = x["x"].reshape(GROUPS, TILES, TILE_IMGS, 3, OUT_SIDE, K, K, OUT_SIDE, K, K)
    patches = img.transpose(3, 6, 9, 0, 1, 5, 8, 2, 4, 7).reshape(STEM_K - 1, -1)
    taps = lambda w: w.transpose(2, 3, 1, 0).reshape(TAPS * C, -1)
    experts1 = np.concatenate([x["ffn_w1"].transpose(1, 0, 2).reshape(DIM, -1), x["ffn_w_fc_sh"]], 1)
    experts2 = np.concatenate([x["ffn_w2"].reshape(-1, DIM), x["ffn_w_proj_sh"]], 0)
    experts2 = np.concatenate([experts2, np.zeros((-len(experts2) % 128, DIM), np.float32)], 0)
    k = np.arange(K)
    at = np.stack(np.meshgrid(np.arange(OUT_SIDE) * K, np.arange(OUT_SIDE) * K, indexing="ij"), -1)
    tap = np.stack(np.meshgrid(k, k, indexing="ij"), -1).reshape(1, TAPS, 2)
    base = np.tile(at.reshape(POS, 1, 2) + tap, (TILE_IMGS, TILES, 1))
    image = np.repeat(np.arange(TILE_IMGS), POS).reshape(-1, 1, 1)
    img_base = np.broadcast_to(image * SIDE * SIDE, (TPOS, TILES, TAPS))
    head = np.arange(HALF) // HEAD_DIM
    a = {
        "xcol": np.concatenate([np.ones((1, patches.shape[1]), np.float32), patches], 0),
        "stem_w": np.concatenate([x["tok_stem_b"][None], x["tok_stem_w"].reshape(C, -1).T], 0),
        "bn1": np.broadcast_to(np.stack([x["tok_bn1_" + n] for n in "gbmv"]), (STEM_K, 4, C)),
        "ident": np.eye(128, dtype=np.float32),
        "off_w": chunks(taps(x["tok_off_w"]), 128),
        "off_b": np.broadcast_to(np.tile(x["tok_off_b"].reshape(TAPS, 2), (TILES, 1)), (TPOS, TILES * TAPS, 2)),
        "base": base.astype(np.float32),
        "img_base": (img_base.reshape(TPOS, -1) + SIDE).astype(np.float32),
        "bn2": cols(x["tok_dcn_b"], *[x["tok_bn2_" + n] for n in "gbmv"]),
        "dcn_w": chunks(taps(x["tok_dcn_w"]), 128),
        "head_mask": np.concatenate([head[:, None] == head, head[:, None] == np.arange(HALF_HEADS)], 1)
        .astype(np.float32),
        "ln_cols": cols(*[x["attn_" + n] for n in ("ln1_w", "ln1_b", "ln2_w", "ln2_b")]),
        "cls_cols": x["cls_tok"].reshape(2, HALF).T,
        "qkv_w": chunks(x["attn_qkv_w"], HALF),
        "qkv_b": x["attn_qkv_b"][None],
        "proj_w": chunks(x["attn_proj_w"], HALF),
        "proj_b": x["attn_proj_b"][None],
        "fc1_w": chunks(x["attn_fc1_w"], HALF),
        "fc1_b": x["attn_fc1_b"].reshape(-1, 128).T,
        "fc2_w": chunks(x["attn_fc2_w"], 128),
        "fc2_b": np.broadcast_to(x["attn_fc2_b"], (128, DIM)),
        "router_w": chunks(x["ffn_router_w"].T, HALF),
        "balance": np.broadcast_to(x["ffn_balance_bias"], (128, EXPERTS)),
        "moe_w1": chunks(experts1, HALF),
        "moe_w2": chunks(experts2, 128),
    }
    nc = bacc.Bacc("TRN2", target_bir_lowering=False, num_devices=1)
    arrays = {f"in_{n}": np.ascontiguousarray(v) for n, v in a.items()}
    args = {n: nc.dram_tensor(f"in_{n}", v.shape, F32, kind="ExternalInput").ap() for n, v in a.items()}
    out = nc.dram_tensor("out", (IMAGES, TOKENS, DIM), F32, kind="ExternalOutput").ap()
    build(nc, args, out)
    return run_bass_kernel_spmd(nc, [arrays], core_ids=[0]).results[0]["out"]
```
